# Optimizing a Trainium2 kernel written in Bass

```python
import numpy as np
import jax
import jax.numpy as jnp

def _softmax(x, axis=-1):
    return jax.nn.softmax(x, axis=axis)
def _gelu(x):
    return jax.nn.gelu(x, approximate=True)
def _silu(x):
    return jax.nn.silu(x)
def _sigmoid(x):
    return jax.nn.sigmoid(x)
def _layernorm(x, axis=-1, eps=1e-5):
    m = jnp.mean(x, axis=axis, keepdims=True)
    v = jnp.var(x, axis=axis, keepdims=True)
    return (x - m) / jnp.sqrt(v + eps)
def _scatter_add(tgt, idx, src, axis=0):
    return tgt.at[idx].add(src)
def _segment_sum(src, seg, n):
    return jax.ops.segment_sum(src, seg, n)

kernel_name = 'mk_metaformer_d2_conv_nchw128_24cb83'

def setup_inputs(seed: int = 0):
    np.random.seed(seed)
    _w = jnp.asarray
    def _rec_inputs():
        import jax
        import jax.numpy as jnp
        _gk = jax.random.key(seed)
        x = -0.0003929 + 0.9999 * jax.random.normal(jax.random.fold_in(_gk, 1), (32, 128, 64, 64), jnp.float32)
        return x
    x = _rec_inputs()
    def _L0_conv_setup():
        import jax, jax.numpy as jnp
        import numpy as np
        DEGREE = 8
        EPS = 1.0

        def _hermite_basis(xf, degree):
            g = np.pi ** (-0.25) * jnp.exp(-xf ** 2 / 2)
            basis = [g]
            if degree > 0:
                basis.append(np.sqrt(2.0) * xf * g)
            for i in range(2, degree + 1):
                basis.append(np.sqrt(2.0 / i) * xf * basis[-1] - np.sqrt((i - 1) / i) * basis[-2])
            return jnp.stack(basis, axis=-1)
        key = jax.random.key(seed)
        k1, k2 = jax.random.split(key)
        B, C_in, C_out, H, W = (32, 128, 128, 64, 64)
        x = jax.random.normal(k1, (B, C_in, H, W), dtype=jnp.float32)
        std = 1.0 / (C_in * (DEGREE + 1))
        weights = jax.random.normal(k2, (C_in, C_out, DEGREE + 1), dtype=jnp.float32) * std
        return {'x': x, 'weights': weights}
    _L0_conv_all = _L0_conv_setup()
    _L0_conv_in = {k: v for k, v in _L0_conv_all.items() if k in ('weights', )}
    del _L0_conv_all

    def _L0_ffn_setup():
        import jax, jax.numpy as jnp
        import numpy as np
        BN_EPS = 1e-05
        key = jax.random.key(seed)
        k1, k2, k3 = jax.random.split(key, 3)
        B, T, I, H = (64, 2048, 128, 128)
        x = jax.random.normal(k1, (B, T, I), dtype=jnp.float32)
        W = jax.random.normal(k2, (H, I), dtype=jnp.float32) * (1.0 / np.sqrt(I))
        V = jnp.linalg.qr(jax.random.normal(k3, (H, H), dtype=jnp.float32))[0]
        gamma = jnp.ones((H,), dtype=jnp.float32)
        beta = jnp.zeros((H,), dtype=jnp.float32)
        return {'x': x, 'W': W, 'V': V, 'gamma': gamma, 'beta': beta}
    _L0_ffn_all = _L0_ffn_setup()
    _L0_ffn_in = {k: v for k, v in _L0_ffn_all.items() if k in ('W', 'V', 'gamma', 'beta', )}
    del _L0_ffn_all

    def _L1_conv_setup():
        import jax, jax.numpy as jnp
        import numpy as np
        from jax import lax
        PAD0, PAD1 = (2, 1)
        UPSAMPLE_FACTOR = 2

        def _make_kernel():
            k = jnp.asarray([1.0, 3.0, 3.0, 1.0], dtype=jnp.float32)
            k = k[None, :] * k[:, None]
            k = k / jnp.sum(k)
            return k * UPSAMPLE_FACTOR ** 2
        key = jax.random.key(seed)
        fmap = jax.random.normal(key, (8, 128, 256, 256), dtype=jnp.float32)
        kernel = _make_kernel()
        return {'fmap': fmap, 'kernel': kernel}
    _L1_conv_all = _L1_conv_setup()
    _L1_conv_in = {k: v for k, v in _L1_conv_all.items() if k in ('kernel', )}
    del _L1_conv_all

    def _L1_ffn_setup():
        import jax, jax.numpy as jnp
        import numpy as np
        B, S, D, E, H, O, K = (512, 2048, 128, 64, 512, 128, 8)
        key = jax.random.key(seed)
        k0, k1, k2, k3 = jax.random.split(key, 4)
        x = jax.random.normal(k0, (B, S, D), dtype=jnp.float32)
        gate_w = jax.random.normal(k1, (E, D), dtype=jnp.float32) * (1.0 / np.sqrt(D))
        gate_b = jnp.zeros((E,), dtype=jnp.float32)
        weight1 = jax.random.uniform(k2, (E, D + 1, H), dtype=jnp.float32, minval=-1.0, maxval=1.0) * (1.0 / np.sqrt(D + 1))
        weight2 = jax.random.uniform(k3, (E, H + 1, O), dtype=jnp.float32, minval=-1.0, maxval=1.0) * (1.0 / np.sqrt(H + 1))
        return {'x': x, 'gate_w': gate_w, 'gate_b': gate_b, 'weight1': weight1, 'weight2': weight2}
    _L1_ffn_all = _L1_ffn_setup()
    _L1_ffn_in = {k: v for k, v in _L1_ffn_all.items() if k in ('gate_w', 'gate_b', 'weight1', 'weight2', )}
    del _L1_ffn_all

    return {
        "x": x,
        "L0_conv_weights": _L0_conv_in["weights"],
        "L0_ffn_W": _L0_ffn_in["W"],
        "L0_ffn_V": _L0_ffn_in["V"],
        "L0_ffn_gamma": _L0_ffn_in["gamma"],
        "L0_ffn_beta": _L0_ffn_in["beta"],
        "L1_conv_kernel": _L1_conv_in["kernel"],
        "L1_ffn_gate_w": _L1_ffn_in["gate_w"],
        "L1_ffn_gate_b": _L1_ffn_in["gate_b"],
        "L1_ffn_weight1": _L1_ffn_in["weight1"],
        "L1_ffn_weight2": _L1_ffn_in["weight2"],
    }

def reference(x, L0_conv_weights, L0_ffn_W, L0_ffn_V, L0_ffn_gamma, L0_ffn_beta, L1_conv_kernel, L1_ffn_gate_w, L1_ffn_gate_b, L1_ffn_weight1, L1_ffn_weight2):
    import jax
    import jax.numpy as jnp
    def _L0_conv_ref(x, weights):
        import jax, jax.numpy as jnp
        import numpy as np
        DEGREE = 8
        EPS = 1.0

        def _hermite_basis(xf, degree):
            g = np.pi ** (-0.25) * jnp.exp(-xf ** 2 / 2)
            basis = [g]
            if degree > 0:
                basis.append(np.sqrt(2.0) * xf * g)
            for i in range(2, degree + 1):
                basis.append(np.sqrt(2.0 / i) * xf * basis[-1] - np.sqrt((i - 1) / i) * basis[-2])
            return jnp.stack(basis, axis=-1)
        B, C, H, W = x.shape
        degree = weights.shape[2] - 1
        xf = x.reshape(B, C, H * W).transpose(0, 2, 1).reshape(-1, C)
        xf = jnp.tanh(xf) * (np.sqrt(2 * degree + 1) + EPS)
        hermite = _hermite_basis(xf, degree)
        y = jnp.einsum('bid,iod->bo', hermite, weights)
        C_out = weights.shape[1]
        y = y.reshape(B, H * W, C_out).transpose(0, 2, 1).reshape(B, C_out, H, W)
        return y

    def _L0_ffn_ref(x, W, V, gamma, beta):
        import jax, jax.numpy as jnp
        import numpy as np
        BN_EPS = 1e-05
        B, T, H = (x.shape[0], x.shape[1], W.shape[0])
        Wx = jnp.einsum('bti,hi->bth', x, W)
        flat = Wx.reshape(B * T, H)
        mean = jnp.mean(flat, axis=0)
        var = jnp.var(flat, axis=0)
        Wx = ((flat - mean) * jax.lax.rsqrt(var + BN_EPS) * gamma + beta).reshape(B, T, H)
        Vt = V.T

        def step(yt, wx_t):
            yt = jax.nn.sigmoid(wx_t + yt @ Vt)
            return (yt, yt)
        y0 = jnp.zeros((B, H), dtype=Wx.dtype)
        _, ys = jax.lax.scan(step, y0, jnp.swapaxes(Wx, 0, 1))
        return jnp.swapaxes(ys, 0, 1)

    def _L1_conv_ref(fmap, kernel):
        import jax, jax.numpy as jnp
        import numpy as np
        from jax import lax
        PAD0, PAD1 = (2, 1)
        UPSAMPLE_FACTOR = 2

        def _make_kernel():
            k = jnp.asarray([1.0, 3.0, 3.0, 1.0], dtype=jnp.float32)
            k = k[None, :] * k[:, None]
            k = k / jnp.sum(k)
            return k * UPSAMPLE_FACTOR ** 2
        N, C, H, W = fmap.shape
        x = jnp.pad(fmap, ((0, 0), (0, 0), (PAD0, PAD1), (PAD0, PAD1)))
        w = jnp.flip(kernel, (0, 1))[None, None, :, :]
        w = jnp.broadcast_to(w, (C, 1) + kernel.shape)
        out = lax.conv_general_dilated(x, w, window_strides=(1, 1), padding='VALID', dimension_numbers=('NCHW', 'OIHW', 'NCHW'), feature_group_count=C)
        return out

    def _L1_ffn_ref(x, gate_w, gate_b, weight1, weight2):
        import jax, jax.numpy as jnp
        import numpy as np
        B, S, D, E, H, O, K = (512, 2048, 128, 64, 512, 128, 8)
        Bn, Sn, Dn = x.shape
        logits = jnp.einsum('bsd,ed->bse', x, gate_w) + gate_b
        probs = jax.nn.softmax(logits, axis=1)
        vals, idx = jax.lax.top_k(probs.transpose(0, 2, 1), K)
        topv = vals.transpose(0, 2, 1)
        topi = idx.transpose(0, 2, 1)
        flat_idx = topi.reshape(Bn, K * E)
        gathered = jnp.take_along_axis(x, flat_idx[:, :, None], axis=1)
        gathered = gathered.reshape(Bn, K, E, Dn)
        pooled = jnp.einsum('bked,bke->bed', gathered, topv)
        ones = jnp.ones((E, Bn, 1), dtype=x.dtype)
        h = jnp.concatenate([pooled.transpose(1, 0, 2), ones], axis=-1)
        h = jax.nn.gelu(jnp.einsum('ebd,edh->ebh', h, weight1), approximate=False)
        h = jnp.concatenate([h, ones], axis=-1)
        out = jnp.einsum('ebh,eho->ebo', h, weight2)
        out = out.transpose(1, 0, 2)
        weighted = jnp.einsum('beo,bke->bkeo', out, topv).reshape(Bn, K * E, O)
        outputs = jnp.zeros((Bn, Sn, O), dtype=x.dtype)
        outputs = outputs.at[jnp.arange(Bn)[:, None], flat_idx].add(weighted)
        return outputs

    def _gn(v, G=32, eps=1e-5):
        B_, C_, H_, W_ = v.shape
        g = v.reshape(B_, G, C_ // G, H_, W_)
        m = jnp.mean(g, axis=(2, 3, 4), keepdims=True)
        s = jnp.var(g, axis=(2, 3, 4), keepdims=True)
        return ((g - m) / jnp.sqrt(s + eps)).reshape(v.shape)

    def _ln_c(v, eps=1e-6):
        m = jnp.mean(v, axis=1, keepdims=True)
        s = jnp.var(v, axis=1, keepdims=True)
        return (v - m) / jnp.sqrt(s + eps)

    def _ln_t(v, eps=1e-5):
        m = jnp.mean(v, axis=-1, keepdims=True)
        s = jnp.var(v, axis=-1, keepdims=True)
        return (v - m) / jnp.sqrt(s + eps)

    def _to_tokens(v):
        B_, C_, H_, W_ = v.shape
        return v.reshape(B_, C_, H_ * W_).transpose(0, 2, 1)
    def _from_tokens(t, like):
        B_, C_, H_, W_ = like.shape
        return t.transpose(0, 2, 1).reshape(B_, C_, H_, W_)

    x = x + _L0_conv_ref(_ln_c(x), L0_conv_weights)
    t = _to_tokens(x)
    t = t + _L0_ffn_ref(_ln_t(t), L0_ffn_W, L0_ffn_V, L0_ffn_gamma, L0_ffn_beta)
    x = _from_tokens(t, x)
    x = x + _L1_conv_ref(_ln_c(x), L1_conv_kernel)
    t = _to_tokens(x)
    t = t + _L1_ffn_ref(_ln_t(t), L1_ffn_gate_w, L1_ffn_gate_b, L1_ffn_weight1, L1_ffn_weight2)
    x = _from_tokens(t, x)
    return x


_drawn_inputs = setup_inputs


def setup_inputs(seed=0):
    import zlib

    import numpy as np

    out = dict(_drawn_inputs(seed))
    spreads = {'L0_ffn_gamma': (1.0, 0.2), 'L0_ffn_beta': (0.0, 0.1), 'L1_ffn_gate_b': (0.0, 0.1)}
    factors = {'L0_conv_weights': 5.921,
     'L1_ffn_gate_w': 8.0,
     'L1_ffn_weight1': 8.0,
     'L1_ffn_weight2': 8.0}
    for name, (base, spread) in spreads.items():
        noise = np.random.default_rng([zlib.crc32(name.encode()), seed]).standard_normal(out[name].shape)
        drawn = base * np.exp(spread * noise) if base else spread * noise
        out[name] = jnp.asarray(drawn.astype(out[name].dtype))
    for name, factor in factors.items():
        out[name] = (out[name] * factor).astype(out[name].dtype)
    return out
```

```python
from contextlib import ExitStack

import numpy as np

import concourse.bass as bass
from concourse import mybir

F32 = mybir.dt.float32
I32 = mybir.dt.int32
ALU = mybir.AluOpType
ACT = mybir.ActivationFunctionType
AX = mybir.AxisListType

P = 128


def hermite_in_products(degree, z_scale):
    even = np.sort(np.unique(np.round((np.polynomial.hermite.hermgauss(8)[0] / z_scale) ** 2, 12)))
    odd = np.sort(np.unique(np.round((np.polynomial.hermite.hermgauss(7)[0] / z_scale) ** 2, 12)))[1:]
    order = {2: even[0], 4: even[2], 6: even[1], 8: even[3], 3: odd[0], 5: odd[1], 7: odd[2]}
    poly = np.polynomial.polynomial
    h = [np.array([np.pi ** -0.25]), np.array([0.0, np.sqrt(2.0) * z_scale * np.pi ** -0.25])]
    f = [np.array([1.0]), np.array([0.0, 1.0])]
    for k in range(2, degree + 1):
        h.append(poly.polysub(np.sqrt(2.0 / k) * poly.polymul([0.0, z_scale], h[-1]), np.sqrt((k - 1) / k) * h[-2]))
        f.append(poly.polymul([-order[k], 0.0, 1.0], f[-2]))
    change = np.zeros((degree + 1, degree + 1))
    for d in range(degree + 1):
        rest = np.zeros(degree + 1)
        rest[:len(h[d])] = h[d]
        for k in range(d, -1, -1):
            change[d, k] = rest[k]
            rest[:k + 1] -= change[d, k] * f[k]
    return order, change


def metaformer(nc, x, herm_w, ffn_w, ffn_v, gamma, beta, blur, gate_w, gate_b, w1, w2, out, scratch):
    B, C, IMG_H, IMG_W = x.shape
    T = IMG_H * IMG_W
    DEG = herm_w.shape[2] - 1
    E, _, HID = w1.shape
    O = w2.shape[2]
    TOK = 512
    IMG_TILES = T // TOK
    TILES = B * IMG_TILES
    SUB = TOK // P
    ROOT_C = float(np.sqrt(C))
    Z_SCALE = float(np.sqrt(2 * DEG + 1) + 1.0)
    CENTRE, CHANGE = hermite_in_products(DEG, Z_SCALE)
    assert C == P and O == P and 2 * E == P and T % TOK == 0

    x_img = x.rearrange("b c h w -> b c (h w)")
    out_img = out.rearrange("b c h w -> b c (h w)")
    x1_dram, wx_dram, y_dram, x3_dram, prob_dram, expert_dram = scratch

    ctx = ExitStack()
    with ctx:
        def sb(name, shape, dt=F32, scope=ctx):
            return scope.enter_context(nc.sbuf_tensor(name, shape, dt))

        def sem(name):
            return ctx.enter_context(nc.semaphore(name))

        def wait(eng, s, r, c, per=1, sub=None, unroll=4):
            sub = per if sub is None else sub
            if not isinstance(r, int) or c >= 0:
                eng.wait_ge(s, per * unroll * r + per * c + sub)

        def wait_slot(eng, slots, r, c, unroll=4):
            ring = len(slots)
            if not isinstance(r, int) or c >= 0:
                eng.wait_ge(slots[c % ring], 16 * (unroll // ring) * r + 16 * (c // ring + 1))

        psum = ctx.enter_context(nc.psum_tensor("psum", [P, 8, 512], F32))
        banks = [psum[:, i, :] for i in range(8)]

        ident = sb("ident", [P, P])
        centre = sb("centre", [P, P])
        minus_half = sb("minus_half", [P, 4])
        eps_c = sb("eps_c", [P, 4])
        eps_t = sb("eps_t", [P, 4])
        norm_a = sb("norm_a", [P, 1])
        norm_b = sb("norm_b", [P, 1])
        v_t = sb("v_t", [P, P])
        passed = sem("passed")
        phase_done = [sem(f"phase_{k}_done") for k in "abcde"]

        def run_phases(eng, *phases):
            for k, phase in enumerate(phases):
                if k:
                    eng.wait_ge(phase_done[k - 1], 5)
                phase(eng)
                eng.drain().then_inc(phase_done[k], 1)

        scope_a = ExitStack()
        herm_raw = sb("herm_raw", [P, P * (DEG + 1)], scope=scope_a)
        herm = sb("herm", [P, DEG + 1, P], scope=scope_a)
        w_raw = sb("w_raw", [P, P], scope=scope_a)
        w_t = sb("w_t", [P, P], scope=scope_a)
        v_raw = sb("v_raw", [P, P], scope=scope_a)
        gam = sb("gam", [P, 1], scope=scope_a)
        bet = sb("bet", [P, 1], scope=scope_a)
        x_in = sb("x_in", [P, 4, TOK], scope=scope_a)
        squares = sb("squares", [P, 2, TOK], scope=scope_a)
        var = sb("var", [P, 2, SUB], scope=scope_a)
        var_eps = sb("var_eps", [P, 2, SUB], scope=scope_a)
        rstd = sb("rstd", [P, 2, SUB], scope=scope_a)
        normed = sb("normed", [P, 2, TOK], scope=scope_a)
        z = sb("z", [P, 2, TOK], scope=scope_a)
        z2 = sb("z2", [P, 2, TOK], scope=scope_a)
        basis = sb("basis", [P, 2, DEG + 1, TOK], scope=scope_a)
        x1 = sb("x1", [P, 4, TOK], scope=scope_a)
        squares2 = sb("squares2", [P, 2, TOK], scope=scope_a)
        var2 = sb("var2", [P, 2, SUB], scope=scope_a)
        var2_eps = sb("var2_eps", [P, 2, SUB], scope=scope_a)
        rstd2 = sb("rstd2", [P, 2, SUB], scope=scope_a)
        normed2 = sb("normed2", [P, 2, TOK], scope=scope_a)
        t_cm = sb("t_cm", [P, 2, TOK], scope=scope_a)
        wx = sb("wx", [P, 4, TOK], scope=scope_a)
        stats = sb("stats", [P, TILES, 6], scope=scope_a)
        mean_var = sb("mean_var", [P, 2], scope=scope_a)
        bn_tmp = sb("bn_tmp", [P, 4], scope=scope_a)
        scope_a.close()
        p_centred, p_flipped, p_conv, p_centred2, p_flipped2, p_wx = (
            banks[0], banks[1], banks[2:4], banks[4], banks[5], banks[6])

        weights_loaded = sem("weights_loaded")
        ones_set = sem("ones_set")
        ident_set = sem("ident_set")
        herm_step = sem("herm_step")
        herm_ready = sem("herm_ready")
        turned = sem("turned")
        turned_used = sem("turned_used")
        x_loaded = [sem(f"x_loaded{i}") for i in range(4)]
        centred = sem("centred")
        squared = sem("squared")
        var_ready = sem("var_ready")
        eps_added = sem("eps_added")
        rstd_ready = sem("rstd_ready")
        norm_ready = sem("norm_ready")
        flipped = sem("flipped")
        z_ready = sem("z_ready")
        z2_ready = sem("z2_ready")
        gauss_ready = sem("gauss_ready")
        basis_ready = sem("basis_ready")
        conv_done = sem("conv_done")
        x1_ready = sem("x1_ready")
        x1_stored = [sem(f"x1_stored{i}") for i in range(4)]
        centred2 = sem("centred2")
        squared2 = sem("squared2")
        var2_ready = sem("var2_ready")
        eps2_added = sem("eps2_added")
        rstd2_ready = sem("rstd2_ready")
        norm2_ready = sem("norm2_ready")
        flipped2 = sem("flipped2")
        t_ready = sem("t_ready")
        wx_done = sem("wx_done")
        wx_ready = sem("wx_ready")
        stats_ready = sem("stats_ready")
        bn_step = sem("bn_step")
        bn_root = sem("bn_root")
        wx_stored = [sem(f"wx_stored{i}") for i in range(4)]

        def sub_tiles(ap):
            return ap.rearrange("p (s c) -> p s c", s=SUB)

        def per_token(ap):
            return ap.unsqueeze(2).to_broadcast([P, SUB, P])

        def pipeline_a(eng, step, unroll=4):
            start, rounds = 8, (TILES - 8) // unroll - 1
            for c in range(-1, start):
                step(0, c, *[0 <= c + d < TILES for d in (1, 0, -1, -2)])
            with eng.Fori(0, rounds) as r:
                for c in range(start, start + unroll):
                    step(r, c, True, True, True, True)
            for c in range(start + rounds * unroll, TILES + 2):
                step(0, c, *[0 <= c + d < TILES for d in (1, 0, -1, -2)])

        def tile_at(tiles, r, c, unroll):
            if isinstance(r, int):
                return tiles[c, :, :]
            return tiles[bass.ds(unroll * r + c, 1), :, :].rearrange("a p n -> p (a n)")

        def x_tile(r, c):
            part = slice(c % IMG_TILES * TOK, (c % IMG_TILES + 1) * TOK)
            if isinstance(r, int):
                return x_img[c // IMG_TILES, :, part]
            return x_img[bass.ds(r + c // IMG_TILES, 1), :, part].rearrange("a p n -> p (a n)")

        GROUP = 4
        GROUPS = B // GROUP
        SEG = IMG_W
        SEGS = T // SEG
        LANES = GROUP * SEGS
        WARM = 16
        HALF = (WARM + SEG) // 2
        TOLERANCE = 2.0 ** -21
        scope_b = ExitStack()
        wxy = [sb(f"wxy{i}", [P, WARM + GROUP * T], scope=scope_b) for i in range(3)]
        state = [sb(f"state{i}", [P, 2, LANES], scope=scope_b) for i in range(2)]
        preact = [sb(f"preact{i}", [P, LANES], scope=scope_b) for i in range(2)]
        first_state = [sb(f"first_state{i}", [P, LANES], scope=scope_b) for i in range(2)]
        gap = sb("gap", [P, GROUP, SEGS - 1], scope=scope_b)
        gap_max = sb("gap_max", [P, GROUPS + 1], scope=scope_b)
        close = sb("close", [P, 2], scope=scope_b)
        close_count = sb("close_count", [1, 1], I32, scope=scope_b)
        scope_b.close()
        AGAIN = 128
        scope_f = ExitStack()
        again_wx = sb("again_wx", [P, B, AGAIN], scope=scope_f)
        again_y = sb("again_y", [P, B, AGAIN], scope=scope_f)
        again_state = sb("again_state", [P, B], scope=scope_f)
        again_pre = sb("again_pre", [P, B], scope=scope_f)
        scope_f.close()

        pads_set = sem("pads_set")
        group_loaded = [sem(f"group_loaded{i}") for i in range(3)]
        group_stored = [sem(f"group_stored{i}") for i in range(3)]
        product_done = [sem(f"product_done{i}") for i in range(2)]
        preact_ready = [sem(f"preact_ready{i}") for i in range(2)]
        state_ready = [sem(f"state_ready{i}") for i in range(2)]
        placed = [sem(f"placed{i}") for i in range(2)]
        first_kept = sem("first_kept")
        gap_step = sem("gap_step")
        count_done = sem("count_done")
        count_ready = sem("count_ready")
        again_loaded = sem("again_loaded")
        again_stored = sem("again_stored")
        again_product = sem("again_product")
        again_preact = sem("again_preact")
        again_step = sem("again_step")
        again_placed = sem("again_placed")

        def tokens_at(g, s):
            slot = wxy[g % 3]
            if isinstance(s, int):
                return slot[:, s:s + SEG * (LANES - 1) + 1:SEG]
            return slot[:, bass.ds(s, LANES, SEG)]

        STEPS = WARM + SEG

        def states(g, s, warm):
            return (g // 2) * (STEPS + 2) + s + (1 if warm else 2)

        def in_halves(eng, step, begin=None, warmed=None, end=None):
            for g in range(GROUPS + 1):
                if g < GROUPS and begin:
                    begin(g)
                for lo, hi, warm in ((0, WARM, True), (WARM, HALF, False)):
                    with eng.Fori(0, (hi - lo) // 2) as i:
                        for odd in range(2):
                            if g < GROUPS:
                                step(g, 2 * i + (lo + odd), odd, warm)
                            if g > 0:
                                step(g - 1, 2 * i + (lo + HALF + odd), odd, False)
                    if warm and g < GROUPS and warmed:
                        warmed(g)
                if g > 0 and end:
                    end(g - 1)

        PAIRS = B // 2
        SUBS = T // P
        LOW = -3.0e38
        pooled = sb("pooled", [P, E, B])
        scope_c = ExitStack()
        gates_raw = sb("gates_raw", [E, P], scope=scope_c)
        gates_t = sb("gates_t", [P, E], scope=scope_c)
        centre_gates = sb("centre_gates", [P, P + E], scope=scope_c)
        gate_bias = sb("gate_bias", [P, 1], scope=scope_c)
        taps = sb("taps", [P, 6, 4], scope=scope_c)
        diags = sb("diags", [P, 4, IMG_W], scope=scope_c)
        diags_low = sb("diags_low", [P, 4, IMG_W], scope=scope_c)
        band = sb("band", [P, 6, IMG_W], scope=scope_c)
        img_x = sb("img_x", [P, 2, T], scope=scope_c)
        img_y = sb("img_y", [P, 2, T], scope=scope_c)
        sq_c = sb("sq_c", [P, 2, TOK], scope=scope_c)
        sum_c = sb("sum_c", [P, 2, SUB], scope=scope_c)
        sum_c_eps = sb("sum_c_eps", [P, 2, SUB], scope=scope_c)
        root_c = sb("root_c", [P, 2, SUB], scope=scope_c)
        blur_in = sb("blur_in", [P, 4, TOK], scope=scope_c)
        sq_t = sb("sq_t", [P, 2, TOK], scope=scope_c)
        sum_t = sb("sum_t", [P, 2, SUB], scope=scope_c)
        sum_t_eps = sb("sum_t_eps", [P, 2, SUB], scope=scope_c)
        root_t = sb("root_t", [P, SUBS, 2], scope=scope_c)
        tokens = sb("tokens", [P, 2, SUBS, P], scope=scope_c)
        logits_tm = sb("logits_tm", [P, SUBS, 2, E], scope=scope_c)
        logits = sb("logits", [P, T], scope=scope_c)
        prob = sb("prob", [P, T], scope=scope_c)
        top8 = sb("top8", [P, 8], scope=scope_c)
        minus_max = sb("minus_max", [P, 1], scope=scope_c)
        exp_sum = sb("exp_sum", [P, 1], scope=scope_c)
        exp_inv = sb("exp_inv", [P, 1], scope=scope_c)
        prob_tm = sb("prob_tm", [P, 2, SUB, 2 * E], scope=scope_c)
        scope_c.close()
        PT = 2 * IMG_TILES

        c_loaded = sem("c_loaded")
        c_const = sem("c_const")
        diag_step = sem("diag_step")
        c_setup = sem("c_setup")
        gates_turned = sem("gates_turned")
        gates_copied = sem("gates_copied")
        img_loaded = [sem(f"img_loaded{i}") for i in range(2)]
        x2_ready = sem("x2_ready")
        c_centred = sem("c_centred")
        c_squared = sem("c_squared")
        c_summed = sem("c_summed")
        c_eps_added = sem("c_eps_added")
        c_root_ready = sem("c_root_ready")
        c_normed = sem("c_normed")
        blurred = sem("blurred")
        x3_ready = sem("x3_ready")
        x3_stored = [sem(f"x3_stored{i}") for i in range(2)]
        gated = sem("gated")
        t_squared = sem("t_squared")
        t_kept = sem("t_kept")
        t_summed = sem("t_summed")
        t_eps_added = sem("t_eps_added")
        t_root_ready = sem("t_root_ready")
        logits_tm_ready = sem("logits_tm_ready")
        logits_turned = sem("logits_turned")
        logits_ready = sem("logits_ready")
        select_step = sem("select_step")
        exp_ready = sem("exp_ready")
        prob_ready = sem("prob_ready")
        prob_stored = sem("prob_stored")
        prob_turned = sem("prob_turned")
        prob_tm_ready = sem("prob_tm_ready")
        pooled_done = sem("pooled_done")
        pooled_ready = sem("pooled_ready")

        def over_tiles(step, ahead):
            for j in range(-ahead, PT + 1):
                step(j)

        def alone(eng, s, value):
            eng.wait_ge(s, value)
            eng.sem_inc(passed, 1)

        HK = HID // P
        UE = 8
        scope_d = ExitStack()
        w1_in = sb("w1_in", [P, UE, HID], scope=scope_d)
        w2_in = sb("w2_in", [P, UE, HK, O], scope=scope_d)
        b1_raw = sb("b1_raw", [E, HID], scope=scope_d)
        b1_t = sb("b1_t", [P, E, HK], scope=scope_d)
        hid_pre = sb("hid_pre", [P, 2, HK * B], scope=scope_d)
        hid = sb("hid", [P, 2, HK * B], scope=scope_d)
        eo = sb("eo", [B, 2, 4, O], scope=scope_d)
        scope_d.close()

        bias1_loaded = sem("bias1_loaded")
        bias1_turned = sem("bias1_turned")
        bias1_ready = sem("bias1_ready")
        w_loaded = [sem(f"w_loaded{i}") for i in range(UE)]
        hid_done = sem("hid_done")
        hid_pre_ready = sem("hid_pre_ready")
        hid_ready = sem("hid_ready")
        eo_done = sem("eo_done")
        eo_ready = sem("eo_ready")
        eo_stored = [sem(f"eo_stored{i}") for i in range(2)]

        def rounds_d(eng, body):
            with eng.Fori(0, E // UE - 1) as r:
                body(r, False)
            body(E // UE - 1, True)

        scope_e = ExitStack()
        outputs = sb("outputs", [P, PAIRS, O], scope=scope_e)
        b2_in = sb("b2_in", [P, O], scope=scope_e)
        chosen = sb("chosen", [P, 2, O], scope=scope_e)
        prob_in = sb("prob_in", [P, 2, T], scope=scope_e)
        x3_in = sb("x3_in", [P, 4, T], scope=scope_e)
        scope_e.close()

        outputs_loaded = sem("outputs_loaded")
        outputs_ready = sem("outputs_ready")
        chosen_ready = sem("chosen_ready")
        pair_loaded = [sem(f"pair_loaded{i}") for i in range(2)]
        spread = sem("spread")
        out_ready = sem("out_ready")
        out_stored = [sem(f"out_stored{i}") for i in range(2)]

        def sync_a(sp):
            for dst, src in ((herm_raw[:], herm_w.rearrange("i o d -> i (o d)")), (w_raw[:], ffn_w), (v_raw[:], ffn_v),
                             (gam[:], gamma.unsqueeze(1)), (bet[:], beta.unsqueeze(1))):
                sp.dma_start(dst, src).then_inc(weights_loaded, 16)
            for n in range(3):
                sp.dma_start(x_in[:, n, :], x_tile(0, n)).then_inc(x_loaded[n], 16)
            U = IMG_TILES

            def step(r, c, s1, s2, s3, s4):
                if s4:
                    k = (c - 2) % 4
                    wait(sp, wx_ready, r, c - 2, unroll=U)
                    sp.dma_start(tile_at(wx_dram, r, c - 2, U), wx[:, k, :]).then_inc(wx_stored[k], 16)
                if s3:
                    k = (c - 1) % 4
                    wait(sp, x1_ready, r, c - 1, unroll=U)
                    sp.dma_start(tile_at(x1_dram, r, c - 1, U), x1[:, k, :]).then_inc(x1_stored[k], 16)
                if not isinstance(r, int) or 3 <= c + 3 < TILES:
                    sp.dma_start(x_in[:, (c + 3) % 4, :], x_tile(r, c + 3)).then_inc(x_loaded[(c + 3) % 4], 16)

            pipeline_a(sp, step, U)
            for k in range(4):
                sp.wait_ge(x1_stored[k], 16 * (TILES // 4))
                sp.wait_ge(wx_stored[k], 16 * (TILES // 4))

        def tensor_a(pe):
            pe.wait_ge(weights_loaded, 80)
            pe.wait_ge(ident_set, 2)
            pe.transpose(banks[7][:, 0:P], v_raw[:], ident[:]).then_inc(turned, 1)
            pe.transpose(banks[7][:, P:2 * P], w_raw[:], ident[:]).then_inc(turned, 1)
            pe.wait_ge(herm_ready, 1)
            pe.wait_ge(turned_used, 2)

            def step(r, c, s1, s2, s3, s4):
                def mix(k0, k1):
                    for k in range(k0, k1):
                        if k == 0:
                            wait(pe, x1_ready, r, c - 2)
                            wait(pe, gauss_ready, r, c)
                        else:
                            wait(pe, basis_ready, r, c, per=DEG, sub=k)
                        mm = pe.matmul(p_conv[c % 2][:], herm[:, k, :], basis[:, c % 2, k, :],
                                       start=(k == 0), stop=(k == DEG))
                    if k1 == DEG + 1:
                        mm.then_inc(conv_done, 1)

                if s1:
                    wait_slot(pe, x_loaded, r, c + 1)
                    wait(pe, norm_ready, r, c)
                    for j in range(SUB):
                        mm = pe.matmul(p_centred[:, j * P:(j + 1) * P], x_in[:, (c + 1) % 4, j * P:(j + 1) * P],
                                       centre[:], start=True, stop=True)
                    mm.then_inc(centred, 1)
                if s2:
                    mix(0, 2)
                if s3:
                    wait(pe, x1_ready, r, c - 1)
                    wait(pe, norm2_ready, r, c - 2)
                    for j in range(SUB):
                        mm = pe.matmul(p_centred2[:, j * P:(j + 1) * P], x1[:, (c - 1) % 4, j * P:(j + 1) * P],
                                       centre[:], start=True, stop=True)
                    mm.then_inc(centred2, 1)
                if s2:
                    mix(2, 4)
                if s1:
                    wait(pe, norm_ready, r, c + 1)
                    wait(pe, z_ready, r, c)
                    for j in range(SUB):
                        mm = pe.transpose(p_flipped[:, j * P:(j + 1) * P], normed[:, (c + 1) % 2, j * P:(j + 1) * P],
                                          ident[:])
                    mm.then_inc(flipped, 1)
                if s2:
                    mix(4, 7)
                if s3:
                    wait(pe, norm2_ready, r, c - 1)
                    wait(pe, t_ready, r, c - 2)
                    for j in range(SUB):
                        mm = pe.transpose(p_flipped2[:, j * P:(j + 1) * P], normed2[:, (c - 1) % 2, j * P:(j + 1) * P],
                                          ident[:])
                    mm.then_inc(flipped2, 1)
                if s2:
                    mix(7, DEG + 1)
                if s3:
                    wait(pe, t_ready, r, c - 1)
                    wait(pe, wx_ready, r, c - 2)
                    pe.matmul(p_wx[:], w_t[:], t_cm[:, (c - 1) % 2, :], start=True, stop=True).then_inc(wx_done, 1)

            pipeline_a(pe, step)

        def scalar_a(act):
            act.wait_ge(turned, 2)
            act.activation(v_t[:], banks[7][:, 0:P], ACT.Copy).then_inc(turned_used, 1)

            def step(r, c, s1, s2, s3, s4):
                if s4:
                    wait(act, wx_done, r, c - 2)
                    wait_slot(act, wx_stored, r, c - 6)
                    wait(act, stats_ready, r, c - 6)
                    act.activation(wx[:, (c - 2) % 4, :], p_wx[:], ACT.Copy).then_inc(wx_ready, 1)
                if s1:
                    wait(act, centred, r, c + 1)
                    wait(act, var_ready, r, c - 1)
                    act.activation(squares[:, (c + 1) % 2, :], p_centred[:], ACT.Square).then_inc(squared, 1)
                if s3:
                    wait(act, centred2, r, c - 1)
                    wait(act, var2_ready, r, c - 3)
                    act.activation(squares2[:, (c - 1) % 2, :], p_centred2[:], ACT.Square).then_inc(squared2, 1)
                if s1:
                    k = (c + 1) % 2
                    wait(act, flipped, r, c + 1)
                    wait(act, conv_done, r, c - 1)
                    act.activation(z[:, k, :], p_flipped[:], ACT.Tanh, scale=ROOT_C).then_inc(z_ready, 1)
                    wait(act, z_ready, r, c + 1)
                    act.activation(z2[:, k, :], z[:, k, :], ACT.Square).then_inc(z2_ready, 1)
                    wait(act, z2_ready, r, c + 1)
                    act.activation(basis[:, k, 0, :], z2[:, k, :], ACT.Exp, scale=-0.5 * Z_SCALE ** 2)\
                       .then_inc(gauss_ready, 1)
                if s3:
                    wait(act, flipped2, r, c - 1)
                    wait(act, wx_done, r, c - 3)
                    act.activation(t_cm[:, (c - 1) % 2, :], p_flipped2[:], ACT.Copy, scale=ROOT_C).then_inc(t_ready, 1)

            pipeline_a(act, step)

        def gpsimd_a(pool):
            pool.memset(ident[:], 0.0).then_inc(ones_set, 1)
            pool.memset(centre[:], -1.0 / C).then_inc(ones_set, 1)
            for tile, value in ((minus_half, -0.5), (eps_c, 1e-6 * C), (eps_t, 1e-5 * C)):
                pool.memset(tile[:], value).then_inc(ones_set, 1)
            pool.wait_ge(ones_set, 5)
            for m, diagonal in ((ident, 1.0), (centre, 1.0 - 1.0 / C)):
                pool.affine_select(out=m[:], in_=m[:], compare_op=ALU.not_equal, fill=diagonal, base=0,
                                   pattern=[[-1, P]], channel_multiplier=1).then_inc(ident_set, 1)

            def inverse_root(r, c, ready, given, eps, total, added_eps, added, result):
                k = c % 2
                wait(pool, given, r, c)
                pool.tensor_tensor(added_eps[:, k, :], total[:, k, :], eps[:], ALU.add).then_inc(added, 1)
                wait(pool, added, r, c)
                pool.tensor_tensor(result[:, k, :], added_eps[:, k, :], minus_half[:], ALU.pow).then_inc(ready, 1)

            def step(r, c, s1, s2, s3, s4):
                if s1:
                    wait(pool, norm_ready, r, c - 1)
                    inverse_root(r, c + 1, rstd_ready, var_ready, eps_c, var, var_eps, eps_added, rstd)
                if s3:
                    wait(pool, norm2_ready, r, c - 3)
                    inverse_root(r, c - 1, rstd2_ready, var2_ready, eps_t, var2, var2_eps, eps2_added, rstd2)

            pipeline_a(pool, step)
            pool.wait_ge(bn_step, 2)
            pool.tensor_tensor(bn_tmp[:, 1:2], bn_tmp[:, 0:1], minus_half[:, 0:1], ALU.pow).then_inc(bn_root, 1)

        def vector_a(dve):
            raw = herm_raw[:].rearrange("i (o d) -> i d o", d=DEG + 1)
            dve.wait_ge(weights_loaded, 80)
            done = 0
            for n, d in enumerate(range(DEG, -1, -1)):
                for k in range(d, -1, -2):
                    first = d >= DEG - 1
                    if first:
                        ins = dve.tensor_scalar(herm[:, k, :], raw[:, d, :], float(CHANGE[d, k]), None, ALU.mult)
                    else:
                        ins = dve.scalar_tensor_tensor(herm[:, k, :], raw[:, d, :], float(CHANGE[d, k]),
                                                       herm[:, k, :], ALU.mult, ALU.add)
                    ins.then_inc(herm_step, 1)
                    done += 1
                dve.wait_ge(herm_step, done)
            dve.wait_ge(turned, 2)
            dve.wait_ge(turned_used, 1)
            dve.tensor_copy(w_t[:], banks[7][:, P:2 * P]).then_inc(turned_used, 1)
            dve.memset(bn_tmp[:], 1e-5).then_inc(herm_ready, 1)

            def step(r, c, s1, s2, s3, s4):
                if s4:
                    n = c - 2
                    wait(dve, wx_ready, r, n)
                    dve.sem_inc(passed, 1)
                    dst = stats[:, n, :] if isinstance(r, int) else stats[:, bass.ds(4 * r + n, 1), :]
                    dve.bn_stats(dst if isinstance(r, int) else dst.rearrange("p a s -> p (a s)"), wx[:, n % 4, :])\
                       .then_inc(stats_ready, 1)
                if s3:
                    wait(dve, conv_done, r, c - 1)
                    wait_slot(dve, x1_stored, r, c - 5)
                    dve.tensor_tensor(x1[:, (c - 1) % 4, :], p_conv[(c - 1) % 2][:], x_in[:, (c - 1) % 4, :], ALU.add)\
                       .then_inc(x1_ready, 1)
                if s1:
                    k = (c + 1) % 2
                    wait(dve, squared, r, c + 1)
                    wait(dve, rstd_ready, r, c - 1)
                    dve.tensor_reduce(var[:, k, :], sub_tiles(squares[:, k, :]), AX.X, ALU.add).then_inc(var_ready, 1)
                    wait(dve, rstd_ready, r, c + 1)
                    wait(dve, flipped, r, c - 1)
                    dve.tensor_tensor(sub_tiles(normed[:, k, :]), sub_tiles(p_centred[:]), per_token(rstd[:, k, :]),
                                      ALU.mult).then_inc(norm_ready, 1)
                if s3:
                    k = (c - 1) % 2
                    wait(dve, squared2, r, c - 1)
                    wait(dve, rstd2_ready, r, c - 3)
                    dve.tensor_reduce(var2[:, k, :], sub_tiles(squares2[:, k, :]), AX.X, ALU.add).then_inc(var2_ready, 1)
                    wait(dve, rstd2_ready, r, c - 1)
                    wait(dve, flipped2, r, c - 3)
                    dve.tensor_tensor(sub_tiles(normed2[:, k, :]), sub_tiles(p_centred2[:]), per_token(rstd2[:, k, :]),
                                      ALU.mult).then_inc(norm2_ready, 1)
                if s1:
                    k = (c + 1) % 2
                    wait(dve, gauss_ready, r, c + 1)
                    wait(dve, conv_done, r, c - 1)
                    dve.tensor_tensor(basis[:, k, 1, :], z[:, k, :], basis[:, k, 0, :], ALU.mult).then_inc(basis_ready, 1)
                    for d in range(2, DEG + 1):
                        if d > 2:
                            wait(dve, basis_ready, r, c + 1, per=DEG, sub=d - 2)
                        dve.scalar_tensor_tensor(basis[:, k, d, :], z2[:, k, :], float(CENTRE[d]), basis[:, k, d - 2, :],
                                                 ALU.subtract, ALU.mult).then_inc(basis_ready, 1)

            pipeline_a(dve, step)
            dve.wait_ge(stats_ready, TILES)
            dve.bn_aggr(mean_var[:], stats[:].rearrange("p n s -> p (n s)")).then_inc(bn_step, 1)
            dve.wait_ge(bn_step, 1)
            dve.tensor_scalar(bn_tmp[:, 0:1], mean_var[:, 1:2], 1e-5, None, ALU.add).then_inc(bn_step, 1)
            dve.wait_ge(bn_root, 1)
            dve.tensor_tensor(norm_a[:], gam[:], bn_tmp[:, 1:2], ALU.mult).then_inc(bn_step, 1)
            dve.wait_ge(bn_step, 3)
            dve.tensor_tensor(bn_tmp[:, 2:3], mean_var[:, 0:1], norm_a[:], ALU.mult).then_inc(bn_step, 1)
            dve.wait_ge(bn_step, 4)
            dve.tensor_tensor(norm_b[:], bet[:], bn_tmp[:, 2:3], ALU.subtract).then_inc(bn_step, 1)

        def group_tiles(tiles, g, img):
            n = (g * GROUP + img) * IMG_TILES
            return tiles[n:n + IMG_TILES, :, :].rearrange("t p n -> p t n")

        def group_slot(g, img):
            lo = WARM + img * T
            return wxy[g % 3][:, lo:lo + T].rearrange("p (t n) -> p t n", n=TOK)

        def if_again(eng):
            eng.wait_ge(count_ready, 1)
            return eng.If(eng.value_load(close_count[0:1, 0:1], min_val=0, max_val=P) < P)

        def sync_b(sp):
            def load(g):
                for img in range(GROUP):
                    sp.dma_start(group_slot(g, img), group_tiles(wx_dram, g, img)).then_inc(group_loaded[g % 3], 16)

            for g in range(2):
                load(g)
            for g in range(2, GROUPS + 2):
                done = g - 2
                if g < GROUPS and g < 3:
                    load(g)
                sp.wait_ge(placed[done % 2], SEG * (done // 2 + 1) + 2)
                for img in range(GROUP):
                    sp.dma_start(group_tiles(y_dram, done, img), group_slot(done, img)).then_inc(group_stored[done % 3], 16)
                if g + 1 < GROUPS:
                    sp.wait_ge(group_stored[done % 3], 16 * GROUP * (done // 3 + 1))
                    load(g + 1)
            for k in range(3):
                sp.wait_ge(group_stored[k], 16 * GROUP * len(range(k, GROUPS, 3)))
            with if_again(sp):
                wx_at = wx_dram.rearrange("(b t) p n -> t p b n", t=IMG_TILES)
                y_at = y_dram.rearrange("(b t) p n -> t p b n", t=IMG_TILES)
                with sp.Fori(0, IMG_TILES) as t:
                    for part in range(TOK // AGAIN):
                        cols = slice(part * AGAIN, (part + 1) * AGAIN)
                        n = t * (TOK // AGAIN) + part
                        sp.dma_start(again_wx[:], wx_at[bass.ds(t, 1), :, :, cols].rearrange("t p b n -> p (t b) n"))\
                          .then_inc(again_loaded, 16)
                        sp.wait_ge(again_placed, n * AGAIN + AGAIN + 1)
                        sp.sem_inc(passed, 1)
                        sp.dma_start(y_at[bass.ds(t, 1), :, :, cols].rearrange("t p b n -> p (t b) n"), again_y[:])\
                          .then_inc(again_stored, 16)
                        sp.wait_ge(again_stored, n * 16 + 16)
                        sp.sem_inc(passed, 1)

        def tensor_b(pe):
            def step(g, s, odd, warm):
                k = g % 2
                pe.wait_ge(state_ready[k], states(g, s, warm))
                pe.matmul(banks[k][:, 0:LANES], v_t[:], state[k][:, 1 - odd, :], start=True, stop=True)\
                  .then_inc(product_done[k], 1)

            in_halves(pe, step)
            pe.wait_ge(gap_step, 2 * GROUPS + 3)
            pe.matmul(banks[2][0:1, 0:1], close[:, 0:1], close[:, 1:2], start=True, stop=True).then_inc(count_done, 1)
            with if_again(pe):
                with pe.Fori(0, T) as t:
                    pe.wait_ge(again_step, t + 1)
                    pe.matmul(banks[3][:, 0:B], v_t[:], again_state[:], start=True, stop=True).then_inc(again_product, 1)

        def vector_b(dve):
            for slot in wxy:
                dve.memset(slot[:, 0:WARM], 0.0).then_inc(pads_set, 1)
            dve.wait_ge(pads_set, 3)

            def begin(g):
                k = g % 2
                dve.wait_ge(group_loaded[g % 3], 16 * GROUP * (g // 3 + 1))
                if g >= 2:
                    dve.wait_ge(placed[k], SEG * (g // 2) + 2)
                    dve.wait_ge(gap_step, 2 * (g - 1))
                dve.memset(state[k][:, 1, :], 0.0).then_inc(state_ready[k], 1)

            def step(g, s, odd, warm):
                k = g % 2
                dve.wait_ge(product_done[k], (g // 2) * STEPS + s + 1)
                dve.scalar_tensor_tensor(preact[k][:], tokens_at(g, s), norm_a[:], banks[k][:, 0:LANES],
                                         ALU.mult, ALU.add).then_inc(preact_ready[k], 1)

            def warmed(g):
                k = g % 2
                dve.wait_ge(state_ready[k], states(g, WARM, True))
                dve.memset(state[k][:, 1, 0:SEGS * (GROUP - 1) + 1:SEGS], 0.0).then_inc(state_ready[k], 1)
                dve.wait_ge(state_ready[k], states(g, WARM, False))
                dve.tensor_copy(first_state[k][:], state[k][:, 1, :]).then_inc(first_kept, 1)

            def end(g):
                k = g % 2
                dve.wait_ge(state_ready[k], states(g, STEPS, False))
                dve.wait_ge(first_kept, g + 1)
                last = state[k][:, 1, :].rearrange("p (b k) -> p b k", b=GROUP)
                first = first_state[k][:].rearrange("p (b k) -> p b k", b=GROUP)
                dve.tensor_tensor(gap[:], last[:, :, 0:SEGS - 1], first[:, :, 1:SEGS], ALU.subtract).then_inc(gap_step, 1)
                dve.wait_ge(gap_step, 2 * g + 1)
                dve.tensor_reduce(gap_max[:, g:g + 1], gap[:].rearrange("p b k -> p (b k)"), AX.X, ALU.max,
                                  apply_absolute_value=True).then_inc(gap_step, 1)

            in_halves(dve, step, begin, warmed, end)
            dve.memset(close[:, 1:2], 1.0).then_inc(gap_step, 1)
            dve.wait_ge(gap_step, 2 * GROUPS + 1)
            dve.tensor_reduce(gap_max[:, GROUPS:GROUPS + 1], gap_max[:, 0:GROUPS], AX.X, ALU.max).then_inc(gap_step, 1)
            dve.wait_ge(gap_step, 2 * GROUPS + 2)
            dve.tensor_scalar(close[:, 0:1], gap_max[:, GROUPS:GROUPS + 1], TOLERANCE, None, ALU.is_le)\
               .then_inc(gap_step, 1)
            dve.wait_ge(count_done, 1)
            dve.tensor_copy(close_count[:], banks[2][0:1, 0:1]).then_inc(count_ready, 1)
            with if_again(dve):
                dve.wait_ge(again_loaded, 16)
                dve.memset(again_state[:], 0.0).then_inc(again_step, 1)
                with dve.Fori(0, T // AGAIN) as n:
                    dve.wait_ge(again_loaded, n * 16 + 16)
                    dve.sem_inc(passed, 1)
                    with dve.Fori(0, AGAIN) as t:
                        dve.wait_ge(again_product, n * AGAIN + t + 1)
                        dve.scalar_tensor_tensor(again_pre[:], again_wx[:, :, bass.ds(t, 1)].rearrange("p b n -> p (b n)"),
                                                 norm_a[:], banks[3][:, 0:B], ALU.mult, ALU.add).then_inc(again_preact, 1)

        def scalar_b(act):
            def step(g, s, odd, warm):
                k = g % 2
                act.wait_ge(preact_ready[k], (g // 2) * STEPS + s + 1)
                if not warm:
                    act.wait_ge(placed[k], (g // 2) * SEG + s - WARM + 1)
                act.activation(state[k][:, odd, :], preact[k][:], ACT.Sigmoid, bias=norm_b[:])\
                   .then_inc(state_ready[k], 1)

            in_halves(act, step)
            with if_again(act):
                with act.Fori(0, T) as t:
                    act.wait_ge(again_preact, t + 1)
                    act.wait_ge(again_placed, t + 1)
                    act.activation(again_state[:], again_pre[:], ACT.Sigmoid, bias=norm_b[:]).then_inc(again_step, 1)

        def gpsimd_b(pool):
            for k in range(2):
                pool.sem_inc(placed[k], 2)

            def step(g, s, odd, warm):
                if warm:
                    return
                k = g % 2
                pool.wait_ge(state_ready[k], states(g, s + 1, False))
                pool.sem_inc(passed, 1)
                pool.tensor_copy(tokens_at(g, s), state[k][:, odd, :]).then_inc(placed[k], 1)

            in_halves(pool, step)
            with if_again(pool):
                pool.sem_inc(again_placed, 1)
                with pool.Fori(0, T // AGAIN) as n:
                    with pool.Fori(0, AGAIN) as t:
                        pool.wait_ge(again_step, n * AGAIN + t + 2)
                        pool.sem_inc(passed, 1)
                        pool.tensor_copy(again_y[:, :, bass.ds(t, 1)].rearrange("p b n -> p (b n)"), again_state[:])\
                            .then_inc(again_placed, 1)

        def wait16(eng, s, r, c, **kw):
            if c >= 0:
                wait(eng, s, r, c, unroll=PT, **kw)

        def cols(c):
            return c // IMG_TILES, slice(c % IMG_TILES * TOK, (c % IMG_TILES + 1) * TOK)

        def img_tiles(tiles, r, img, t0=0, t1=IMG_TILES):
            n0 = img * IMG_TILES + t0
            if isinstance(r, int):
                return tiles[r * PT + n0:r * PT + n0 + t1 - t0, :, :].rearrange("t p n -> p t n")
            return tiles[bass.ds(r * PT + n0, t1 - t0), :, :].rearrange("t p n -> p t n")

        def sync_c(sp):
            sp.dma_start(gates_raw[:], gate_w).then_inc(c_loaded, 16)
            for half in range(2):
                sp.dma_start(gate_bias[half * E:(half + 1) * E, :], gate_b.unsqueeze(1)).then_inc(c_loaded, 16)
            sp.wait_ge(c_const, 1)
            for half in range(2):
                sp.dma_start(taps[half * IMG_W:(half + 1) * IMG_W, 1 + half:5 + half, :],
                             blur.rearrange("u v -> (u v)").partition_broadcast(IMG_W)
                             .rearrange("p (u v) -> p u v", v=4)).then_inc(c_loaded, 16)

            def load(r, img):
                for tiles, dst in ((x1_dram, img_x), (y_dram, img_y)):
                    sp.dma_start(dst[:, img, :].rearrange("p (t n) -> p t n", n=TOK), img_tiles(tiles, r, img))\
                      .then_inc(img_loaded[img], 16)

            def body(r, last):
                for c in range(PT):
                    img, at = cols(c)
                    wait16(sp, x3_ready, r, c)
                    sp.dma_start(img_tiles(x3_dram, r, img, c % IMG_TILES, c % IMG_TILES + 1)
                                 .rearrange("p t n -> p (t n)"), img_x[:, img, at]).then_inc(x3_stored[img], 16)
                    if c % IMG_TILES == 1 and c > 1 and not last:
                        reload(r, 0)
                if not last:
                    reload(r, 1)
                sp.wait_ge(prob_ready, r + 1)
                dst = prob_dram[r, :, :] if isinstance(r, int) else prob_dram[bass.ds(r, 1), :, :].rearrange("a p n -> p (a n)")
                sp.dma_start(dst, prob[:]).then_inc(prob_stored, 16)

            def reload(r, img):
                sp.wait_ge(x3_stored[img], 16 * IMG_TILES * r + 16 * IMG_TILES)
                wait16(sp, gated, r, (img + 1) * IMG_TILES - 1)
                sp.sem_inc(passed, 1)
                load(r + 1, img)

            sp.sem_inc(prob_stored, 16)
            for img in range(2):
                load(0, img)
            with sp.Fori(0, PAIRS - 1) as r:
                body(r, False)
            body(PAIRS - 1, True)
            for img in range(2):
                sp.wait_ge(x3_stored[img], 16 * IMG_TILES * PAIRS)
            sp.wait_ge(prob_stored, 16 * PAIRS + 16)

        def gate_banks(c):
            k = 4 + c % 2 * 2
            return psum[:, k:k + 2, 0:2 * (P + E)].rearrange("p k (j n) -> p k j n", n=P + E)

        def tensor_c(pe):
            pe.wait_ge(c_loaded, 80)
            pe.transpose(banks[0][:, 0:E], gates_raw[:], ident[0:E, 0:E]).then_inc(gates_turned, 1)
            pe.wait_ge(gates_copied, 1)
            pe.matmul(banks[1][:, 0:E], centre[:], gates_t[:], start=True, stop=True).then_inc(gates_turned, 1)
            pe.wait_ge(c_setup, 1)
            pe.sem_inc(pooled_done, 1)

            def body(r):
                def step(j):
                    c = j + 2
                    if 0 <= c < PT:
                        img, at = cols(c)
                        wait16(pe, x2_ready, r, c)
                        wait16(pe, c_normed, r, c - 2)
                        for s in range(SUB):
                            lo = at.start + s * P
                            mm = pe.matmul(banks[c % 2][:, s * P:(s + 1) * P], img_x[:, img, lo:lo + P], centre[:],
                                           start=True, stop=True)
                        mm.then_inc(c_centred, 1)
                    c = j
                    if 0 <= c < PT:
                        img, at = cols(c)
                        wait16(pe, c_normed, r, c + 1 if (c + 1) % IMG_TILES else c)
                        wait16(pe, x3_ready, r, c - 2)
                        first = c % IMG_TILES * SUB
                        reach = range(max(first - 1, 0), min(first + SUB + 1, SUBS))
                        for s in reach:
                            lo, hi = max(s - 1, first), min(s + 1, first + SUB - 1)
                            n = img * SUBS + s
                            mm = pe.matmul(banks[2 + c % 2][:, (lo - first) * P:(hi + 1 - first) * P],
                                           blur_in[:, n // SUB % 4, n % SUB * P:(n % SUB + 1) * P],
                                           band[:].rearrange("p w j -> p (w j)")[:, (lo - s + 1) * P:(hi - s + 2) * P],
                                           start=(s == reach[0]), stop=(s == reach[-1]), skip_group_check=True)
                        mm.then_inc(blurred, 1)
                    c = j - 1
                    if 0 <= c < PT:
                        img, at = cols(c)
                        wait16(pe, x3_ready, r, c)
                        wait16(pe, logits_tm_ready, r, c - 2)
                        for s in range(SUB):
                            lo = at.start + s * P
                            mm = pe.matmul(gate_banks(c)[:, s // 2, s % 2, :], img_x[:, img, lo:lo + P], centre_gates[:],
                                           start=True, stop=True)
                        mm.then_inc(gated, 1)

                over_tiles(step, 2)
                wait16(pe, logits_tm_ready, r, PT - 1)
                for q in range(IMG_TILES):
                    if q >= 2:
                        pe.wait_ge(logits_ready, r * IMG_TILES + q - 1)
                    for s in range(SUB):
                        mm = pe.transpose(banks[q % 2][:, s * P:(s + 1) * P],
                                          logits_tm[:, q * SUB + s, :, :].rearrange("p i e -> p (i e)"), ident[:])
                    mm.then_inc(logits_turned, 1)

                def turn(q):
                    if q >= 2:
                        pe.wait_ge(prob_tm_ready, r * IMG_TILES + q - 1)
                    for s in range(SUB):
                        lo = q * TOK + s * P
                        mm = pe.transpose(banks[2 + q % 2][:, s * P:(s + 1) * P], prob[:, lo:lo + P], ident[:])
                    mm.then_inc(prob_turned, 1)

                pe.wait_ge(prob_ready, r + 1)
                turn(0)
                for q in range(IMG_TILES):
                    if q + 1 < IMG_TILES:
                        turn(q + 1)
                    pe.wait_ge(prob_tm_ready, r * IMG_TILES + q + 1)
                    for s in range(SUB):
                        for img in range(2):
                            mm = pe.matmul(banks[4 + img][:, 0:E], tokens[:, img, q * SUB + s, :],
                                           prob_tm[:, q % 2, s, img * E:(img + 1) * E],
                                           start=(q == 0 and s == 0), stop=(q == IMG_TILES - 1 and s == SUB - 1))
                mm.then_inc(pooled_done, 1)

            with pe.Fori(0, PAIRS) as r:
                body(r)

        def scalar_c(act):
            def body(r):
                def step(j):
                    c = j + 2
                    if 0 <= c < PT:
                        wait16(act, c_centred, r, c)
                        wait16(act, c_summed, r, c - 2)
                        act.activation(sq_c[:, c % 2, :], banks[c % 2][:], ACT.Square).then_inc(c_squared, 1)
                    c = j - 1
                    if 0 <= c < PT:
                        img, _ = cols(c)
                        s = c % IMG_TILES * SUB
                        wait16(act, gated, r, c)
                        wait16(act, t_summed, r, c - 2)
                        act.activation(sq_t[:, c % 2, :].rearrange("p (k j n) -> p k j n", k=2, j=2),
                                       gate_banks(c)[:, :, :, 0:P], ACT.Square).then_inc(t_squared, 1)
                        if c == 0:
                            act.wait_ge(pooled_done, r + 1)
                        act.activation(tokens[:, img, s:s + SUB, :].rearrange("p (k j) n -> p k j n", k=2),
                                       gate_banks(c)[:, :, :, 0:P], ACT.Copy, scale=ROOT_C).then_inc(t_kept, 1)

                over_tiles(step, 2)
                for q in range(IMG_TILES):
                    act.wait_ge(logits_turned, r * IMG_TILES + q + 1)
                    act.activation(logits[:, q * TOK:(q + 1) * TOK], banks[q % 2][:], ACT.Identity, bias=gate_bias[:])\
                       .then_inc(logits_ready, 1)
                act.wait_ge(select_step, r * 6 + 2)
                act.wait_ge(prob_stored, 16 * r + 16)
                act.activation(prob[:], logits[:], ACT.Exp, bias=minus_max[:], accum_out=exp_sum[:]).then_inc(exp_ready, 1)

            with act.Fori(0, PAIRS) as r:
                body(r)

        def gpsimd_c(pool):
            pool.memset(taps[:], 0.0).then_inc(c_const, 1)
            for k, (m, shift) in enumerate(((diags, 0), (diags_low, IMG_W))):
                pool.memset(m[:], 0.0).then_inc(diag_step, 1)
                pool.wait_ge(diag_step, 2 * k + 1)
                pool.affine_select(out=m[:], in_=m[:], compare_op=ALU.not_equal, fill=1.0, base=shift + 1,
                                   pattern=[[-1, 4], [1, IMG_W]], channel_multiplier=-1).then_inc(diag_step, 1)

            def body(r):
                def step(j):
                    c = j + 2
                    k = c % 2
                    if 0 <= c < PT:
                        wait16(pool, c_summed, r, c)
                        pool.tensor_tensor(sum_c_eps[:, k, :], sum_c[:, k, :], eps_c[:], ALU.add).then_inc(c_eps_added, 1)
                        wait16(pool, c_eps_added, r, c)
                        wait16(pool, c_normed, r, c - 2)
                        pool.tensor_tensor(root_c[:, k, :], sum_c_eps[:, k, :], minus_half[:], ALU.pow)\
                            .then_inc(c_root_ready, 1)
                    c = j - 1
                    k = c % 2
                    if 0 <= c < PT:
                        s = c % IMG_TILES * SUB
                        wait16(pool, t_summed, r, c)
                        pool.tensor_tensor(sum_t_eps[:, k, :], sum_t[:, k, :], eps_t[:], ALU.add).then_inc(t_eps_added, 1)
                        wait16(pool, t_eps_added, r, c)
                        pool.tensor_tensor(root_t[:, s:s + SUB, c // IMG_TILES], sum_t_eps[:, k, :], minus_half[:], ALU.pow)\
                            .then_inc(t_root_ready, 1)

                over_tiles(step, 2)

            with pool.Fori(0, PAIRS) as r:
                body(r)

        def vector_c(dve):
            dve.wait_ge(gates_turned, 1)
            dve.tensor_copy(gates_t[:], banks[0][:, 0:E]).then_inc(gates_copied, 1)
            dve.wait_ge(gates_turned, 2)
            dve.tensor_scalar(centre_gates[:, P:P + E], banks[1][:, 0:E], ROOT_C, None, ALU.mult).then_inc(gates_copied, 1)
            dve.tensor_copy(centre_gates[:, 0:P], centre[:]).then_inc(gates_copied, 1)
            dve.wait_ge(diag_step, 4)
            dve.tensor_copy(diags[IMG_W:P, :, :], diags_low[IMG_W:P, :, :]).then_inc(gates_copied, 1)
            dve.wait_ge(c_loaded, 80)
            dve.tensor_scalar(taps[:], taps[:], ROOT_C, None, ALU.mult).then_inc(gates_copied, 1)
            dve.wait_ge(gates_copied, 5)
            for v in range(4):
                for w in range(6):
                    if v == 0:
                        ins = dve.tensor_scalar(band[:, w, :], diags[:, v, :], taps[:, w, v:v + 1], None, ALU.mult)
                    else:
                        ins = dve.scalar_tensor_tensor(band[:, w, :], diags[:, v, :], taps[:, w, v:v + 1], band[:, w, :],
                                                       ALU.mult, ALU.add)
                    ins.then_inc(gates_copied, 1)
                dve.wait_ge(gates_copied, 5 + 6 * (v + 1))
            dve.memset(exp_inv[:], 0.0).then_inc(c_setup, 1)

            def body(r):
                def step(j):
                    c = j + 3
                    if 0 <= c < PT:
                        img, at = cols(c)
                        if c % IMG_TILES == 0:
                            dve.wait_ge(img_loaded[img], 32 * r + 32)
                        dve.tensor_tensor(img_x[:, img, at], img_x[:, img, at], img_y[:, img, at], ALU.add)\
                           .then_inc(x2_ready, 1)
                    c = j + 2
                    if 0 <= c < PT:
                        k = c % 2
                        wait16(dve, c_squared, r, c)
                        wait16(dve, c_root_ready, r, c - 2)
                        dve.tensor_reduce(sum_c[:, k, :], sub_tiles(sq_c[:, k, :]), AX.X, ALU.add).then_inc(c_summed, 1)
                        wait16(dve, c_root_ready, r, c)
                        wait16(dve, blurred, r, c - 3)
                        dve.tensor_tensor(sub_tiles(blur_in[:, c % 4, :]), sub_tiles(banks[k][:]),
                                          per_token(root_c[:, k, :]), ALU.mult).then_inc(c_normed, 1)
                    c = j
                    if 0 <= c < PT:
                        img, at = cols(c)
                        wait16(dve, blurred, r, c)
                        dve.tensor_tensor(img_x[:, img, at], banks[2 + c % 2][:], img_x[:, img, at], ALU.add)\
                           .then_inc(x3_ready, 1)
                    c = j - 1
                    if 0 <= c < PT:
                        k = c % 2
                        s = c % IMG_TILES * SUB
                        wait16(dve, t_squared, r, c)
                        wait16(dve, t_eps_added, r, c - 2)
                        dve.tensor_reduce(sum_t[:, k, :], sub_tiles(sq_t[:, k, :]), AX.X, ALU.add).then_inc(t_summed, 1)
                        wait16(dve, t_root_ready, r, c)
                        wait16(dve, t_kept, r, c)
                        scale = root_t[:, s:s + SUB, c // IMG_TILES].rearrange("p (k j) -> p k j", k=2).unsqueeze(3)\
                            .to_broadcast([P, 2, 2, E])
                        dve.tensor_tensor(logits_tm[:, s:s + SUB, c // IMG_TILES, :].rearrange("p (k j) e -> p k j e", k=2),
                                          gate_banks(c)[:, :, :, P:P + E], scale, ALU.mult).then_inc(logits_tm_ready, 1)

                over_tiles(step, 3)
                alone(dve, logits_ready, r * IMG_TILES + IMG_TILES)
                dve.max(top8[:], logits[:]).then_inc(select_step, 1)
                dve.wait_ge(select_step, r * 6 + 1)
                dve.tensor_scalar(minus_max[:], top8[:, 0:1], -1.0, None, ALU.mult).then_inc(select_step, 1)
                alone(dve, exp_ready, r + 1)
                dve.match_replace(logits[:], top8[:], logits[:], LOW).then_inc(select_step, 1)
                dve.reciprocal(exp_inv[:], exp_sum[:]).then_inc(select_step, 1)
                dve.wait_ge(select_step, r * 6 + 4)
                dve.scalar_tensor_tensor(prob[:], logits[:], LOW, prob[:], ALU.is_equal, ALU.mult).then_inc(select_step, 1)
                dve.wait_ge(select_step, r * 6 + 5)
                dve.tensor_scalar(prob[:], prob[:], exp_inv[:], None, ALU.mult).then_inc(prob_ready, 1)
                dve.sem_inc(select_step, 1)
                for q in range(IMG_TILES):
                    dve.wait_ge(prob_turned, r * IMG_TILES + q + 1)
                    scale = root_t[:, q * SUB:(q + 1) * SUB, :].unsqueeze(3).to_broadcast([P, SUB, 2, E])
                    dve.tensor_tensor(prob_tm[:, q % 2, :, :].rearrange("p s (i e) -> p s i e", i=2),
                                      banks[2 + q % 2][:].rearrange("p (s i e) -> p s i e", s=SUB, i=2), scale, ALU.mult)\
                       .then_inc(prob_tm_ready, 1)
                alone(dve, pooled_done, r + 2)
                for img in range(2):
                    dve.tensor_copy(pooled[:, :, bass.ds(2 * r + img, 1)].rearrange("p e b -> p (e b)"),
                                    banks[4 + img][:, 0:E]).then_inc(pooled_ready, 1)

            with dve.Fori(0, PAIRS) as r:
                body(r)

        def expert_of(ap, r, c):
            if isinstance(r, int):
                return ap[UE * r + c]
            return ap[bass.ds(UE * r + c, 1)].rearrange("a d h -> (a d) h")

        def sync_d(sp):
            sp.dma_start(b1_raw[:], w1[:, P, :]).then_inc(bias1_loaded, 16)

            def load(r, c):
                sp.dma_start(w1_in[:, c, :], expert_of(w1[:, 0:P, :], r, c)).then_inc(w_loaded[c], 16)
                sp.dma_start(w2_in[:, c, :, :], expert_of(w2[:, 0:HID, :], r, c).rearrange("(k p) o -> p k o", p=P))\
                  .then_inc(w_loaded[c], 16)

            for k in range(2):
                sp.sem_inc(eo_stored[k], 16)
            for c in range(UE):
                load(0, c)

            def body(r, last):
                for c in range(UE):
                    sp.wait_ge(eo_ready, r * UE + c + 1)
                    sp.sem_inc(passed, 1)
                    if not last:
                        load(r + 1, c)
                    if c % 4 == 3:
                        k = c // 4
                        dst = (expert_dram[:, r * UE + c - 3:r * UE + c + 1, :] if last
                               else expert_dram[:, bass.ds(UE * r + c - 3, 4), :])
                        sp.dma_start(dst, eo[:, k, :, :]).then_inc(eo_stored[k], 16)

            rounds_d(sp, body)
            for k in range(2):
                sp.wait_ge(eo_stored[k], 16 + 16 * (E // UE))

        def tensor_d(pe):
            pe.wait_ge(bias1_loaded, 16)
            for k in range(HK):
                mm = pe.transpose(banks[4][:, k * E:(k + 1) * E], b1_raw[:, k * P:(k + 1) * P], ident[0:E, 0:E])
            mm.then_inc(bias1_turned, 1)

            def hidden(r, c):
                if c == UE:
                    r, c = r + 1, 0
                e = UE * r + c
                pe.wait_ge(w_loaded[c], 32 * r + 32)
                if not isinstance(r, int) or e >= 2:
                    pe.wait_ge(hid_pre_ready, e - 1)
                for k in range(HK):
                    mm = pe.matmul(banks[c % 2][:, k * B:(k + 1) * B], w1_in[:, c, k * P:(k + 1) * P],
                                   pooled[:, e, :] if isinstance(r, int)
                                   else pooled[:, bass.ds(e, 1), :].rearrange("p a b -> p (a b)"), start=True, stop=True)
                mm.then_inc(hid_done, 1)

            def output(r, c):
                pe.wait_ge(hid_ready, UE * r + c + 1)
                if not isinstance(r, int) or UE * r + c >= 2:
                    pe.wait_ge(eo_ready, UE * r + c - 1)
                for k in range(HK):
                    mm = pe.matmul(banks[2 + c % 2][0:B, 0:O], hid[:, c % 2, k * B:(k + 1) * B], w2_in[:, c, k, :],
                                   start=(k == 0), stop=(k == HK - 1))
                mm.then_inc(eo_done, 1)

            def body(r, last):
                for c in range(UE):
                    if not (last and c == UE - 1):
                        hidden(r, c + 1)
                    output(r, c)

            hidden(0, 0)
            body(0, False)
            with pe.Fori(1, E // UE - 1) as r:
                body(r, False)
            body(E // UE - 1, True)

        def vector_d(dve):
            dve.wait_ge(bias1_turned, 1)
            dve.tensor_copy(b1_t[:], banks[4][:, 0:HK * E].rearrange("p (k e) -> p e k", k=HK)).then_inc(bias1_ready, 1)
            dve.wait_ge(bias1_ready, 1)

            def body(r, last):
                for c in range(UE):
                    e = UE * r + c
                    dve.wait_ge(hid_done, e + 1)
                    bias = b1_t[:, e, :] if last else b1_t[:, bass.ds(e, 1), :].rearrange("p a k -> p (a k)")
                    dve.tensor_tensor(hid_pre[:, c % 2, :].rearrange("p (k b) -> p k b", k=HK),
                                      banks[c % 2][:, 0:HK * B].rearrange("p (k b) -> p k b", k=HK),
                                      bias.unsqueeze(2).to_broadcast([P, HK, B]), ALU.add).then_inc(hid_pre_ready, 1)

            rounds_d(dve, body)

        def scalar_d(act):
            def body(r, last):
                for c in range(UE):
                    e = UE * r + c
                    act.wait_ge(hid_pre_ready, e + 1)
                    act.activation(hid[:, c % 2, :], hid_pre[:, c % 2, :], ACT.Gelu).then_inc(hid_ready, 1)
                    act.wait_ge(eo_done, e + 1)
                    if c % 4 == 0:
                        act.wait_ge(eo_stored[c // 4], 16 * r + 16)
                    act.activation(eo[:, c // 4, c % 4, :], banks[2 + c % 2][0:B, 0:O], ACT.Copy).then_inc(eo_ready, 1)

            rounds_d(act, body)

        def gpsimd_d(pool):
            pass

        def sync_e(sp):
            by_expert = expert_dram.rearrange("(q i) e o -> i e q o", i=2)
            for img in range(2):
                half = slice(img * E, (img + 1) * E)
                sp.dma_start(outputs[half, :, :], by_expert[img]).then_inc(outputs_loaded, 16)
                sp.dma_start(b2_in[half, :], w2[:, HID, :]).then_inc(outputs_loaded, 16)

            def load(r, c):
                q = 2 * r + c
                src = prob_dram[q, :, :] if isinstance(q, int) else prob_dram[bass.ds(q, 1), :, :].rearrange("a p n -> p (a n)")
                sp.dma_start(prob_in[:, c, :], src).then_inc(pair_loaded[c], 16)
                for img in range(2):
                    sp.dma_start(x3_in[:, 2 * c + img, :].rearrange("p (t n) -> p t n", n=TOK),
                                 img_tiles(x3_dram, q, img)).then_inc(pair_loaded[c], 16)

            def store(r, c, img):
                b = 4 * r + 2 * c + img
                dst = out_img[b, :, :] if isinstance(b, int) else out_img[bass.ds(b, 1), :, :].rearrange("a p n -> p (a n)")
                sp.dma_start(dst, x3_in[:, 2 * c + img, :]).then_inc(out_stored[c], 16)

            for c in range(2):
                load(0, c)

            def body(r, last):
                for c in range(2):
                    for img in range(2):
                        sp.wait_ge(out_ready, (4 * r + 2 * c + img + 1) * IMG_TILES)
                        sp.sem_inc(passed, 1)
                        store(r, c, img)
                    if not last:
                        sp.wait_ge(out_stored[c], 32 * r + 32)
                        sp.sem_inc(passed, 1)
                        load(r + 1, c)

            with sp.Fori(0, PAIRS // 2 - 1) as r:
                body(r, False)
            body(PAIRS // 2 - 1, True)
            for c in range(2):
                sp.wait_ge(out_stored[c], 32 * (PAIRS // 2))

        def tensor_e(pe):
            def body(r, first):
                for c in range(2):
                    pe.wait_ge(chosen_ready, 2 * r + c + 1)
                    pe.wait_ge(pair_loaded[c], 48 * r + 48)
                    for img in range(2):
                        half = slice(img * E, (img + 1) * E)
                        for t in range(IMG_TILES):
                            n = (2 * c + img) * IMG_TILES + t
                            if not first or n >= 8:
                                pe.wait_ge(out_ready, 4 * IMG_TILES * r + n - 7)
                            pe.matmul(banks[t][:], chosen[half, c, :], prob_in[half, c, t * TOK:(t + 1) * TOK],
                                      start=True, stop=True).then_inc(spread, 1)

            body(0, True)
            with pe.Fori(1, PAIRS // 2) as r:
                body(r, False)

        def vector_e(dve):
            dve.wait_ge(outputs_loaded, 64)
            dve.tensor_tensor(outputs[:], outputs[:], b2_in[:].unsqueeze(1).to_broadcast([P, PAIRS, O]), ALU.add)\
               .then_inc(outputs_ready, 1)
            dve.wait_ge(outputs_ready, 1)

            def choose(r, c):
                dve.tensor_copy(chosen[:, c, :], outputs[:, bass.ds(2 * r + c, 1), :].rearrange("p a o -> p (a o)"))\
                   .then_inc(chosen_ready, 1)

            with dve.Fori(0, PAIRS // 2) as r:
                for c in range(2):
                    choose(r, c)
                for c in range(2):
                    for img in range(2):
                        for t in range(IMG_TILES):
                            at = slice(t * TOK, (t + 1) * TOK)
                            dve.wait_ge(spread, 4 * IMG_TILES * r + (2 * c + img) * IMG_TILES + t + 1)
                            dve.tensor_tensor(x3_in[:, 2 * c + img, at], banks[t][:], x3_in[:, 2 * c + img, at], ALU.add)\
                               .then_inc(out_ready, 1)

        def scalar_e(act):
            pass

        def gpsimd_e(pool):
            pass

        block = ctx.enter_context(nc.Block())

        @block.sync
        def _(sp):
            run_phases(sp, sync_a, sync_b, sync_c, sync_d, sync_e)

        @block.tensor
        def _(pe):
            run_phases(pe, tensor_a, tensor_b, tensor_c, tensor_d, tensor_e)

        @block.scalar
        def _(act):
            run_phases(act, scalar_a, scalar_b, scalar_c, scalar_d, scalar_e)

        @block.gpsimd
        def _(pool):
            run_phases(pool, gpsimd_a, gpsimd_b, gpsimd_c, gpsimd_d, gpsimd_e)

        @block.vector
        def _(dve):
            run_phases(dve, vector_a, vector_b, vector_c, vector_d, vector_e)

_INS = ["x", "L0_conv_weights", "L0_ffn_W", "L0_ffn_V", "L0_ffn_gamma", "L0_ffn_beta", "L1_conv_kernel",
        "L1_ffn_gate_w", "L1_ffn_gate_b", "L1_ffn_weight1", "L1_ffn_weight2"]
_SCRATCH = [("x1", (256, 128, 512)), ("wx", (256, 128, 512)), ("y", (256, 128, 512)), ("x3", (256, 128, 512)),
            ("prob", (16, 128, 4096)), ("expert", (32, 64, 128))]


def kernel(**inputs):
    import concourse.bacc as _bacc
    from concourse import mybir as _mybir
    from concourse.bass_utils import run_bass_kernel_spmd as _run

    nc = _bacc.Bacc("TRN2", target_bir_lowering=False, num_devices=1)
    arrays, args = {}, []
    for name in _INS:
        a = np.ascontiguousarray(inputs[name])
        arrays[f"in_{name}_dram"] = a
        args.append(nc.dram_tensor(f"in_{name}_dram", a.shape, _mybir.dt.from_np(a.dtype), kind="ExternalInput").ap())
    out = nc.dram_tensor("out_0_dram", (32, 128, 64, 64), _mybir.dt.float32, kind="ExternalOutput").ap()
    scratch = [nc.dram_tensor(f"{name}_dram", shape, _mybir.dt.float32, kind="Internal").ap()
               for name, shape in _SCRATCH]
    metaformer(nc, *args, out, scratch)
    r = _run(nc, [arrays], core_ids=[0])
    return r.results[0]['out_0_dram']
```

```python
from contextlib import ExitStack

import numpy as np

import concourse.bass as bass
from concourse import mybir

F32 = mybir.dt.float32
I32 = mybir.dt.int32
ALU = mybir.AluOpType
ACT = mybir.ActivationFunctionType
AX = mybir.AxisListType

P = 128


def hermite_in_products(degree, z_scale):
    even = np.sort(np.unique(np.round((np.polynomial.hermite.hermgauss(8)[0] / z_scale) ** 2, 12)))
    odd = np.sort(np.unique(np.round((np.polynomial.hermite.hermgauss(7)[0] / z_scale) ** 2, 12)))[1:]
    order = {2: even[0], 4: even[2], 6: even[1], 8: even[3], 3: odd[0], 5: odd[1], 7: odd[2]}
    poly = np.polynomial.polynomial
    h = [np.array([np.pi ** -0.25]), np.array([0.0, np.sqrt(2.0) * z_scale * np.pi ** -0.25])]
    f = [np.array([1.0]), np.array([0.0, 1.0])]
    for k in range(2, degree + 1):
        h.append(poly.polysub(np.sqrt(2.0 / k) * poly.polymul([0.0, z_scale], h[-1]), np.sqrt((k - 1) / k) * h[-2]))
        f.append(poly.polymul([-order[k], 0.0, 1.0], f[-2]))
    change = np.zeros((degree + 1, degree + 1))
    for d in range(degree + 1):
        rest = np.zeros(degree + 1)
        rest[:len(h[d])] = h[d]
        for k in range(d, -1, -1):
            change[d, k] = rest[k]
            rest[:k + 1] -= change[d, k] * f[k]
    return order, change


def metaformer(nc, x, herm_w, ffn_w, ffn_v, gamma, beta, blur, gate_w, gate_b, w1, w2, out, scratch):
    B, C, IMG_H, IMG_W = x.shape
    T = IMG_H * IMG_W
    DEG = herm_w.shape[2] - 1
    E, _, HID = w1.shape
    O = w2.shape[2]
    TOK = 512
    IMG_TILES = T // TOK
    TILES = B * IMG_TILES
    SUB = TOK // P
    ROOT_C = float(np.sqrt(C))
    Z_SCALE = float(np.sqrt(2 * DEG + 1) + 1.0)
    CENTRE, CHANGE = hermite_in_products(DEG, Z_SCALE)
    assert C == P and O == P and 2 * E == P and T % TOK == 0

    x_img = x.rearrange("b c h w -> b c (h w)")
    out_img = out.rearrange("b c h w -> b c (h w)")
    x1_dram, wx_dram, y_dram, x3_dram, prob_dram, expert_dram = scratch

    ctx = ExitStack()
    with ctx:
        def sb(name, shape, dt=F32, scope=ctx):
            return scope.enter_context(nc.sbuf_tensor(name, shape, dt))

        def sem(name):
            return ctx.enter_context(nc.semaphore(name))

        def wait(eng, s, r, c, per=1, sub=None, unroll=4):
            sub = per if sub is None else sub
            if not isinstance(r, int) or c >= 0:
                eng.wait_ge(s, per * unroll * r + per * c + sub)

        def wait_slot(eng, slots, r, c, unroll=4):
            ring = len(slots)
            if not isinstance(r, int) or c >= 0:
                eng.wait_ge(slots[c % ring], 16 * (unroll // ring) * r + 16 * (c // ring + 1))

        psum = ctx.enter_context(nc.psum_tensor("psum", [P, 8, 512], F32))
        banks = [psum[:, i, :] for i in range(8)]

        ident = sb("ident", [P, P])
        centre = sb("centre", [P, P])
        minus_half = sb("minus_half", [P, 4])
        eps_c = sb("eps_c", [P, 4])
        eps_t = sb("eps_t", [P, 4])
        norm_a = sb("norm_a", [P, 1])
        norm_b = sb("norm_b", [P, 1])
        v_t = sb("v_t", [P, P])
        passed = sem("passed")
        phase_done = [sem(f"phase_{k}_done") for k in "abcde"]

        def run_phases(eng, *phases):
            for k, phase in enumerate(phases):
                if k:
                    eng.wait_ge(phase_done[k - 1], 5)
                phase(eng)
                eng.drain().then_inc(phase_done[k], 1)

        scope_a = ExitStack()
        herm_raw = sb("herm_raw", [P, P * (DEG + 1)], scope=scope_a)
        herm = sb("herm", [P, DEG + 1, P], scope=scope_a)
        w_raw = sb("w_raw", [P, P], scope=scope_a)
        w_t = sb("w_t", [P, P], scope=scope_a)
        v_raw = sb("v_raw", [P, P], scope=scope_a)
        gam = sb("gam", [P, 1], scope=scope_a)
        bet = sb("bet", [P, 1], scope=scope_a)
        x_in = sb("x_in", [P, 4, TOK], scope=scope_a)
        sub_stats = sb("sub_stats", [P, 2, SUB, 6], scope=scope_a)
        moments = sb("moments", [P, 2, SUB, 2], scope=scope_a)
        var_eps = sb("var_eps", [P, 2, SUB], scope=scope_a)
        rstd = sb("rstd", [P, 2, SUB], scope=scope_a)
        shift = sb("shift", [P, 2, SUB], scope=scope_a)
        z_tm = sb("z_tm", [P, 2, TOK], scope=scope_a)
        z2 = sb("z2", [P, 2, TOK], scope=scope_a)
        basis = sb("basis", [P, 2, DEG + 1, TOK], scope=scope_a)
        x1 = sb("x1", [P, 4, TOK], scope=scope_a)
        sub_stats2 = sb("sub_stats2", [P, 2, SUB, 6], scope=scope_a)
        moments2 = sb("moments2", [P, 2, SUB, 2], scope=scope_a)
        var2_eps = sb("var2_eps", [P, 2, SUB], scope=scope_a)
        rstd2 = sb("rstd2", [P, 2, SUB], scope=scope_a)
        shift2 = sb("shift2", [P, 2, SUB], scope=scope_a)
        t_tm = sb("t_tm", [P, 2, TOK], scope=scope_a)
        t_cm = sb("t_cm", [P, 2, TOK], scope=scope_a)
        wx = sb("wx", [P, 4, TOK], scope=scope_a)
        stats = sb("stats", [P, TILES, 6], scope=scope_a)
        mean_var = sb("mean_var", [P, 2], scope=scope_a)
        bn_tmp = sb("bn_tmp", [P, 4], scope=scope_a)
        scope_a.close()
        p_x, p_z, p_conv, p_x1, p_t, p_wx = (banks[0], banks[7]), banks[1], banks[2:4], banks[4], banks[5], banks[6]

        weights_loaded = sem("weights_loaded")
        ones_set = sem("ones_set")
        ident_set = sem("ident_set")
        herm_step = sem("herm_step")
        herm_ready = sem("herm_ready")
        turned = sem("turned")
        turned_used = sem("turned_used")
        x_loaded = [sem(f"x_loaded{i}") for i in range(4)]
        x_turned = sem("x_turned")
        sub_done = sem("sub_done")
        moments_ready = sem("moments_ready")
        eps_added = sem("eps_added")
        rstd_ready = sem("rstd_ready")
        shift_ready = sem("shift_ready")
        z_ready = sem("z_ready")
        z_turned = sem("z_turned")
        z2_ready = sem("z2_ready")
        gauss_ready = sem("gauss_ready")
        basis_ready = sem("basis_ready")
        conv_done = sem("conv_done")
        x1_ready = sem("x1_ready")
        x1_stored = [sem(f"x1_stored{i}") for i in range(4)]
        x1_turned = sem("x1_turned")
        sub2_done = sem("sub2_done")
        moments2_ready = sem("moments2_ready")
        eps2_added = sem("eps2_added")
        rstd2_ready = sem("rstd2_ready")
        shift2_ready = sem("shift2_ready")
        t_tm_ready = sem("t_tm_ready")
        t_turned = sem("t_turned")
        t_ready = sem("t_ready")
        wx_done = sem("wx_done")
        wx_ready = sem("wx_ready")
        stats_ready = sem("stats_ready")
        bn_step = sem("bn_step")
        bn_root = sem("bn_root")
        wx_stored = [sem(f"wx_stored{i}") for i in range(4)]

        def alone(eng, s, value):
            eng.wait_ge(s, value)
            eng.sem_inc(passed, 1)

        def pipeline(eng, step, unroll, start, lead, lag):
            rounds = (TILES - start - lead) // unroll
            for c in range(-lead, start):
                step(0, c, lambda d: 0 <= c + d < TILES)
            with eng.Fori(0, rounds) as r:
                for c in range(start, start + unroll):
                    step(r, c, lambda d: True)
            for c in range(start + rounds * unroll, TILES + lag):
                step(0, c, lambda d: 0 <= c + d < TILES)

        def tile_at(tiles, r, c, unroll):
            if isinstance(r, int):
                return tiles[c, :, :]
            return tiles[bass.ds(unroll * r + c, 1), :, :].rearrange("a p n -> p (a n)")

        def x_tile(r, c):
            part = slice(c % IMG_TILES * TOK, (c % IMG_TILES + 1) * TOK)
            if isinstance(r, int):
                return x_img[c // IMG_TILES, :, part]
            return x_img[bass.ds(r + c // IMG_TILES, 1), :, part].rearrange("a p n -> p (a n)")

        GROUP = 4
        GROUPS = B // GROUP
        SEG = IMG_W
        SEGS = T // SEG
        LANES = GROUP * SEGS
        WARM = 16
        HALF = (WARM + SEG) // 2
        TOLERANCE = 2.0 ** -21
        scope_b = ExitStack()
        wxy = [sb(f"wxy{i}", [P, WARM + GROUP * T], scope=scope_b) for i in range(3)]
        state = [sb(f"state{i}", [P, 2, LANES], scope=scope_b) for i in range(2)]
        preact = [sb(f"preact{i}", [P, LANES], scope=scope_b) for i in range(2)]
        first_state = [sb(f"first_state{i}", [P, LANES], scope=scope_b) for i in range(2)]
        gap = sb("gap", [P, GROUP, SEGS - 1], scope=scope_b)
        gap_max = sb("gap_max", [P, GROUPS + 1], scope=scope_b)
        close = sb("close", [P, 2], scope=scope_b)
        close_count = sb("close_count", [1, 1], I32, scope=scope_b)
        scope_b.close()
        AGAIN = 128
        scope_f = ExitStack()
        again_wx = sb("again_wx", [P, B, AGAIN], scope=scope_f)
        again_y = sb("again_y", [P, B, AGAIN], scope=scope_f)
        again_state = sb("again_state", [P, B], scope=scope_f)
        again_pre = sb("again_pre", [P, B], scope=scope_f)
        scope_f.close()

        pads_set = sem("pads_set")
        group_loaded = [sem(f"group_loaded{i}") for i in range(3)]
        group_stored = [sem(f"group_stored{i}") for i in range(3)]
        product_done = [sem(f"product_done{i}") for i in range(2)]
        preact_ready = [sem(f"preact_ready{i}") for i in range(2)]
        state_ready = [sem(f"state_ready{i}") for i in range(2)]
        placed = [sem(f"placed{i}") for i in range(2)]
        first_kept = sem("first_kept")
        gap_step = sem("gap_step")
        count_done = sem("count_done")
        count_ready = sem("count_ready")
        again_loaded = sem("again_loaded")
        again_stored = sem("again_stored")
        again_product = sem("again_product")
        again_preact = sem("again_preact")
        again_step = sem("again_step")
        again_placed = sem("again_placed")

        def tokens_at(g, s):
            slot = wxy[g % 3]
            if isinstance(s, int):
                return slot[:, s:s + SEG * (LANES - 1) + 1:SEG]
            return slot[:, bass.ds(s, LANES, SEG)]

        STEPS = WARM + SEG

        def states(g, s, warm):
            return (g // 2) * (STEPS + 2) + s + (1 if warm else 2)

        def in_halves(eng, step, begin=None, warmed=None, end=None):
            for g in range(GROUPS + 1):
                if g < GROUPS and begin:
                    begin(g)
                for lo, hi, warm in ((0, WARM, True), (WARM, HALF, False)):
                    with eng.Fori(0, (hi - lo) // 2) as i:
                        for odd in range(2):
                            if g < GROUPS:
                                step(g, 2 * i + (lo + odd), odd, warm)
                            if g > 0:
                                step(g - 1, 2 * i + (lo + HALF + odd), odd, False)
                    if warm and g < GROUPS and warmed:
                        warmed(g)
                if g > 0 and end:
                    end(g - 1)

        PAIRS = B // 2
        PT = 2 * IMG_TILES
        SUBS = T // P
        LOW = -3.0e38
        pooled = sb("pooled", [P, E, B])
        scope_c = ExitStack()
        gates_raw = sb("gates_raw", [E, P], scope=scope_c)
        gates_t = sb("gates_t", [P, E], scope=scope_c)
        gates_c = sb("gates_c", [P, E], scope=scope_c)
        gate_bias = sb("gate_bias", [P, 1], scope=scope_c)
        taps = sb("taps", [P, 6, 4], scope=scope_c)
        diags = sb("diags", [P, 4, IMG_W], scope=scope_c)
        diags_low = sb("diags_low", [P, 4, IMG_W], scope=scope_c)
        band = sb("band", [P, 6, IMG_W], scope=scope_c)
        x_ring = sb("x_ring", [P, PT, TOK], scope=scope_c)
        y_ring = sb("y_ring", [P, 8, TOK], scope=scope_c)
        parts_c = sb("parts_c", [P, 2, SUB, 6], scope=scope_c)
        mom_c = sb("mom_c", [P, 2, SUB, 2], scope=scope_c)
        eps_sum_c = sb("eps_sum_c", [P, 2, SUB], scope=scope_c)
        root_c = sb("root_c", [P, 2, SUB], scope=scope_c)
        shift_c = sb("shift_c", [P, 2, SUB], scope=scope_c)
        blur_in = sb("blur_in", [P, 8, TOK], scope=scope_c)
        parts_t = sb("parts_t", [P, 2, SUB, 6], scope=scope_c)
        mom_t = sb("mom_t", [P, 2, SUB, 2], scope=scope_c)
        eps_sum_t = sb("eps_sum_t", [P, 2, SUB], scope=scope_c)
        root_t = sb("root_t", [P, 2, 2, SUB], scope=scope_c)
        shift_t = sb("shift_t", [P, 2, SUB], scope=scope_c)
        tokens = sb("tokens", [P, 2, 2, SUBS, P], scope=scope_c)
        logits_tm = sb("logits_tm", [P, 4, SUB, 2, E], scope=scope_c)
        logits = sb("logits", [P, 2, T], scope=scope_c)
        prob = sb("prob", [P, T], scope=scope_c)
        part_top = sb("part_top", [P, 4, 8], scope=scope_c)
        top8 = sb("top8", [P, 8], scope=scope_c)
        minus_max = sb("minus_max", [P, 1], scope=scope_c)
        exp_sum = sb("exp_sum", [P, 1], scope=scope_c)
        exp_inv = sb("exp_inv", [P, 1], scope=scope_c)
        prob_tm = sb("prob_tm", [P, 2, SUB, 2 * E], scope=scope_c)
        scope_c.close()
        p_x2, p_x3, p_blur, p_gates, p_turned, p_pool = banks[0:2], banks[2:4], banks[4], banks[5], banks[6], banks[7]

        c_loaded = sem("c_loaded")
        c_const = sem("c_const")
        diag_step = sem("diag_step")
        c_setup = sem("c_setup")
        gates_turned = sem("gates_turned")
        gates_copied = sem("gates_copied")
        xy_loaded = [sem(f"xy_loaded{i}") for i in range(8)]
        x2_ready = sem("x2_ready")
        x2_turned = sem("x2_turned")
        parts_c_done = sem("parts_c_done")
        mom_c_ready = sem("mom_c_ready")
        eps_c_added = sem("eps_c_added")
        root_c_ready = sem("root_c_ready")
        shift_c_ready = sem("shift_c_ready")
        blur_in_ready = sem("blur_in_ready")
        blurred = sem("blurred")
        x3_ready = sem("x3_ready")
        x3_stored = [sem(f"x3_stored{i}") for i in range(4)]
        x3_turned = sem("x3_turned")
        parts_t_done = sem("parts_t_done")
        mom_t_ready = sem("mom_t_ready")
        eps_t_added = sem("eps_t_added")
        root_t_ready = sem("root_t_ready")
        shift_t_ready = sem("shift_t_ready")
        tokens_ready = sem("tokens_ready")
        gated = sem("gated")
        logits_tm_ready = sem("logits_tm_ready")
        logits_turned = sem("logits_turned")
        logits_ready = sem("logits_ready")
        part_top_ready = sem("part_top_ready")
        top_found = sem("top_found")
        minus_max_ready = sem("minus_max_ready")
        exp_ready = sem("exp_ready")
        marked = sem("marked")
        exp_inv_ready = sem("exp_inv_ready")
        masked = sem("masked")
        prob_ready = sem("prob_ready")
        prob_stored = sem("prob_stored")
        prob_turned = sem("prob_turned")
        prob_tm_ready = sem("prob_tm_ready")
        pooled_done = sem("pooled_done")
        pooled_ready = sem("pooled_ready")

        LOGITS_AT = {(2 * q + 5) % PT: q for q in range(IMG_TILES)}
        PROB_FIRST_AT = {8 + q: q for q in range(0, IMG_TILES, 2)}
        PROB_SECOND_AT = {8 + q: q + 1 for q in range(0, IMG_TILES, 2)}
        POOL_AT = {8 + q: q for q in range(IMG_TILES)}
        QUARTER = T // 4
        PART_TOP_AT = {10: 0, 14: 1, 0: 2, 3: 3}
        MASK_AT = {6: 0, 7: 1, 8: 2, 9: 3}
        SCALE_AT = {7: 0, 8: 1, 9: 2, 10: 3}
        TOP_AT, EXP_AT, MARK_AT, STORE_AT, POOLED_AT = 3, 4, 5, 11, 15

        def pipeline_c(eng, step):
            pipeline(eng, step, 2 * PT, PT, 6, PT)

        def wait_c(eng, s, r, c, **kw):
            wait(eng, s, r, c, unroll=2 * PT, **kw)

        def pair_of(r, c):
            pair = 2 * r + c // PT - 1
            return (pair if not isinstance(r, int) or 0 <= pair < PAIRS else None), c % PT

        def coming_pair(r, c):
            m = c % PT
            pair = 2 * r + c // PT - (1 if m < 4 else 0)
            return (pair if not isinstance(r, int) or 0 <= pair < PAIRS else None), m

        HK = HID // P
        UE = 8
        scope_d = ExitStack()
        w1_in = sb("w1_in", [P, UE, HID], scope=scope_d)
        w2_in = sb("w2_in", [P, UE, HK, O], scope=scope_d)
        b1_raw = sb("b1_raw", [E, HID], scope=scope_d)
        b1_t = sb("b1_t", [P, E, HK], scope=scope_d)
        hid_pre = sb("hid_pre", [P, 2, HK * B], scope=scope_d)
        hid = sb("hid", [P, 2, HK * B], scope=scope_d)
        eo = sb("eo", [B, 2, 4, O], scope=scope_d)
        scope_d.close()

        bias1_loaded = sem("bias1_loaded")
        bias1_turned = sem("bias1_turned")
        bias1_ready = sem("bias1_ready")
        w_loaded = [sem(f"w_loaded{i}") for i in range(UE)]
        hid_done = sem("hid_done")
        hid_pre_ready = sem("hid_pre_ready")
        hid_ready = sem("hid_ready")
        eo_done = sem("eo_done")
        eo_ready = sem("eo_ready")
        eo_stored = [sem(f"eo_stored{i}") for i in range(2)]

        def rounds_d(eng, body):
            with eng.Fori(0, E // UE - 1) as r:
                body(r, False)
            body(E // UE - 1, True)

        scope_e = ExitStack()
        outputs = sb("outputs", [P, PAIRS, O], scope=scope_e)
        b2_in = sb("b2_in", [P, O], scope=scope_e)
        chosen = sb("chosen", [P, 2, O], scope=scope_e)
        prob_in = sb("prob_in", [P, 2, T], scope=scope_e)
        x3_in = sb("x3_in", [P, 4, T], scope=scope_e)
        scope_e.close()

        outputs_loaded = sem("outputs_loaded")
        outputs_ready = sem("outputs_ready")
        chosen_ready = sem("chosen_ready")
        pair_loaded = [sem(f"pair_loaded{i}") for i in range(2)]
        spread = sem("spread")
        out_ready = sem("out_ready")
        out_stored = [sem(f"out_stored{i}") for i in range(2)]

        def sync_a(sp):
            for dst, src in ((herm_raw[:], herm_w.rearrange("i o d -> i (o d)")), (w_raw[:], ffn_w), (v_raw[:], ffn_v),
                             (gam[:], gamma.unsqueeze(1)), (bet[:], beta.unsqueeze(1))):
                sp.dma_start(dst, src).then_inc(weights_loaded, 16)
            for n in range(4):
                sp.dma_start(x_in[:, n, :], x_tile(0, n)).then_inc(x_loaded[n], 16)
            U = IMG_TILES

            def step(r, c, has):
                if has(-1):
                    k = (c - 1) % 4
                    wait(sp, x1_ready, r, c - 1, unroll=U)
                    sp.dma_start(tile_at(x1_dram, r, c - 1, U), x1[:, k, :]).then_inc(x1_stored[k], 16)
                if has(3) and c >= 1:
                    sp.dma_start(x_in[:, (c + 3) % 4, :], x_tile(r, c + 3)).then_inc(x_loaded[(c + 3) % 4], 16)
                if has(-2):
                    k = (c - 2) % 4
                    wait(sp, wx_ready, r, c - 2, unroll=U)
                    sp.dma_start(tile_at(wx_dram, r, c - 2, U), wx[:, k, :]).then_inc(wx_stored[k], 16)

            pipeline(sp, step, U, 8, 3, 2)
            for k in range(4):
                sp.wait_ge(x1_stored[k], 16 * (TILES // 4))
                sp.wait_ge(wx_stored[k], 16 * (TILES // 4))

        def tensor_a(pe):
            pe.wait_ge(weights_loaded, 80)
            pe.wait_ge(ident_set, 2)
            pe.transpose(banks[7][:, 0:P], v_raw[:], ident[:]).then_inc(turned, 1)
            pe.transpose(banks[7][:, P:2 * P], w_raw[:], ident[:]).then_inc(turned, 1)
            pe.wait_ge(herm_ready, 1)
            pe.wait_ge(turned_used, 2)

            def turn(bank, src, done):
                for j in range(SUB):
                    mm = pe.transpose(bank[:, j * P:(j + 1) * P], src[:, j * P:(j + 1) * P], ident[:])
                mm.then_inc(done, 1)

            def step(r, c, has):
                def mix(k0, k1):
                    if not has(0):
                        return
                    for k in range(k0, k1):
                        if k == 0:
                            wait(pe, x1_ready, r, c - 2)
                            wait(pe, gauss_ready, r, c)
                        else:
                            wait(pe, basis_ready, r, c, per=DEG, sub=k)
                        mm = pe.matmul(p_conv[c % 2][:], herm[:, k, :], basis[:, c % 2, k, :],
                                       start=(k == 0), stop=(k == DEG))
                    if k1 == DEG + 1:
                        mm.then_inc(conv_done, 1)

                if has(1):
                    wait(pe, z_ready, r, c + 1)
                    wait(pe, basis_ready, r, c, per=DEG, sub=1)
                    turn(p_z, z_tm[:, (c + 1) % 2, :], z_turned)
                if has(-2):
                    wait(pe, t_tm_ready, r, c - 2)
                    wait(pe, t_ready, r, c - 3)
                    turn(p_t, t_tm[:, c % 2, :], t_turned)
                mix(0, 1)
                if has(-1):
                    wait(pe, x1_ready, r, c - 1)
                    wait(pe, t_tm_ready, r, c - 2)
                    turn(p_x1, x1[:, (c - 1) % 4, :], x1_turned)
                mix(1, 3)
                if has(2):
                    wait_slot(pe, x_loaded, r, c + 2)
                    wait(pe, z_ready, r, c)
                    turn(p_x[c % 2], x_in[:, (c + 2) % 4, :], x_turned)
                mix(3, 5)
                if has(-2):
                    wait(pe, t_ready, r, c - 2)
                    wait(pe, wx_ready, r, c - 3)
                    pe.matmul(p_wx[:], w_t[:], t_cm[:, c % 2, :], start=True, stop=True).then_inc(wx_done, 1)
                mix(5, DEG + 1)

            pipeline(pe, step, 4, 8, 2, 2)

        def scalar_a(act):
            act.wait_ge(turned, 2)
            act.activation(v_t[:], banks[7][:, 0:P], ACT.Copy).then_inc(turned_used, 1)

            def normalise(dst, func, src, scale, bias, done):
                for j in range(SUB):
                    at = slice(j * P, (j + 1) * P)
                    ins = act.activation(dst[:, at], src[:, at], func, bias=bias[:, j:j + 1], scale=scale[:, j:j + 1])
                ins.then_inc(done, 1)

            def step(r, c, has):
                if has(1):
                    k = (c + 1) % 2
                    wait(act, z_turned, r, c + 1)
                    wait(act, conv_done, r, c - 1)
                    act.activation(z2[:, k, :], p_z[:], ACT.Square).then_inc(z2_ready, 1)
                    wait(act, z2_ready, r, c + 1)
                    act.activation(basis[:, k, 0, :], z2[:, k, :], ACT.Exp, scale=-0.5 * Z_SCALE ** 2)\
                       .then_inc(gauss_ready, 1)
                if has(-2):
                    k = c % 2
                    wait(act, t_turned, r, c - 2)
                    wait(act, wx_done, r, c - 4)
                    act.activation(t_cm[:, k, :], p_t[:], ACT.Copy).then_inc(t_ready, 1)
                if has(-1):
                    k = (c - 1) % 2
                    wait(act, shift2_ready, r, c - 1)
                    wait(act, t_turned, r, c - 3)
                    normalise(t_tm[:, k, :], ACT.Identity, p_x1, rstd2[:, k, :], shift2[:, k, :], t_tm_ready)
                if has(2):
                    k = c % 2
                    wait(act, shift_ready, r, c + 2)
                    wait(act, z_turned, r, c)
                    normalise(z_tm[:, k, :], ACT.Tanh, p_x[k], rstd[:, k, :], shift[:, k, :], z_ready)
                if has(-2):
                    wait(act, wx_done, r, c - 2)
                    wait_slot(act, wx_stored, r, c - 6)
                    wait(act, stats_ready, r, c - 6)
                    act.activation(wx[:, (c - 2) % 4, :], p_wx[:], ACT.Copy).then_inc(wx_ready, 1)

            pipeline(act, step, 4, 8, 2, 2)

        def gpsimd_a(pool):
            pool.memset(ident[:], 0.0).then_inc(ones_set, 1)
            pool.memset(centre[:], -1.0 / C).then_inc(ones_set, 1)
            for tile, value in ((minus_half, -0.5), (eps_c, 1e-6), (eps_t, 1e-5)):
                pool.memset(tile[:], value).then_inc(ones_set, 1)
            pool.wait_ge(ones_set, 5)
            for m, diagonal in ((ident, 1.0), (centre, 1.0 - 1.0 / C)):
                pool.affine_select(out=m[:], in_=m[:], compare_op=ALU.not_equal, fill=diagonal, base=0,
                                   pattern=[[-1, P]], channel_multiplier=1).then_inc(ident_set, 1)

            def inverse_root(r, c, given, eps, values, added_eps, added, result, ready, free):
                k = c % 2
                wait(pool, given, r, c)
                pool.tensor_tensor(added_eps[:, k, :], values[:, k, :, 1], eps[:], ALU.add).then_inc(added, 1)
                wait(pool, added, r, c)
                wait(pool, free, r, c - 2)
                pool.tensor_tensor(result[:, k, :], added_eps[:, k, :], minus_half[:], ALU.pow).then_inc(ready, 1)

            def step(r, c, has):
                if has(-1):
                    inverse_root(r, c - 1, moments2_ready, eps_t, moments2, var2_eps, eps2_added, rstd2, rstd2_ready,
                                 t_tm_ready)
                if has(2):
                    inverse_root(r, c + 2, moments_ready, eps_c, moments, var_eps, eps_added, rstd, rstd_ready, z_ready)

            pipeline(pool, step, 4, 8, 2, 2)
            pool.wait_ge(bn_step, 2)
            pool.tensor_tensor(bn_tmp[:, 1:2], bn_tmp[:, 0:1], minus_half[:, 0:1], ALU.pow).then_inc(bn_root, 1)

        def vector_a(dve):
            raw = herm_raw[:].rearrange("i (o d) -> i d o", d=DEG + 1)
            dve.wait_ge(weights_loaded, 80)
            done = 0
            for n, d in enumerate(range(DEG, -1, -1)):
                for k in range(d, -1, -2):
                    first = d >= DEG - 1
                    if first:
                        ins = dve.tensor_scalar(herm[:, k, :], raw[:, d, :], float(CHANGE[d, k]), None, ALU.mult)
                    else:
                        ins = dve.scalar_tensor_tensor(herm[:, k, :], raw[:, d, :], float(CHANGE[d, k]),
                                                       herm[:, k, :], ALU.mult, ALU.add)
                    ins.then_inc(herm_step, 1)
                    done += 1
                dve.wait_ge(herm_step, done)
            dve.wait_ge(turned, 2)
            dve.wait_ge(turned_used, 1)
            dve.tensor_copy(w_t[:], banks[7][:, P:2 * P]).then_inc(turned_used, 1)
            dve.memset(bn_tmp[:], 1e-5).then_inc(herm_ready, 1)

            def token_moments(r, c, given, src, parts, parts_done, values, ready):
                k = c % 2
                wait(dve, given, r, c)
                for j in range(SUB):
                    ins = dve.bn_stats(parts[:, k, j, :], src[:, j * P:(j + 1) * P])
                ins.then_inc(parts_done, 1)
                wait(dve, parts_done, r, c)
                dve.sem_inc(passed, 1)
                for j in range(SUB):
                    ins = dve.bn_aggr(values[:, k, j, :], parts[:, k, j, :])
                ins.then_inc(ready, 1)

            def shifts(r, c, root_ready, values, root, result, free, ready):
                k = c % 2
                wait(dve, root_ready, r, c)
                wait(dve, free, r, c - 2)
                dve.scalar_tensor_tensor(result[:, k, :], values[:, k, :, 0], -1.0, root[:, k, :], ALU.mult, ALU.mult)\
                   .then_inc(ready, 1)

            def basis_functions(r, c, lo, hi):
                k = c % 2
                for d in range(lo, hi):
                    if d == 1:
                        wait(dve, gauss_ready, r, c)
                        wait(dve, conv_done, r, c - 2)
                        dve.tensor_tensor(basis[:, k, 1, :], p_z[:], basis[:, k, 0, :], ALU.mult).then_inc(basis_ready, 1)
                        continue
                    if d > 2:
                        wait(dve, basis_ready, r, c, per=DEG, sub=d - 2)
                    dve.scalar_tensor_tensor(basis[:, k, d, :], z2[:, k, :], float(CENTRE[d]), basis[:, k, d - 2, :],
                                             ALU.subtract, ALU.mult).then_inc(basis_ready, 1)

            def step(r, c, has):
                if has(-1):
                    wait(dve, conv_done, r, c - 1)
                    wait_slot(dve, x1_stored, r, c - 5)
                    dve.tensor_tensor(x1[:, (c - 1) % 4, :], p_conv[(c - 1) % 2][:], x_in[:, (c - 1) % 4, :], ALU.add)\
                       .then_inc(x1_ready, 1)
                if has(-1):
                    token_moments(r, c - 1, x1_turned, p_x1, sub_stats2, sub2_done, moments2, moments2_ready)
                if has(1):
                    basis_functions(r, c + 1, 1, 4)
                if has(2):
                    token_moments(r, c + 2, x_turned, p_x[c % 2], sub_stats, sub_done, moments, moments_ready)
                if has(-1):
                    shifts(r, c - 1, rstd2_ready, moments2, rstd2, shift2, t_tm_ready, shift2_ready)
                if has(1):
                    basis_functions(r, c + 1, 4, 7)
                if has(2):
                    shifts(r, c + 2, rstd_ready, moments, rstd, shift, z_ready, shift_ready)
                if has(1):
                    basis_functions(r, c + 1, 7, DEG + 1)
                if has(-3):
                    n = c - 3
                    wait(dve, wx_ready, r, n)
                    dve.sem_inc(passed, 1)
                    dst = stats[:, n, :] if isinstance(r, int) else stats[:, bass.ds(4 * r + n, 1), :].rearrange("p a s -> p (a s)")
                    dve.bn_stats(dst, wx[:, n % 4, :]).then_inc(stats_ready, 1)

            pipeline(dve, step, 4, 8, 2, 3)
            dve.wait_ge(stats_ready, TILES)
            dve.bn_aggr(mean_var[:], stats[:].rearrange("p n s -> p (n s)")).then_inc(bn_step, 1)
            dve.wait_ge(bn_step, 1)
            dve.tensor_scalar(bn_tmp[:, 0:1], mean_var[:, 1:2], 1e-5, None, ALU.add).then_inc(bn_step, 1)
            dve.wait_ge(bn_root, 1)
            dve.tensor_tensor(norm_a[:], gam[:], bn_tmp[:, 1:2], ALU.mult).then_inc(bn_step, 1)
            dve.wait_ge(bn_step, 3)
            dve.tensor_tensor(bn_tmp[:, 2:3], mean_var[:, 0:1], norm_a[:], ALU.mult).then_inc(bn_step, 1)
            dve.wait_ge(bn_step, 4)
            dve.tensor_tensor(norm_b[:], bet[:], bn_tmp[:, 2:3], ALU.subtract).then_inc(bn_step, 1)

        def group_tiles(tiles, g, img):
            n = (g * GROUP + img) * IMG_TILES
            return tiles[n:n + IMG_TILES, :, :].rearrange("t p n -> p t n")

        def group_slot(g, img):
            lo = WARM + img * T
            return wxy[g % 3][:, lo:lo + T].rearrange("p (t n) -> p t n", n=TOK)

        def if_again(eng):
            eng.wait_ge(count_ready, 1)
            return eng.If(eng.value_load(close_count[0:1, 0:1], min_val=0, max_val=P) < P)

        def sync_b(sp):
            def load(g):
                for img in range(GROUP):
                    sp.dma_start(group_slot(g, img), group_tiles(wx_dram, g, img)).then_inc(group_loaded[g % 3], 16)

            for g in range(2):
                load(g)
            for g in range(2, GROUPS + 2):
                done = g - 2
                if g < GROUPS and g < 3:
                    load(g)
                sp.wait_ge(placed[done % 2], SEG * (done // 2 + 1) + 2)
                for img in range(GROUP):
                    sp.dma_start(group_tiles(y_dram, done, img), group_slot(done, img)).then_inc(group_stored[done % 3], 16)
                if g + 1 < GROUPS:
                    sp.wait_ge(group_stored[done % 3], 16 * GROUP * (done // 3 + 1))
                    load(g + 1)
            for k in range(3):
                sp.wait_ge(group_stored[k], 16 * GROUP * len(range(k, GROUPS, 3)))
            with if_again(sp):
                wx_at = wx_dram.rearrange("(b t) p n -> t p b n", t=IMG_TILES)
                y_at = y_dram.rearrange("(b t) p n -> t p b n", t=IMG_TILES)
                with sp.Fori(0, IMG_TILES) as t:
                    for part in range(TOK // AGAIN):
                        cols = slice(part * AGAIN, (part + 1) * AGAIN)
                        n = t * (TOK // AGAIN) + part
                        sp.dma_start(again_wx[:], wx_at[bass.ds(t, 1), :, :, cols].rearrange("t p b n -> p (t b) n"))\
                          .then_inc(again_loaded, 16)
                        sp.wait_ge(again_placed, n * AGAIN + AGAIN + 1)
                        sp.sem_inc(passed, 1)
                        sp.dma_start(y_at[bass.ds(t, 1), :, :, cols].rearrange("t p b n -> p (t b) n"), again_y[:])\
                          .then_inc(again_stored, 16)
                        sp.wait_ge(again_stored, n * 16 + 16)
                        sp.sem_inc(passed, 1)

        def tensor_b(pe):
            def step(g, s, odd, warm):
                k = g % 2
                pe.wait_ge(state_ready[k], states(g, s, warm))
                pe.matmul(banks[k][:, 0:LANES], v_t[:], state[k][:, 1 - odd, :], start=True, stop=True)\
                  .then_inc(product_done[k], 1)

            in_halves(pe, step)
            pe.wait_ge(gap_step, 2 * GROUPS + 3)
            pe.matmul(banks[2][0:1, 0:1], close[:, 0:1], close[:, 1:2], start=True, stop=True).then_inc(count_done, 1)
            with if_again(pe):
                with pe.Fori(0, T) as t:
                    pe.wait_ge(again_step, t + 1)
                    pe.matmul(banks[3][:, 0:B], v_t[:], again_state[:], start=True, stop=True).then_inc(again_product, 1)

        def vector_b(dve):
            for slot in wxy:
                dve.memset(slot[:, 0:WARM], 0.0).then_inc(pads_set, 1)
            dve.wait_ge(pads_set, 3)

            def begin(g):
                k = g % 2
                dve.wait_ge(group_loaded[g % 3], 16 * GROUP * (g // 3 + 1))
                if g >= 2:
                    dve.wait_ge(placed[k], SEG * (g // 2) + 2)
                    dve.wait_ge(gap_step, 2 * (g - 1))
                dve.memset(state[k][:, 1, :], 0.0).then_inc(state_ready[k], 1)

            def step(g, s, odd, warm):
                k = g % 2
                dve.wait_ge(product_done[k], (g // 2) * STEPS + s + 1)
                dve.scalar_tensor_tensor(preact[k][:], tokens_at(g, s), norm_a[:], banks[k][:, 0:LANES],
                                         ALU.mult, ALU.add).then_inc(preact_ready[k], 1)

            def warmed(g):
                k = g % 2
                dve.wait_ge(state_ready[k], states(g, WARM, True))
                dve.memset(state[k][:, 1, 0:SEGS * (GROUP - 1) + 1:SEGS], 0.0).then_inc(state_ready[k], 1)
                dve.wait_ge(state_ready[k], states(g, WARM, False))
                dve.tensor_copy(first_state[k][:], state[k][:, 1, :]).then_inc(first_kept, 1)

            def end(g):
                k = g % 2
                dve.wait_ge(state_ready[k], states(g, STEPS, False))
                dve.wait_ge(first_kept, g + 1)
                last = state[k][:, 1, :].rearrange("p (b k) -> p b k", b=GROUP)
                first = first_state[k][:].rearrange("p (b k) -> p b k", b=GROUP)
                dve.tensor_tensor(gap[:], last[:, :, 0:SEGS - 1], first[:, :, 1:SEGS], ALU.subtract).then_inc(gap_step, 1)
                dve.wait_ge(gap_step, 2 * g + 1)
                dve.tensor_reduce(gap_max[:, g:g + 1], gap[:].rearrange("p b k -> p (b k)"), AX.X, ALU.max,
                                  apply_absolute_value=True).then_inc(gap_step, 1)

            in_halves(dve, step, begin, warmed, end)
            dve.memset(close[:, 1:2], 1.0).then_inc(gap_step, 1)
            dve.wait_ge(gap_step, 2 * GROUPS + 1)
            dve.tensor_reduce(gap_max[:, GROUPS:GROUPS + 1], gap_max[:, 0:GROUPS], AX.X, ALU.max).then_inc(gap_step, 1)
            dve.wait_ge(gap_step, 2 * GROUPS + 2)
            dve.tensor_scalar(close[:, 0:1], gap_max[:, GROUPS:GROUPS + 1], TOLERANCE, None, ALU.is_le)\
               .then_inc(gap_step, 1)
            dve.wait_ge(count_done, 1)
            dve.tensor_copy(close_count[:], banks[2][0:1, 0:1]).then_inc(count_ready, 1)
            with if_again(dve):
                dve.wait_ge(again_loaded, 16)
                dve.memset(again_state[:], 0.0).then_inc(again_step, 1)
                with dve.Fori(0, T // AGAIN) as n:
                    dve.wait_ge(again_loaded, n * 16 + 16)
                    dve.sem_inc(passed, 1)
                    with dve.Fori(0, AGAIN) as t:
                        dve.wait_ge(again_product, n * AGAIN + t + 1)
                        dve.scalar_tensor_tensor(again_pre[:], again_wx[:, :, bass.ds(t, 1)].rearrange("p b n -> p (b n)"),
                                                 norm_a[:], banks[3][:, 0:B], ALU.mult, ALU.add).then_inc(again_preact, 1)

        def scalar_b(act):
            def step(g, s, odd, warm):
                k = g % 2
                act.wait_ge(preact_ready[k], (g // 2) * STEPS + s + 1)
                if not warm:
                    act.wait_ge(placed[k], (g // 2) * SEG + s - WARM + 1)
                act.activation(state[k][:, odd, :], preact[k][:], ACT.Sigmoid, bias=norm_b[:])\
                   .then_inc(state_ready[k], 1)

            in_halves(act, step)
            with if_again(act):
                with act.Fori(0, T) as t:
                    act.wait_ge(again_preact, t + 1)
                    act.wait_ge(again_placed, t + 1)
                    act.activation(again_state[:], again_pre[:], ACT.Sigmoid, bias=norm_b[:]).then_inc(again_step, 1)

        def gpsimd_b(pool):
            for k in range(2):
                pool.sem_inc(placed[k], 2)

            def step(g, s, odd, warm):
                if warm:
                    return
                k = g % 2
                pool.wait_ge(state_ready[k], states(g, s + 1, False))
                pool.sem_inc(passed, 1)
                pool.tensor_copy(tokens_at(g, s), state[k][:, odd, :]).then_inc(placed[k], 1)

            in_halves(pool, step)
            with if_again(pool):
                pool.sem_inc(again_placed, 1)
                with pool.Fori(0, T // AGAIN) as n:
                    with pool.Fori(0, AGAIN) as t:
                        pool.wait_ge(again_step, n * AGAIN + t + 2)
                        pool.sem_inc(passed, 1)
                        pool.tensor_copy(again_y[:, :, bass.ds(t, 1)].rearrange("p b n -> p (b n)"), again_state[:])\
                            .then_inc(again_placed, 1)

        band_cols = band[:].rearrange("p w j -> p (w j)")

        def sync_c(sp):
            sp.dma_start(gates_raw[:], gate_w).then_inc(c_loaded, 16)
            for half in range(2):
                sp.dma_start(gate_bias[half * E:(half + 1) * E, :], gate_b.unsqueeze(1)).then_inc(c_loaded, 16)
            sp.wait_ge(c_const, 1)
            for half in range(2):
                sp.dma_start(taps[half * IMG_W:(half + 1) * IMG_W, 1 + half:5 + half, :],
                             blur.rearrange("u v -> (u v)").partition_broadcast(IMG_W)
                             .rearrange("p (u v) -> p u v", v=4)).then_inc(c_loaded, 16)

            def at(tiles, r, c):
                n = c // PT * PT + c % 2 * IMG_TILES + c % PT // 2
                return tile_at(tiles, r, n, 2 * PT)

            def load(r, c):
                sp.dma_start(x_ring[:, c % PT, :], at(x1_dram, r, c)).then_inc(xy_loaded[c % 8], 16)
                sp.dma_start(y_ring[:, c % 8, :], at(y_dram, r, c)).then_inc(xy_loaded[c % 8], 16)

            for k in range(8):
                load(0, k)
            sp.sem_inc(prob_stored, 16)

            def step(r, c, has):
                if has(0):
                    if not isinstance(r, int) or c >= 4:
                        alone(sp, x3_stored[c % 4], 16 * (8 * r + (c - 4) // 4 + 1))
                    wait_c(sp, x3_ready, r, c)
                    sp.sem_inc(passed, 1)
                    sp.dma_start(at(x3_dram, r, c), x_ring[:, c % PT, :]).then_inc(x3_stored[c % 4], 16)
                if has(8) and c >= 0:
                    if not isinstance(r, int) or c >= 8:
                        wait_c(sp, gated, r, c - 8)
                        sp.sem_inc(passed, 1)
                    load(r, c + 8)
                pair, m = pair_of(r, c)
                if pair is not None and m == STORE_AT:
                    sp.wait_ge(prob_ready, 4 * pair + 4)
                    sp.sem_inc(passed, 1)
                    dst = (prob_dram[pair, :, :] if isinstance(r, int)
                           else prob_dram[bass.ds(pair, 1), :, :].rearrange("a p n -> p (a n)"))
                    sp.dma_start(dst, prob[:]).then_inc(prob_stored, 16)

            pipeline(sp, step, 2 * PT, PT, 8, PT)
            for k in range(4):
                sp.wait_ge(x3_stored[k], 16 * (TILES // 4))
            sp.wait_ge(prob_stored, 16 * PAIRS + 16)

        def tensor_c(pe):
            pe.wait_ge(c_loaded, 80)
            pe.transpose(banks[0][:, 0:E], gates_raw[:], ident[0:E, 0:E]).then_inc(gates_turned, 1)
            pe.wait_ge(gates_copied, 1)
            pe.matmul(banks[1][:, 0:E], centre[:], gates_t[:], start=True, stop=True).then_inc(gates_turned, 1)
            pe.wait_ge(c_setup, 1)
            pe.sem_inc(pooled_done, 1)

            def turn(bank, src, done):
                for j in range(SUB):
                    mm = pe.transpose(bank[:, j * P:(j + 1) * P], src[:, j * P:(j + 1) * P], ident[:])
                mm.then_inc(done, 1)

            def step(r, c, has):
                coming, m = coming_pair(r, c)
                pair, _ = pair_of(r, c)

                def turn_logits(q):
                    pe.wait_ge(logits_tm_ready, 8 * coming + q + 1)
                    if 2 <= q < 6 and pair is not None:
                        pe.wait_ge(prob_tm_ready, 8 * pair + 2 * (q - 1))
                    elif not isinstance(coming, int) or 8 * coming + q:
                        pe.wait_ge(logits_ready, 8 * coming + q)
                    turn(p_turned, logits_tm[:, q % 4, :, :, :].rearrange("p s i e -> p (s i e)"), logits_turned)

                def turn_prob(q):
                    pe.wait_ge(prob_ready, 4 * pair + q // 2 + 1)
                    if q % 2:
                        pe.wait_ge(prob_tm_ready, 8 * pair + q)
                    elif coming is not None:
                        pe.wait_ge(logits_ready, 8 * coming + 2 + q // 2)
                    elif q:
                        pe.wait_ge(prob_tm_ready, 8 * pair + q)
                    turn(p_turned, prob[:, q * TOK:(q + 1) * TOK], prob_turned)

                if coming is not None and m in LOGITS_AT:
                    turn_logits(LOGITS_AT[m])
                if pair is not None and m in PROB_FIRST_AT:
                    turn_prob(PROB_FIRST_AT[m])
                if has(-2):
                    n = c - 2
                    wait_c(pe, x3_ready, r, n)
                    wait_c(pe, tokens_ready, r, n - 2)
                    turn(p_x3[n % 2], x_ring[:, n % PT, :], x3_turned)
                if has(4):
                    n = c + 4
                    wait_c(pe, x2_ready, r, n)
                    wait_c(pe, blur_in_ready, r, n - 2)
                    turn(p_x2[n % 2], x_ring[:, n % PT, :], x2_turned)
                if has(0):
                    wait_c(pe, blur_in_ready, r, c + 2 if c % PT < PT - 2 else c)
                    wait_c(pe, x3_ready, r, c - 1)
                    part = c % PT // 2
                    first, end = part * TOK, (part + 1) * TOK
                    reach = [s for s in range(part * SUB - 1, part * SUB + SUB + 1) if 0 <= s < SUBS]
                    for s in reach:
                        lo, hi = max(s * P - IMG_W, first), min((s + 2) * P, end)
                        if lo >= hi:
                            continue
                        n = c + 2 * (s // SUB - part)
                        mm = pe.matmul(p_blur[:, lo - first:hi - first],
                                       blur_in[:, n % 8, s % SUB * P:(s % SUB + 1) * P],
                                       band_cols[:, lo - s * P + P:hi - s * P + P],
                                       start=(s == reach[0]), stop=(s == reach[-1]), skip_group_check=True)
                    mm.then_inc(blurred, 1)
                if pair is not None and m in PROB_SECOND_AT:
                    turn_prob(PROB_SECOND_AT[m])
                if has(-2):
                    n = c - 2
                    if n % 2 == 0:
                        wait(pe, logits_tm_ready, r, n // 2 - 1, unroll=PT)
                    out = p_gates.rearrange("p (s i e) -> p s i e", s=SUB, i=2)
                    for s in range(SUB):
                        mm = pe.matmul(out[:, s, n % 2, :], x_ring[:, n % PT, s * P:(s + 1) * P], gates_c[:],
                                       start=True, stop=True)
                    mm.then_inc(gated, 1)
                if pair is not None and m in POOL_AT:
                    q = POOL_AT[m]
                    pe.wait_ge(prob_tm_ready, 8 * pair + q + 1)
                    for s in range(SUB):
                        for img in range(2):
                            mm = pe.matmul(p_pool[:, img * E:(img + 1) * E],
                                           tokens[:, (c // PT - 1) % 2, img, q * SUB + s, :],
                                           prob_tm[:, q % 2, s, img * E:(img + 1) * E],
                                           start=(q == 0 and s == 0 and img == 0),
                                           stop=(q == IMG_TILES - 1 and s == SUB - 1), skip_group_check=True)
                    if q == IMG_TILES - 1:
                        mm.then_inc(pooled_done, 1)

            pipeline_c(pe, step)

        def scalar_c(act):
            def normalise(dst, src, scale, bias, done):
                for j in range(SUB):
                    at = slice(j * P, (j + 1) * P)
                    ins = act.activation(dst[:, at], src[:, at], ACT.Identity, bias=bias[:, j:j + 1],
                                         scale=scale[:, j:j + 1])
                ins.then_inc(done, 1)

            def step(r, c, has):
                coming, m = coming_pair(r, c)
                pair, _ = pair_of(r, c)

                def copy_prob(q):
                    act.wait_ge(prob_turned, 8 * pair + q + 1)
                    act.activation(prob_tm[:, q % 2, :, :].rearrange("p s e -> p (s e)"), p_turned, ACT.Copy)\
                       .then_inc(prob_tm_ready, 1)

                if coming is not None and m in LOGITS_AT:
                    q = LOGITS_AT[m]
                    act.wait_ge(logits_turned, 8 * coming + q + 1)
                    if q == 0:
                        act.wait_ge(masked, 4 * coming) if not isinstance(coming, int) or coming else None
                    act.activation(logits[:, (c - 4) // PT % 2, q * TOK:(q + 1) * TOK], p_turned, ACT.Identity,
                                   bias=gate_bias[:]).then_inc(logits_ready, 1)
                if pair is not None and m in PROB_FIRST_AT:
                    copy_prob(PROB_FIRST_AT[m])
                if has(-2):
                    n = c - 2
                    k = n % 2
                    if n % PT == 0:
                        act.wait_ge(pooled_done, 2 * r + n // PT) if not isinstance(r, int) or n // PT else None
                    wait_c(act, shift_t_ready, r, n)
                    lo = n % PT // 2 * SUB
                    normalise(tokens[:, n // PT % 2, n % 2, lo:lo + SUB, :].rearrange("p s d -> p (s d)"), p_x3[n % 2],
                              root_t[:, n // 2 % 2, n % 2, :], shift_t[:, k, :], tokens_ready)
                if pair is not None and m in PROB_SECOND_AT:
                    copy_prob(PROB_SECOND_AT[m])
                if has(4):
                    n = c + 4
                    wait_c(act, shift_c_ready, r, n)
                    wait_c(act, blurred, r, n - 5)
                    normalise(blur_in[:, n % 8, :], p_x2[n % 2], root_c[:, n % 2, :], shift_c[:, n % 2, :], blur_in_ready)
                if pair is not None and m == EXP_AT:
                    act.wait_ge(minus_max_ready, pair + 1)
                    act.wait_ge(prob_stored, 16 * pair + 16)
                    act.activation(prob[:], logits[:, (c // PT - 1) % 2, :], ACT.Exp, bias=minus_max[:],
                                   accum_out=exp_sum[:]).then_inc(exp_ready, 1)

            pipeline_c(act, step)

        def gpsimd_c(pool):
            pool.memset(taps[:], 0.0).then_inc(c_const, 1)
            for k, (m, shift) in enumerate(((diags, 0), (diags_low, IMG_W))):
                pool.memset(m[:], 0.0).then_inc(diag_step, 1)
                pool.wait_ge(diag_step, 2 * k + 1)
                pool.affine_select(out=m[:], in_=m[:], compare_op=ALU.not_equal, fill=1.0, base=shift + 1,
                                   pattern=[[-1, 4], [1, IMG_W]], channel_multiplier=-1).then_inc(diag_step, 1)

            def inverse_root(r, n, given, eps, values, added_eps, added, result, ready, free):
                wait_c(pool, given, r, n)
                pool.tensor_tensor(added_eps[:, n % 2, :], values[:, n % 2, :, 1], eps[:], ALU.add).then_inc(added, 1)
                wait_c(pool, added, r, n)
                wait_c(pool, free, r, n - 2)
                pool.tensor_tensor(result, added_eps[:, n % 2, :], minus_half[:], ALU.pow).then_inc(ready, 1)

            def step(r, c, has):
                if has(-2):
                    n = c - 2
                    if n % 2 == 0:
                        wait(pool, logits_tm_ready, r, n // 2 - 2, unroll=PT)
                    inverse_root(r, n, mom_t_ready, eps_t, mom_t, eps_sum_t, eps_t_added, root_t[:, n // 2 % 2, n % 2, :],
                                 root_t_ready, tokens_ready)
                if has(4):
                    n = c + 4
                    inverse_root(r, n, mom_c_ready, eps_c, mom_c, eps_sum_c, eps_c_added, root_c[:, n % 2, :],
                                 root_c_ready, blur_in_ready)
                if has(6):
                    n = c + 6
                    pool.wait_ge(xy_loaded[n % 8], 32 * (4 * r + n // 8 + 1))
                    pool.tensor_tensor(x_ring[:, n % PT, :], x_ring[:, n % PT, :], y_ring[:, n % 8, :], ALU.add)\
                        .then_inc(x2_ready, 1)

            pipeline_c(pool, step)

        def vector_c(dve):
            dve.wait_ge(gates_turned, 1)
            dve.tensor_copy(gates_t[:], banks[0][:, 0:E]).then_inc(gates_copied, 1)
            dve.wait_ge(gates_turned, 2)
            dve.tensor_copy(gates_c[:], banks[1][:, 0:E]).then_inc(gates_copied, 1)
            dve.wait_ge(diag_step, 4)
            dve.tensor_copy(diags[IMG_W:P, :, :], diags_low[IMG_W:P, :, :]).then_inc(gates_copied, 1)
            dve.wait_ge(c_loaded, 80)
            dve.wait_ge(gates_copied, 3)
            for v in range(4):
                for w in range(6):
                    if v == 0:
                        ins = dve.tensor_scalar(band[:, w, :], diags[:, v, :], taps[:, w, v:v + 1], None, ALU.mult)
                    else:
                        ins = dve.scalar_tensor_tensor(band[:, w, :], diags[:, v, :], taps[:, w, v:v + 1], band[:, w, :],
                                                       ALU.mult, ALU.add)
                    ins.then_inc(gates_copied, 1)
                dve.wait_ge(gates_copied, 3 + 6 * (v + 1))
            dve.memset(exp_inv[:], 0.0).then_inc(c_setup, 1)

            dve.sem_inc(masked, 4)

            def token_moments(r, n, given, src, parts, parts_done, values, ready):
                wait_c(dve, given, r, n)
                for j in range(SUB):
                    ins = dve.bn_stats(parts[:, n % 2, j, :], src[:, j * P:(j + 1) * P])
                ins.then_inc(parts_done, 1)
                wait_c(dve, parts_done, r, n)
                dve.sem_inc(passed, 1)
                for j in range(SUB):
                    ins = dve.bn_aggr(values[:, n % 2, j, :], parts[:, n % 2, j, :])
                ins.then_inc(ready, 1)

            def shifts(r, n, root_ready, values, root, result, ready):
                wait_c(dve, root_ready, r, n)
                dve.scalar_tensor_tensor(result[:, n % 2, :], values[:, n % 2, :, 0], -1.0, root, ALU.mult, ALU.mult)\
                   .then_inc(ready, 1)

            def select(pair, m, slot):
                if m == TOP_AT:
                    alone(dve, part_top_ready, 4 * pair + 4)
                    dve.max(top8[:], part_top[:].rearrange("p k n -> p (k n)")).then_inc(top_found, 1)
                    dve.wait_ge(top_found, pair + 1)
                    dve.tensor_scalar(minus_max[:], top8[:, 0:1], -1.0, None, ALU.mult).then_inc(minus_max_ready, 1)
                if m == MARK_AT:
                    alone(dve, exp_ready, pair + 1)
                    dve.match_replace(logits[:, slot, :], top8[:], logits[:, slot, :], LOW).then_inc(marked, 1)
                    dve.reciprocal(exp_inv[:], exp_sum[:]).then_inc(exp_inv_ready, 1)
                if m in MASK_AT:
                    at = slice(MASK_AT[m] * QUARTER, (MASK_AT[m] + 1) * QUARTER)
                    if MASK_AT[m] == 0:
                        dve.wait_ge(marked, pair + 1)
                    dve.scalar_tensor_tensor(prob[:, at], logits[:, slot, at], LOW, prob[:, at], ALU.is_equal, ALU.mult)\
                       .then_inc(masked, 1)
                if m in SCALE_AT:
                    k = SCALE_AT[m]
                    at = slice(k * QUARTER, (k + 1) * QUARTER)
                    dve.wait_ge(masked, 4 * pair + k + 5)
                    if k == 0:
                        dve.wait_ge(exp_inv_ready, pair + 1)
                    dve.tensor_scalar(prob[:, at], prob[:, at], exp_inv[:], None, ALU.mult).then_inc(prob_ready, 1)

            def step(r, c, has):
                if has(-2):
                    token_moments(r, c - 2, x3_turned, p_x3[c % 2], parts_t, parts_t_done, mom_t, mom_t_ready)
                if has(4):
                    token_moments(r, c + 4, x2_turned, p_x2[c % 2], parts_c, parts_c_done, mom_c, mom_c_ready)
                coming, m = coming_pair(r, c)
                if coming is not None and m in PART_TOP_AT:
                    k = PART_TOP_AT[m]
                    alone(dve, logits_ready, 8 * coming + 2 * k + 2)
                    dve.max(part_top[:, k, :], logits[:, (c - 4) // PT % 2, k * QUARTER:(k + 1) * QUARTER])\
                       .then_inc(part_top_ready, 1)
                if has(-2):
                    n = c - 2
                    wait_c(dve, tokens_ready, r, n - 2)
                    shifts(r, n, root_t_ready, mom_t, root_t[:, n // 2 % 2, n % 2, :], shift_t, shift_t_ready)
                if has(0):
                    wait_c(dve, blurred, r, c)
                    dve.tensor_tensor(x_ring[:, c % PT, :], p_blur, x_ring[:, c % PT, :], ALU.add).then_inc(x3_ready, 1)
                if has(4):
                    wait_c(dve, blur_in_ready, r, c + 2)
                    shifts(r, c + 4, root_c_ready, mom_c, root_c[:, c % 2, :], shift_c, shift_c_ready)
                if has(-2) and c % 2 == 1:
                    n = c - 2
                    wait_c(dve, gated, r, n)
                    wait_c(dve, root_t_ready, r, n)
                    scale = root_t[:, n // 2 % 2, :, :].rearrange("p i s -> p s i").unsqueeze(3).to_broadcast([P, SUB, 2, E])
                    dve.tensor_tensor(logits_tm[:, n // 2 % 4, :, :, :], p_gates.rearrange("p (s i e) -> p s i e", s=SUB, i=2),
                                      scale, ALU.mult).then_inc(logits_tm_ready, 1)
                pair, m = pair_of(r, c)
                if pair is not None:
                    select(pair, m, (c // PT - 1) % 2)
                if pair is not None and m == POOLED_AT:
                    alone(dve, pooled_done, pair + 2)
                    for img in range(2):
                        b = 2 * pair + img
                        dst = (pooled[:, :, b] if isinstance(pair, int)
                               else pooled[:, :, bass.ds(b, 1)].rearrange("p e b -> p (e b)"))
                        dve.tensor_copy(dst, p_pool[:, img * E:(img + 1) * E]).then_inc(pooled_ready, 1)

            pipeline_c(dve, step)

        def expert_of(ap, r, c):
            if isinstance(r, int):
                return ap[UE * r + c]
            return ap[bass.ds(UE * r + c, 1)].rearrange("a d h -> (a d) h")

        def sync_d(sp):
            sp.dma_start(b1_raw[:], w1[:, P, :]).then_inc(bias1_loaded, 16)

            def load(r, c):
                sp.dma_start(w1_in[:, c, :], expert_of(w1[:, 0:P, :], r, c)).then_inc(w_loaded[c], 16)
                sp.dma_start(w2_in[:, c, :, :], expert_of(w2[:, 0:HID, :], r, c).rearrange("(k p) o -> p k o", p=P))\
                  .then_inc(w_loaded[c], 16)

            for k in range(2):
                sp.sem_inc(eo_stored[k], 16)
            for c in range(UE):
                load(0, c)

            def body(r, last):
                for c in range(UE):
                    sp.wait_ge(eo_ready, r * UE + c + 1)
                    sp.sem_inc(passed, 1)
                    if not last:
                        load(r + 1, c)
                    if c % 4 == 3:
                        k = c // 4
                        dst = (expert_dram[:, r * UE + c - 3:r * UE + c + 1, :] if last
                               else expert_dram[:, bass.ds(UE * r + c - 3, 4), :])
                        sp.dma_start(dst, eo[:, k, :, :]).then_inc(eo_stored[k], 16)

            rounds_d(sp, body)
            for k in range(2):
                sp.wait_ge(eo_stored[k], 16 + 16 * (E // UE))

        def tensor_d(pe):
            pe.wait_ge(bias1_loaded, 16)
            for k in range(HK):
                mm = pe.transpose(banks[4][:, k * E:(k + 1) * E], b1_raw[:, k * P:(k + 1) * P], ident[0:E, 0:E])
            mm.then_inc(bias1_turned, 1)

            def hidden(r, c):
                if c == UE:
                    r, c = r + 1, 0
                e = UE * r + c
                pe.wait_ge(w_loaded[c], 32 * r + 32)
                if not isinstance(r, int) or e >= 2:
                    pe.wait_ge(hid_pre_ready, e - 1)
                for k in range(HK):
                    mm = pe.matmul(banks[c % 2][:, k * B:(k + 1) * B], w1_in[:, c, k * P:(k + 1) * P],
                                   pooled[:, e, :] if isinstance(r, int)
                                   else pooled[:, bass.ds(e, 1), :].rearrange("p a b -> p (a b)"), start=True, stop=True)
                mm.then_inc(hid_done, 1)

            def output(r, c):
                pe.wait_ge(hid_ready, UE * r + c + 1)
                if not isinstance(r, int) or UE * r + c >= 2:
                    pe.wait_ge(eo_ready, UE * r + c - 1)
                for k in range(HK):
                    mm = pe.matmul(banks[2 + c % 2][0:B, 0:O], hid[:, c % 2, k * B:(k + 1) * B], w2_in[:, c, k, :],
                                   start=(k == 0), stop=(k == HK - 1))
                mm.then_inc(eo_done, 1)

            def body(r, last):
                for c in range(UE):
                    if not (last and c == UE - 1):
                        hidden(r, c + 1)
                    output(r, c)

            hidden(0, 0)
            body(0, False)
            with pe.Fori(1, E // UE - 1) as r:
                body(r, False)
            body(E // UE - 1, True)

        def vector_d(dve):
            dve.wait_ge(bias1_turned, 1)
            dve.tensor_copy(b1_t[:], banks[4][:, 0:HK * E].rearrange("p (k e) -> p e k", k=HK)).then_inc(bias1_ready, 1)
            dve.wait_ge(bias1_ready, 1)

            def body(r, last):
                for c in range(UE):
                    e = UE * r + c
                    dve.wait_ge(hid_done, e + 1)
                    bias = b1_t[:, e, :] if last else b1_t[:, bass.ds(e, 1), :].rearrange("p a k -> p (a k)")
                    dve.tensor_tensor(hid_pre[:, c % 2, :].rearrange("p (k b) -> p k b", k=HK),
                                      banks[c % 2][:, 0:HK * B].rearrange("p (k b) -> p k b", k=HK),
                                      bias.unsqueeze(2).to_broadcast([P, HK, B]), ALU.add).then_inc(hid_pre_ready, 1)

            rounds_d(dve, body)

        def scalar_d(act):
            def body(r, last):
                for c in range(UE):
                    e = UE * r + c
                    act.wait_ge(hid_pre_ready, e + 1)
                    act.activation(hid[:, c % 2, :], hid_pre[:, c % 2, :], ACT.Gelu).then_inc(hid_ready, 1)
                    act.wait_ge(eo_done, e + 1)
                    if c % 4 == 0:
                        act.wait_ge(eo_stored[c // 4], 16 * r + 16)
                    act.activation(eo[:, c // 4, c % 4, :], banks[2 + c % 2][0:B, 0:O], ACT.Copy).then_inc(eo_ready, 1)

            rounds_d(act, body)

        def gpsimd_d(pool):
            pass

        def img_tiles(tiles, q, img):
            n = q * PT + img * IMG_TILES
            if isinstance(q, int):
                return tiles[n:n + IMG_TILES, :, :].rearrange("t p n -> p t n")
            return tiles[bass.ds(n, IMG_TILES), :, :].rearrange("t p n -> p t n")

        def sync_e(sp):
            by_expert = expert_dram.rearrange("(q i) e o -> i e q o", i=2)
            for img in range(2):
                half = slice(img * E, (img + 1) * E)
                sp.dma_start(outputs[half, :, :], by_expert[img]).then_inc(outputs_loaded, 16)
                sp.dma_start(b2_in[half, :], w2[:, HID, :]).then_inc(outputs_loaded, 16)

            def load(r, c):
                q = 2 * r + c
                src = prob_dram[q, :, :] if isinstance(q, int) else prob_dram[bass.ds(q, 1), :, :].rearrange("a p n -> p (a n)")
                sp.dma_start(prob_in[:, c, :], src).then_inc(pair_loaded[c], 16)
                for img in range(2):
                    sp.dma_start(x3_in[:, 2 * c + img, :].rearrange("p (t n) -> p t n", n=TOK),
                                 img_tiles(x3_dram, q, img)).then_inc(pair_loaded[c], 16)

            def store(r, c, img):
                b = 4 * r + 2 * c + img
                dst = out_img[b, :, :] if isinstance(b, int) else out_img[bass.ds(b, 1), :, :].rearrange("a p n -> p (a n)")
                sp.dma_start(dst, x3_in[:, 2 * c + img, :]).then_inc(out_stored[c], 16)

            for c in range(2):
                load(0, c)

            def body(r, last):
                for c in range(2):
                    for img in range(2):
                        sp.wait_ge(out_ready, (4 * r + 2 * c + img + 1) * IMG_TILES)
                        sp.sem_inc(passed, 1)
                        store(r, c, img)
                    if not last:
                        sp.wait_ge(out_stored[c], 32 * r + 32)
                        sp.sem_inc(passed, 1)
                        load(r + 1, c)

            with sp.Fori(0, PAIRS // 2 - 1) as r:
                body(r, False)
            body(PAIRS // 2 - 1, True)
            for c in range(2):
                sp.wait_ge(out_stored[c], 32 * (PAIRS // 2))

        def tensor_e(pe):
            def body(r, first):
                for c in range(2):
                    pe.wait_ge(chosen_ready, 2 * r + c + 1)
                    pe.wait_ge(pair_loaded[c], 48 * r + 48)
                    for img in range(2):
                        half = slice(img * E, (img + 1) * E)
                        for t in range(IMG_TILES):
                            n = (2 * c + img) * IMG_TILES + t
                            if not first or n >= 8:
                                pe.wait_ge(out_ready, 4 * IMG_TILES * r + n - 7)
                            pe.matmul(banks[t][:], chosen[half, c, :], prob_in[half, c, t * TOK:(t + 1) * TOK],
                                      start=True, stop=True).then_inc(spread, 1)

            body(0, True)
            with pe.Fori(1, PAIRS // 2) as r:
                body(r, False)

        def vector_e(dve):
            dve.wait_ge(outputs_loaded, 64)
            dve.tensor_tensor(outputs[:], outputs[:], b2_in[:].unsqueeze(1).to_broadcast([P, PAIRS, O]), ALU.add)\
               .then_inc(outputs_ready, 1)
            dve.wait_ge(outputs_ready, 1)

            def choose(r, c):
                dve.tensor_copy(chosen[:, c, :], outputs[:, bass.ds(2 * r + c, 1), :].rearrange("p a o -> p (a o)"))\
                   .then_inc(chosen_ready, 1)

            with dve.Fori(0, PAIRS // 2) as r:
                for c in range(2):
                    choose(r, c)
                for c in range(2):
                    for img in range(2):
                        for t in range(IMG_TILES):
                            at = slice(t * TOK, (t + 1) * TOK)
                            dve.wait_ge(spread, 4 * IMG_TILES * r + (2 * c + img) * IMG_TILES + t + 1)
                            dve.tensor_tensor(x3_in[:, 2 * c + img, at], banks[t][:], x3_in[:, 2 * c + img, at], ALU.add)\
                               .then_inc(out_ready, 1)

        def scalar_e(act):
            pass

        def gpsimd_e(pool):
            pass

        block = ctx.enter_context(nc.Block())

        @block.sync
        def _(sp):
            run_phases(sp, sync_a, sync_b, sync_c, sync_d, sync_e)

        @block.tensor
        def _(pe):
            run_phases(pe, tensor_a, tensor_b, tensor_c, tensor_d, tensor_e)

        @block.scalar
        def _(act):
            run_phases(act, scalar_a, scalar_b, scalar_c, scalar_d, scalar_e)

        @block.gpsimd
        def _(pool):
            run_phases(pool, gpsimd_a, gpsimd_b, gpsimd_c, gpsimd_d, gpsimd_e)

        @block.vector
        def _(dve):
            run_phases(dve, vector_a, vector_b, vector_c, vector_d, vector_e)

_INS = ["x", "L0_conv_weights", "L0_ffn_W", "L0_ffn_V", "L0_ffn_gamma", "L0_ffn_beta", "L1_conv_kernel",
        "L1_ffn_gate_w", "L1_ffn_gate_b", "L1_ffn_weight1", "L1_ffn_weight2"]
_SCRATCH = [("x1", (256, 128, 512)), ("wx", (256, 128, 512)), ("y", (256, 128, 512)), ("x3", (256, 128, 512)),
            ("prob", (16, 128, 4096)), ("expert", (32, 64, 128))]


def kernel(**inputs):
    import concourse.bacc as _bacc
    from concourse import mybir as _mybir
    from concourse.bass_utils import run_bass_kernel_spmd as _run

    nc = _bacc.Bacc("TRN2", target_bir_lowering=False, num_devices=1)
    arrays, args = {}, []
    for name in _INS:
        a = np.ascontiguousarray(inputs[name])
        arrays[f"in_{name}_dram"] = a
        args.append(nc.dram_tensor(f"in_{name}_dram", a.shape, _mybir.dt.from_np(a.dtype), kind="ExternalInput").ap())
    out = nc.dram_tensor("out_0_dram", (32, 128, 64, 64), _mybir.dt.float32, kind="ExternalOutput").ap()
    scratch = [nc.dram_tensor(f"{name}_dram", shape, _mybir.dt.float32, kind="Internal").ap()
               for name, shape in _SCRATCH]
    metaformer(nc, *args, out, scratch)
    r = _run(nc, [arrays], core_ids=[0])
    return r.results[0]['out_0_dram']
```

```python
from contextlib import ExitStack

import numpy as np

import concourse.bass as bass
from concourse import mybir

F32 = mybir.dt.float32
I32 = mybir.dt.int32
ALU = mybir.AluOpType
ACT = mybir.ActivationFunctionType
AX = mybir.AxisListType

P = 128


def hermite_in_products(degree, z_scale):
    even = np.sort(np.unique(np.round((np.polynomial.hermite.hermgauss(8)[0] / z_scale) ** 2, 12)))
    odd = np.sort(np.unique(np.round((np.polynomial.hermite.hermgauss(7)[0] / z_scale) ** 2, 12)))[1:]
    order = {2: even[0], 4: even[2], 6: even[1], 8: even[3], 3: odd[0], 5: odd[1], 7: odd[2]}
    poly = np.polynomial.polynomial
    h = [np.array([np.pi ** -0.25]), np.array([0.0, np.sqrt(2.0) * z_scale * np.pi ** -0.25])]
    f = [np.array([1.0]), np.array([0.0, 1.0])]
    for k in range(2, degree + 1):
        h.append(poly.polysub(np.sqrt(2.0 / k) * poly.polymul([0.0, z_scale], h[-1]), np.sqrt((k - 1) / k) * h[-2]))
        f.append(poly.polymul([-order[k], 0.0, 1.0], f[-2]))
    change = np.zeros((degree + 1, degree + 1))
    for d in range(degree + 1):
        rest = np.zeros(degree + 1)
        rest[:len(h[d])] = h[d]
        for k in range(d, -1, -1):
            change[d, k] = rest[k]
            rest[:k + 1] -= change[d, k] * f[k]
    return order, change


def metaformer(nc, x, herm_w, ffn_w, ffn_v, gamma, beta, blur, gate_w, gate_b, w1, w2, out, scratch):
    B, C, IMG_H, IMG_W = x.shape
    T = IMG_H * IMG_W
    DEG = herm_w.shape[2] - 1
    E, _, HID = w1.shape
    O = w2.shape[2]
    TOK = 512
    IMG_TILES = T // TOK
    TILES = B * IMG_TILES
    SUB = TOK // P
    Z_SCALE = float(np.sqrt(2 * DEG + 1) + 1.0)
    CENTRE, CHANGE = hermite_in_products(DEG, Z_SCALE)
    assert C == P and O == P and 2 * E == P and T % TOK == 0

    x_img = x.rearrange("b c h w -> b c (h w)")
    out_img = out.rearrange("b c h w -> b c (h w)")
    x1_dram, wx_dram, y_dram, x3_dram, prob_dram, expert_dram = scratch

    ctx = ExitStack()
    with ctx:
        def sb(name, shape, dt=F32, scope=ctx):
            return scope.enter_context(nc.sbuf_tensor(name, shape, dt))

        def sem(name):
            return ctx.enter_context(nc.semaphore(name))

        def wait(eng, s, r, c, per=1, sub=None, unroll=4):
            sub = per if sub is None else sub
            if not isinstance(r, int) or c >= 0:
                eng.wait_ge(s, per * unroll * r + per * c + sub)

        def wait_slot(eng, slots, r, c, unroll=4):
            ring = len(slots)
            if not isinstance(r, int) or c >= 0:
                eng.wait_ge(slots[c % ring], 16 * (unroll // ring) * r + 16 * (c // ring + 1))

        psum = ctx.enter_context(nc.psum_tensor("psum", [P, 8, 512], F32))
        banks = [psum[:, i, :] for i in range(8)]

        ident = sb("ident", [P, P])
        centre = sb("centre", [P, P])
        minus_half = sb("minus_half", [P, 4])
        eps_c = sb("eps_c", [P, 4])
        eps_t = sb("eps_t", [P, 4])
        norm_a = sb("norm_a", [P, 1])
        norm_b = sb("norm_b", [P, 1])
        v_t = sb("v_t", [P, P])
        passed = sem("passed")
        phase_ended = sem("phase_ended")

        def run_phases(eng, *phases):
            for k, phase in enumerate(phases):
                if k:
                    eng.wait_ge(phase_ended, 5 * k)
                phase(eng)
                eng.drain().then_inc(phase_ended, 1)

        scope_a = ExitStack()
        herm_raw = sb("herm_raw", [P, P * (DEG + 1)], scope=scope_a)
        herm = sb("herm", [P, DEG + 1, P], scope=scope_a)
        w_raw = sb("w_raw", [P, P], scope=scope_a)
        w_t = sb("w_t", [P, P], scope=scope_a)
        v_raw = sb("v_raw", [P, P], scope=scope_a)
        gam = sb("gam", [P, 1], scope=scope_a)
        bet = sb("bet", [P, 1], scope=scope_a)
        x_in = sb("x_in", [P, 4, TOK], scope=scope_a)
        sub_stats = sb("sub_stats", [P, 2, SUB, 6], scope=scope_a)
        moments = sb("moments", [P, 2, SUB, 2], scope=scope_a)
        var_eps = sb("var_eps", [P, 2, SUB], scope=scope_a)
        rstd = sb("rstd", [P, 2, SUB], scope=scope_a)
        shift = sb("shift", [P, 2, SUB], scope=scope_a)
        z_tm = sb("z_tm", [P, 2, TOK], scope=scope_a)
        z2 = sb("z2", [P, 2, TOK], scope=scope_a)
        basis = sb("basis", [P, 2, DEG + 1, TOK], scope=scope_a)
        x1 = sb("x1", [P, 4, TOK], scope=scope_a)
        sub_stats2 = sb("sub_stats2", [P, 2, SUB, 6], scope=scope_a)
        moments2 = sb("moments2", [P, 2, SUB, 2], scope=scope_a)
        var2_eps = sb("var2_eps", [P, 2, SUB], scope=scope_a)
        rstd2 = sb("rstd2", [P, 2, SUB], scope=scope_a)
        shift2 = sb("shift2", [P, 2, SUB], scope=scope_a)
        t_tm = sb("t_tm", [P, 2, TOK], scope=scope_a)
        t_cm = sb("t_cm", [P, 2, TOK], scope=scope_a)
        wx = sb("wx", [P, 4, TOK], scope=scope_a)
        stats = sb("stats", [P, TILES, 6], scope=scope_a)
        mean_var = sb("mean_var", [P, 2], scope=scope_a)
        bn_tmp = sb("bn_tmp", [P, 4], scope=scope_a)
        scope_a.close()
        p_x, p_z, p_conv, p_x1, p_t, p_wx = (banks[0], banks[7]), banks[1], banks[2:4], banks[4], banks[5], banks[6]

        weights_loaded = sem("weights_loaded")
        ones_set = sem("ones_set")
        ident_set = sem("ident_set")
        herm_step = sem("herm_step")
        herm_ready = sem("herm_ready")
        turned = sem("turned")
        turned_used = sem("turned_used")
        x_loaded = [sem(f"x_loaded{i}") for i in range(4)]
        x_turned = sem("x_turned")
        sub_done = sem("sub_done")
        moments_ready = sem("moments_ready")
        eps_added = sem("eps_added")
        rstd_ready = sem("rstd_ready")
        shift_ready = sem("shift_ready")
        z_ready = sem("z_ready")
        z_turned = sem("z_turned")
        z2_ready = sem("z2_ready")
        gauss_ready = sem("gauss_ready")
        basis_ready = sem("basis_ready")
        conv_done = sem("conv_done")
        x1_ready = sem("x1_ready")
        x1_stored = [sem(f"x1_stored{i}") for i in range(2)]
        x1_turned = sem("x1_turned")
        sub2_done = sem("sub2_done")
        moments2_ready = sem("moments2_ready")
        eps2_added = sem("eps2_added")
        rstd2_ready = sem("rstd2_ready")
        shift2_ready = sem("shift2_ready")
        t_tm_ready = sem("t_tm_ready")
        t_turned = sem("t_turned")
        t_ready = sem("t_ready")
        wx_done = sem("wx_done")
        wx_ready = sem("wx_ready")
        stats_ready = sem("stats_ready")
        bn_step = sem("bn_step")
        bn_root = sem("bn_root")
        wx_stored = [sem(f"wx_stored{i}") for i in range(2)]

        def alone(eng, s, value):
            eng.wait_ge(s, value)
            eng.sem_inc(passed, 1)

        def pipeline(eng, step, unroll, start, lead, lag):
            rounds = (TILES - start - lead) // unroll
            for c in range(-lead, start):
                step(0, c, lambda d: 0 <= c + d < TILES)
            with eng.Fori(0, rounds) as r:
                for c in range(start, start + unroll):
                    step(r, c, lambda d: True)
            for c in range(start + rounds * unroll, TILES + lag):
                step(0, c, lambda d: 0 <= c + d < TILES)

        def tile_at(tiles, r, c, unroll):
            if isinstance(r, int):
                return tiles[c, :, :]
            return tiles[bass.ds(unroll * r + c, 1), :, :].rearrange("a p n -> p (a n)")

        def x_tile(r, c):
            part = slice(c % IMG_TILES * TOK, (c % IMG_TILES + 1) * TOK)
            if isinstance(r, int):
                return x_img[c // IMG_TILES, :, part]
            return x_img[bass.ds(r + c // IMG_TILES, 1), :, part].rearrange("a p n -> p (a n)")

        GROUP = 2
        STREAMS = 4
        SLOTS = STREAMS + 2
        GROUPS = B // GROUP
        SEG = IMG_W
        SEGS = T // SEG
        LANES = GROUP * SEGS
        WARM = 16
        QUARTER_STEPS = (WARM + SEG) // STREAMS
        TOLERANCE = 2.0 ** -21
        scope_b = ExitStack()
        wxy = [sb(f"wxy{i}", [P, WARM + GROUP * T], scope=scope_b) for i in range(SLOTS)]
        state = [sb(f"state{i}", [P, 2, LANES], scope=scope_b) for i in range(STREAMS)]
        preact = [sb(f"preact{i}", [P, LANES], scope=scope_b) for i in range(STREAMS)]
        first_state = [sb(f"first_state{i}", [P, LANES], scope=scope_b) for i in range(STREAMS)]
        gap = sb("gap", [P, GROUP, SEGS - 1], scope=scope_b)
        gap_max = sb("gap_max", [P, GROUPS + 1], scope=scope_b)
        close = sb("close", [P, 2], scope=scope_b)
        close_count = sb("close_count", [1, 1], I32, scope=scope_b)
        scope_b.close()
        AGAIN = 128
        scope_f = ExitStack()
        again_wx = sb("again_wx", [P, B, AGAIN], scope=scope_f)
        again_y = sb("again_y", [P, B, AGAIN], scope=scope_f)
        again_state = sb("again_state", [P, B], scope=scope_f)
        again_pre = sb("again_pre", [P, B], scope=scope_f)
        scope_f.close()

        pads_set = sem("pads_set")
        group_loaded = [sem(f"group_loaded{i}") for i in range(SLOTS)]
        group_stored = sem("group_stored")
        product_done = [sem(f"product_done{i}") for i in range(STREAMS)]
        preact_ready = [sem(f"preact_ready{i}") for i in range(STREAMS)]
        state_ready = [sem(f"state_ready{i}") for i in range(STREAMS)]
        first_kept = sem("first_kept")
        gap_step = sem("gap_step")
        count_done = sem("count_done")
        count_ready = sem("count_ready")
        again_loaded = sem("again_loaded")
        again_stored = sem("again_stored")
        again_product = sem("again_product")
        again_preact = sem("again_preact")
        again_step = sem("again_step")
        again_placed = sem("again_placed")

        def tokens_at(g, s):
            slot = wxy[g % SLOTS]
            if isinstance(s, int):
                return slot[:, s:s + SEG * (LANES - 1) + 1:SEG]
            return slot[:, bass.ds(s, LANES, SEG)]

        STEPS = WARM + SEG

        def states(g, s, warm):
            return (g // STREAMS) * (STEPS + 2) + s + (1 if warm else 2)

        def staggered(eng, step, begin=None, warmed=None, end=None):
            for q in range(GROUPS + STREAMS):
                if q >= STREAMS and end:
                    end(q - STREAMS)
                if q < GROUPS and begin:
                    begin(q)
                running = [(g, (q - g) * QUARTER_STEPS) for g in range(q, q - STREAMS, -1) if 0 <= g < GROUPS]
                if not running:
                    continue
                with eng.Fori(0, WARM // 4) as i:
                    for j in range(4):
                        for g, first in running:
                            step(g, 4 * i + (first + j), j % 2, g == q)
                if q < GROUPS and warmed:
                    warmed(q)
                for j in range(WARM, QUARTER_STEPS):
                    for g, first in running:
                        step(g, first + j, j % 2, False)

        PAIRS = B // 2
        PT = 2 * IMG_TILES
        SUBS = T // P
        LOW = -3.0e38
        pooled = sb("pooled", [P, E, B])
        scope_c = ExitStack()
        gates_raw = sb("gates_raw", [E, P], scope=scope_c)
        gates_t = sb("gates_t", [P, E], scope=scope_c)
        gates_c = sb("gates_c", [P, E], scope=scope_c)
        gate_bias = sb("gate_bias", [P, 1], scope=scope_c)
        taps = sb("taps", [P, 6, 4], scope=scope_c)
        diags = sb("diags", [P, 4, IMG_W], scope=scope_c)
        diags_low = sb("diags_low", [P, 4, IMG_W], scope=scope_c)
        band = sb("band", [P, 6, IMG_W], scope=scope_c)
        x_ring = sb("x_ring", [P, PT, TOK], scope=scope_c)
        y_ring = sb("y_ring", [P, 8, TOK], scope=scope_c)
        parts_c = sb("parts_c", [P, 2, SUB, 6], scope=scope_c)
        mom_c = sb("mom_c", [P, 2, SUB, 2], scope=scope_c)
        eps_sum_c = sb("eps_sum_c", [P, 2, SUB], scope=scope_c)
        root_c = sb("root_c", [P, 2, SUB], scope=scope_c)
        shift_c = sb("shift_c", [P, 2, SUB], scope=scope_c)
        blur_in = sb("blur_in", [P, 8, TOK], scope=scope_c)
        parts_t = sb("parts_t", [P, 2, SUB, 6], scope=scope_c)
        mom_t = sb("mom_t", [P, 2, SUB, 2], scope=scope_c)
        eps_sum_t = sb("eps_sum_t", [P, 2, SUB], scope=scope_c)
        root_t = sb("root_t", [P, 2, 2, SUB], scope=scope_c)
        shift_t = sb("shift_t", [P, 2, SUB], scope=scope_c)
        tokens = sb("tokens", [P, 2, 2, SUBS, P], scope=scope_c)
        logits_tm = sb("logits_tm", [P, 4, SUB, 2, E], scope=scope_c)
        logits = sb("logits", [P, 2, T], scope=scope_c)
        prob = sb("prob", [P, T], scope=scope_c)
        part_top = sb("part_top", [P, 4, 8], scope=scope_c)
        top8 = sb("top8", [P, 8], scope=scope_c)
        minus_max = sb("minus_max", [P, 1], scope=scope_c)
        exp_sum = sb("exp_sum", [P, 3], scope=scope_c)
        exp_inv = sb("exp_inv", [P, 1], scope=scope_c)
        prob_tm = sb("prob_tm", [P, 2, SUB, 2 * E], scope=scope_c)
        scope_c.close()
        p_x2, p_x3, p_blur, p_gates, p_turned, p_pool = banks[0:2], banks[2:4], banks[4], banks[5], banks[6], banks[7]

        c_loaded = sem("c_loaded")
        c_const = sem("c_const")
        diag_step = sem("diag_step")
        gates_turned = sem("gates_turned")
        gates_copied = sem("gates_copied")
        xy_loaded = [sem(f"xy_loaded{i}") for i in range(8)]
        x2_ready = sem("x2_ready")
        x2_turned = sem("x2_turned")
        parts_c_done = sem("parts_c_done")
        mom_c_ready = sem("mom_c_ready")
        eps_c_added = sem("eps_c_added")
        root_c_ready = sem("root_c_ready")
        shift_c_ready = sem("shift_c_ready")
        blur_in_ready = sem("blur_in_ready")
        blurred = sem("blurred")
        x3_ready = sem("x3_ready")
        x3_stored = [sem(f"x3_stored{i}") for i in range(4)]
        x3_turned = sem("x3_turned")
        parts_t_done = sem("parts_t_done")
        mom_t_ready = sem("mom_t_ready")
        eps_t_added = sem("eps_t_added")
        root_t_ready = sem("root_t_ready")
        shift_t_ready = sem("shift_t_ready")
        tokens_ready = sem("tokens_ready")
        gated = sem("gated")
        logits_tm_ready = sem("logits_tm_ready")
        logits_turned = sem("logits_turned")
        logits_ready = sem("logits_ready")
        part_top_ready = sem("part_top_ready")
        top_found = sem("top_found")
        minus_max_ready = sem("minus_max_ready")
        exp_ready = sem("exp_ready")
        marked = sem("marked")
        exp_inv_ready = sem("exp_inv_ready")
        masked = sem("masked")
        prob_ready = sem("prob_ready")
        prob_stored = sem("prob_stored")
        prob_turned = sem("prob_turned")
        prob_tm_ready = sem("prob_tm_ready")
        pooled_done = sem("pooled_done")
        pooled_ready = sem("pooled_ready")

        LOGITS_AT = {(2 * q + 5) % PT: q for q in range(IMG_TILES)}
        PROB_FIRST_AT = {8 + q: q for q in range(0, IMG_TILES, 2)}
        PROB_SECOND_AT = {8 + q: q + 1 for q in range(0, IMG_TILES, 2)}
        POOL_AT = {8 + q: q for q in range(IMG_TILES)}
        QUARTER = T // 4
        PART_TOP_AT = {10: 0, 14: 1, 0: 2, 3: 3}
        MASK_AT = {6: 0, 7: 1, 8: 2, 9: 3}
        SCALE_AT = MASK_AT
        TOP_AT, EXP_AT, MARK_AT, STORE_AT, POOLED_AT = 3, 4, 5, 11, 15

        def pipeline_c(eng, step):
            pipeline(eng, step, 2 * PT, PT, 6, PT)

        def wait_c(eng, s, r, c, **kw):
            wait(eng, s, r, c, unroll=2 * PT, **kw)

        def pair_of(r, c):
            pair = 2 * r + c // PT - 1
            return (pair if not isinstance(r, int) or 0 <= pair < PAIRS else None), c % PT

        def coming_pair(r, c):
            m = c % PT
            pair = 2 * r + c // PT - (1 if m < 4 else 0)
            return (pair if not isinstance(r, int) or 0 <= pair < PAIRS else None), m

        HK = HID // P
        UE = 8
        scope_d = ExitStack()
        w1_in = sb("w1_in", [P, UE, HID], scope=scope_d)
        w2_in = sb("w2_in", [P, UE, HK, O], scope=scope_d)
        b1_raw = sb("b1_raw", [E, HID], scope=scope_d)
        b1_t = sb("b1_t", [P, E, HK], scope=scope_d)
        hid_pre = sb("hid_pre", [P, 2, HK * B], scope=scope_d)
        hid = sb("hid", [P, 2, HK * B], scope=scope_d)
        eo = sb("eo", [B, 2, 4, O], scope=scope_d)

        bias1_loaded = sem("bias1_loaded")
        bias1_turned = sem("bias1_turned")
        bias1_ready = sem("bias1_ready")
        w_loaded = [sem(f"w_loaded{i}") for i in range(UE)]
        hid_done = sem("hid_done")
        hid_pre_ready = sem("hid_pre_ready")
        hid_ready = sem("hid_ready")
        eo_done = sem("eo_done")
        eo_ready = sem("eo_ready")
        eo_stored = [sem(f"eo_stored{i}") for i in range(2)]

        def skewed(eng, first, second):
            def body(r, last):
                for c in range(UE):
                    if not (last and c == UE - 1):
                        first(r, c + 1)
                    second(r, c)

            first(0, 0)
            body(0, False)
            with eng.Fori(1, E // UE - 1) as r:
                body(r, False)
            body(E // UE - 1, True)

        scope_e = ExitStack()
        RING = 3
        FULL = PAIRS // RING
        outputs = sb("outputs", [P, PAIRS, O], scope=scope_e)
        b2_in = sb("b2_in", [P, O], scope=scope_e)
        chosen = sb("chosen", [P, RING, O], scope=scope_e)
        prob_in = sb("prob_in", [P, RING, T], scope=scope_e)
        x3_in = sb("x3_in", [P, 2 * RING, T], scope=scope_e)
        scope_e.close()
        scope_d.close()

        outputs_loaded = sem("outputs_loaded")
        outputs_ready = sem("outputs_ready")
        chosen_ready = sem("chosen_ready")
        pair_loaded = [sem(f"pair_loaded{i}") for i in range(RING)]
        spread = sem("spread")
        out_ready = sem("out_ready")
        out_stored = [sem(f"out_stored{i}") for i in range(RING)]

        def img_tiles(tiles, q, img):
            n = q * PT + img * IMG_TILES
            if isinstance(q, int):
                return tiles[n:n + IMG_TILES, :, :].rearrange("t p n -> p t n")
            return tiles[bass.ds(n, IMG_TILES), :, :].rearrange("t p n -> p t n")

        def load_pair(sp, r, c):
            c, r = c % RING, r + c // RING
            q = RING * r + c
            src = prob_dram[q, :, :] if isinstance(q, int) else prob_dram[bass.ds(q, 1), :, :].rearrange("a p n -> p (a n)")
            sp.dma_start(prob_in[:, c, :], src).then_inc(pair_loaded[c], 16)
            for img in range(2):
                sp.dma_start(x3_in[:, 2 * c + img, :].rearrange("p (t n) -> p t n", n=TOK),
                             img_tiles(x3_dram, q, img)).then_inc(pair_loaded[c], 16)

        def sync_a(sp):
            for dst, src in ((herm_raw[:], herm_w.rearrange("i o d -> i (o d)")), (w_raw[:], ffn_w), (v_raw[:], ffn_v),
                             (gam[:], gamma.unsqueeze(1)), (bet[:], beta.unsqueeze(1))):
                sp.dma_start(dst, src).then_inc(weights_loaded, 16)
            for n in range(4):
                sp.dma_start(x_in[:, n, :], x_tile(0, n)).then_inc(x_loaded[n], 16)
            U = IMG_TILES

            def store(tiles, slots, ready, stored, r, n):
                wait_slot(sp, stored, r, n - 2, unroll=U)
                sp.sem_inc(passed, 1)
                wait(sp, ready, r, n, unroll=U)
                sp.sem_inc(passed, 1)
                sp.dma_start(tile_at(tiles, r, n, U), slots[:, n % 4, :]).then_inc(stored[n % 2], 16)

            def step(r, c, has):
                if has(-1):
                    store(x1_dram, x1, x1_ready, x1_stored, r, c - 1)
                if has(3) and c >= 1:
                    sp.dma_start(x_in[:, (c + 3) % 4, :], x_tile(r, c + 3)).then_inc(x_loaded[(c + 3) % 4], 16)
                if has(-2):
                    store(wx_dram, wx, wx_ready, wx_stored, r, c - 2)

            pipeline(sp, step, U, 8, 3, 2)
            for k in range(2):
                sp.wait_ge(x1_stored[k], 16 * (TILES // 2))
                sp.wait_ge(wx_stored[k], 16 * (TILES // 2))

        def tensor_a(pe):
            pe.wait_ge(weights_loaded, 80)
            pe.wait_ge(ident_set, 2)
            pe.transpose(banks[7][:, 0:P], v_raw[:], ident[:]).then_inc(turned, 1)
            pe.transpose(banks[7][:, P:2 * P], w_raw[:], ident[:]).then_inc(turned, 1)
            pe.wait_ge(herm_ready, 1)
            pe.wait_ge(turned_used, 2)

            def turn(bank, src, done):
                for j in range(SUB):
                    mm = pe.transpose(bank[:, j * P:(j + 1) * P], src[:, j * P:(j + 1) * P], ident[:])
                mm.then_inc(done, 1)

            def step(r, c, has):
                def mix(k0, k1):
                    if not has(0):
                        return
                    for k in range(k0, k1):
                        if k == 0:
                            wait(pe, x1_ready, r, c - 2)
                            wait(pe, gauss_ready, r, c)
                        else:
                            wait(pe, basis_ready, r, c, per=DEG, sub=k)
                        mm = pe.matmul(p_conv[c % 2][:], herm[:, k, :], basis[:, c % 2, k, :],
                                       start=(k == 0), stop=(k == DEG))
                    if k1 == DEG + 1:
                        mm.then_inc(conv_done, 1)

                if has(1):
                    wait(pe, z_ready, r, c + 1)
                    wait(pe, basis_ready, r, c, per=DEG, sub=1)
                    turn(p_z, z_tm[:, (c + 1) % 2, :], z_turned)
                if has(-2):
                    wait(pe, t_tm_ready, r, c - 2)
                    wait(pe, t_ready, r, c - 3)
                    turn(p_t, t_tm[:, c % 2, :], t_turned)
                mix(0, 1)
                if has(-1):
                    wait(pe, x1_ready, r, c - 1)
                    wait(pe, t_tm_ready, r, c - 2)
                    turn(p_x1, x1[:, (c - 1) % 4, :], x1_turned)
                mix(1, 3)
                if has(2):
                    wait_slot(pe, x_loaded, r, c + 2)
                    wait(pe, z_ready, r, c)
                    turn(p_x[c % 2], x_in[:, (c + 2) % 4, :], x_turned)
                mix(3, 5)
                if has(-2):
                    wait(pe, t_ready, r, c - 2)
                    wait(pe, wx_ready, r, c - 3)
                    pe.matmul(p_wx[:], w_t[:], t_cm[:, c % 2, :], start=True, stop=True).then_inc(wx_done, 1)
                mix(5, DEG + 1)

            pipeline(pe, step, 4, 8, 2, 2)

        def scalar_a(act):
            act.wait_ge(turned, 2)
            act.activation(v_t[:], banks[7][:, 0:P], ACT.Copy).then_inc(turned_used, 1)

            def normalise(dst, func, src, scale, bias, done):
                for j in range(SUB):
                    at = slice(j * P, (j + 1) * P)
                    ins = act.activation(dst[:, at], src[:, at], func, bias=bias[:, j:j + 1], scale=scale[:, j:j + 1])
                ins.then_inc(done, 1)

            def step(r, c, has):
                if has(1):
                    k = (c + 1) % 2
                    wait(act, z_turned, r, c + 1)
                    wait(act, conv_done, r, c - 1)
                    act.activation(z2[:, k, :], p_z[:], ACT.Square).then_inc(z2_ready, 1)
                    wait(act, z2_ready, r, c + 1)
                    act.activation(basis[:, k, 0, :], z2[:, k, :], ACT.Exp, scale=-0.5 * Z_SCALE ** 2)\
                       .then_inc(gauss_ready, 1)
                if has(-2):
                    k = c % 2
                    wait(act, t_turned, r, c - 2)
                    wait(act, wx_done, r, c - 4)
                    act.activation(t_cm[:, k, :], p_t[:], ACT.Copy).then_inc(t_ready, 1)
                if has(-1):
                    k = (c - 1) % 2
                    wait(act, shift2_ready, r, c - 1)
                    wait(act, t_turned, r, c - 3)
                    normalise(t_tm[:, k, :], ACT.Identity, p_x1, rstd2[:, k, :], shift2[:, k, :], t_tm_ready)
                if has(2):
                    k = c % 2
                    wait(act, shift_ready, r, c + 2)
                    wait(act, z_turned, r, c)
                    normalise(z_tm[:, k, :], ACT.Tanh, p_x[k], rstd[:, k, :], shift[:, k, :], z_ready)
                if has(-2):
                    wait(act, wx_done, r, c - 2)
                    wait_slot(act, wx_stored, r, c - 6)
                    wait(act, stats_ready, r, c - 6)
                    act.activation(wx[:, (c - 2) % 4, :], p_wx[:], ACT.Copy).then_inc(wx_ready, 1)

            pipeline(act, step, 4, 8, 2, 2)

        def gpsimd_a(pool):
            pool.memset(ident[:], 0.0).then_inc(ones_set, 1)
            pool.memset(centre[:], -1.0 / C).then_inc(ones_set, 1)
            for tile, value in ((minus_half, -0.5), (eps_c, 1e-6), (eps_t, 1e-5)):
                pool.memset(tile[:], value).then_inc(ones_set, 1)
            pool.wait_ge(ones_set, 5)
            for m, diagonal in ((ident, 1.0), (centre, 1.0 - 1.0 / C)):
                pool.affine_select(out=m[:], in_=m[:], compare_op=ALU.not_equal, fill=diagonal, base=0,
                                   pattern=[[-1, P]], channel_multiplier=1).then_inc(ident_set, 1)

            def inverse_root(r, c, given, eps, values, added_eps, added, result, ready, free):
                k = c % 2
                wait(pool, given, r, c)
                pool.tensor_tensor(added_eps[:, k, :], values[:, k, :, 1], eps[:], ALU.add).then_inc(added, 1)
                wait(pool, added, r, c)
                wait(pool, free, r, c - 2)
                pool.tensor_tensor(result[:, k, :], added_eps[:, k, :], minus_half[:], ALU.pow).then_inc(ready, 1)

            def step(r, c, has):
                if has(-1):
                    inverse_root(r, c - 1, moments2_ready, eps_t, moments2, var2_eps, eps2_added, rstd2, rstd2_ready,
                                 t_tm_ready)
                if has(2):
                    inverse_root(r, c + 2, moments_ready, eps_c, moments, var_eps, eps_added, rstd, rstd_ready, z_ready)

            pipeline(pool, step, 4, 8, 2, 2)
            pool.wait_ge(bn_step, 2)
            pool.tensor_tensor(bn_tmp[:, 1:2], bn_tmp[:, 0:1], minus_half[:, 0:1], ALU.pow).then_inc(bn_root, 1)

        def vector_a(dve):
            raw = herm_raw[:].rearrange("i (o d) -> i d o", d=DEG + 1)
            dve.wait_ge(weights_loaded, 80)
            done = 0
            for n, d in enumerate(range(DEG, -1, -1)):
                for k in range(d, -1, -2):
                    first = d >= DEG - 1
                    if first:
                        ins = dve.tensor_scalar(herm[:, k, :], raw[:, d, :], float(CHANGE[d, k]), None, ALU.mult)
                    else:
                        ins = dve.scalar_tensor_tensor(herm[:, k, :], raw[:, d, :], float(CHANGE[d, k]),
                                                       herm[:, k, :], ALU.mult, ALU.add)
                    ins.then_inc(herm_step, 1)
                    done += 1
                dve.wait_ge(herm_step, done)
            dve.wait_ge(turned, 2)
            dve.wait_ge(turned_used, 1)
            dve.tensor_copy(w_t[:], banks[7][:, P:2 * P]).then_inc(turned_used, 1)
            dve.memset(bn_tmp[:], 1e-5).then_inc(herm_ready, 1)

            def token_moments(r, c, given, src, parts, parts_done, values, ready):
                k = c % 2
                wait(dve, given, r, c)
                for j in range(SUB):
                    ins = dve.bn_stats(parts[:, k, j, :], src[:, j * P:(j + 1) * P])
                ins.then_inc(parts_done, 1)
                wait(dve, parts_done, r, c)
                dve.sem_inc(passed, 1)
                for j in range(SUB):
                    ins = dve.bn_aggr(values[:, k, j, :], parts[:, k, j, :])
                ins.then_inc(ready, 1)

            def shifts(r, c, root_ready, values, root, result, free, ready):
                k = c % 2
                wait(dve, root_ready, r, c)
                wait(dve, free, r, c - 2)
                dve.scalar_tensor_tensor(result[:, k, :], values[:, k, :, 0], -1.0, root[:, k, :], ALU.mult, ALU.mult)\
                   .then_inc(ready, 1)

            def basis_functions(r, c, lo, hi):
                k = c % 2
                for d in range(lo, hi):
                    if d == 1:
                        wait(dve, gauss_ready, r, c)
                        wait(dve, conv_done, r, c - 2)
                        dve.tensor_tensor(basis[:, k, 1, :], p_z[:], basis[:, k, 0, :], ALU.mult).then_inc(basis_ready, 1)
                        continue
                    if d > 2:
                        wait(dve, basis_ready, r, c, per=DEG, sub=d - 2)
                    dve.scalar_tensor_tensor(basis[:, k, d, :], z2[:, k, :], float(CENTRE[d]), basis[:, k, d - 2, :],
                                             ALU.subtract, ALU.mult).then_inc(basis_ready, 1)

            def step(r, c, has):
                if has(-1):
                    wait(dve, conv_done, r, c - 1)
                    wait_slot(dve, x1_stored, r, c - 5)
                    dve.tensor_tensor(x1[:, (c - 1) % 4, :], p_conv[(c - 1) % 2][:], x_in[:, (c - 1) % 4, :], ALU.add)\
                       .then_inc(x1_ready, 1)
                if has(-1):
                    token_moments(r, c - 1, x1_turned, p_x1, sub_stats2, sub2_done, moments2, moments2_ready)
                if has(1):
                    basis_functions(r, c + 1, 1, 4)
                if has(2):
                    token_moments(r, c + 2, x_turned, p_x[c % 2], sub_stats, sub_done, moments, moments_ready)
                if has(-1):
                    shifts(r, c - 1, rstd2_ready, moments2, rstd2, shift2, t_tm_ready, shift2_ready)
                if has(1):
                    basis_functions(r, c + 1, 4, 7)
                if has(2):
                    shifts(r, c + 2, rstd_ready, moments, rstd, shift, z_ready, shift_ready)
                if has(1):
                    basis_functions(r, c + 1, 7, DEG + 1)
                if has(-3):
                    n = c - 3
                    wait(dve, wx_ready, r, n)
                    dve.sem_inc(passed, 1)
                    dst = stats[:, n, :] if isinstance(r, int) else stats[:, bass.ds(4 * r + n, 1), :].rearrange("p a s -> p (a s)")
                    dve.bn_stats(dst, wx[:, n % 4, :]).then_inc(stats_ready, 1)

            pipeline(dve, step, 4, 8, 2, 3)
            dve.wait_ge(stats_ready, TILES)
            dve.bn_aggr(mean_var[:], stats[:].rearrange("p n s -> p (n s)")).then_inc(bn_step, 1)
            dve.wait_ge(bn_step, 1)
            dve.tensor_scalar(bn_tmp[:, 0:1], mean_var[:, 1:2], 1e-5, None, ALU.add).then_inc(bn_step, 1)
            dve.wait_ge(bn_root, 1)
            dve.tensor_tensor(norm_a[:], gam[:], bn_tmp[:, 1:2], ALU.mult).then_inc(bn_step, 1)
            dve.wait_ge(bn_step, 3)
            dve.tensor_tensor(bn_tmp[:, 2:3], mean_var[:, 0:1], norm_a[:], ALU.mult).then_inc(bn_step, 1)
            dve.wait_ge(bn_step, 4)
            dve.tensor_tensor(norm_b[:], bet[:], bn_tmp[:, 2:3], ALU.subtract).then_inc(bn_step, 1)

        def group_tiles(tiles, g, img):
            n = (g * GROUP + img) * IMG_TILES
            return tiles[n:n + IMG_TILES, :, :].rearrange("t p n -> p t n")

        def group_slot(g, img):
            lo = WARM + img * T
            return wxy[g % SLOTS][:, lo:lo + T].rearrange("p (t n) -> p t n", n=TOK)

        def if_again(eng):
            eng.wait_ge(count_ready, 1)
            return eng.If(eng.value_load(close_count[0:1, 0:1], min_val=0, max_val=P) < P)

        def sync_b(sp):
            def load(g):
                for img in range(GROUP):
                    sp.dma_start(group_slot(g, img), group_tiles(wx_dram, g, img)).then_inc(group_loaded[g % SLOTS], 16)

            for g in range(SLOTS):
                load(g)
            for g in range(GROUPS):
                sp.wait_ge(state_ready[g % STREAMS], (g // STREAMS + 1) * (STEPS + 2))
                for img in range(GROUP):
                    sp.dma_start(group_tiles(y_dram, g, img), group_slot(g, img)).then_inc(group_stored, 16)
                if g + SLOTS < GROUPS:
                    sp.wait_ge(group_stored, 16 * GROUP * (g + 1))
                    sp.wait_ge(gap_step, 2 * g + 2)
                    load(g + SLOTS)
            sp.wait_ge(group_stored, 16 * GROUP * GROUPS)
            with if_again(sp):
                wx_at = wx_dram.rearrange("(b t) p n -> t p b n", t=IMG_TILES)
                y_at = y_dram.rearrange("(b t) p n -> t p b n", t=IMG_TILES)
                with sp.Fori(0, IMG_TILES) as t:
                    for part in range(TOK // AGAIN):
                        cols = slice(part * AGAIN, (part + 1) * AGAIN)
                        n = t * (TOK // AGAIN) + part
                        sp.dma_start(again_wx[:], wx_at[bass.ds(t, 1), :, :, cols].rearrange("t p b n -> p (t b) n"))\
                          .then_inc(again_loaded, 16)
                        sp.wait_ge(again_placed, n * AGAIN + AGAIN + 1)
                        sp.sem_inc(passed, 1)
                        sp.dma_start(y_at[bass.ds(t, 1), :, :, cols].rearrange("t p b n -> p (t b) n"), again_y[:])\
                          .then_inc(again_stored, 16)
                        sp.wait_ge(again_stored, n * 16 + 16)
                        sp.sem_inc(passed, 1)

        def tensor_b(pe):
            def step(g, s, odd, warm):
                k = g % STREAMS
                before = state[k][:, 1 - odd, :] if warm or (isinstance(s, int) and s == WARM) else tokens_at(g, s - 1)
                pe.wait_ge(state_ready[k], states(g, s, warm))
                pe.matmul(banks[k][:, 0:LANES], v_t[:], before, start=True, stop=True).then_inc(product_done[k], 1)

            staggered(pe, step)
            pe.wait_ge(gap_step, 2 * GROUPS + 3)
            pe.matmul(banks[4][0:1, 0:1], close[:, 0:1], close[:, 1:2], start=True, stop=True).then_inc(count_done, 1)
            with if_again(pe):
                with pe.Fori(0, T) as t:
                    pe.wait_ge(again_step, t + 1)
                    pe.matmul(banks[5][:, 0:B], v_t[:], again_state[:], start=True, stop=True).then_inc(again_product, 1)

        def vector_b(dve):
            for slot in wxy:
                dve.memset(slot[:, 0:WARM], 0.0).then_inc(pads_set, 1)
            dve.wait_ge(pads_set, SLOTS)

            def begin(g):
                dve.wait_ge(group_loaded[g % SLOTS], 16 * GROUP * (g // SLOTS + 1))
                dve.memset(state[g % STREAMS][:, 1, :], 0.0).then_inc(state_ready[g % STREAMS], 1)

            def step(g, s, odd, warm):
                k = g % STREAMS
                dve.wait_ge(product_done[k], (g // STREAMS) * STEPS + s + 1)
                dve.scalar_tensor_tensor(preact[k][:], tokens_at(g, s), norm_a[:], banks[k][:, 0:LANES],
                                         ALU.mult, ALU.add).then_inc(preact_ready[k], 1)

            def warmed(g):
                k = g % STREAMS
                dve.wait_ge(state_ready[k], states(g, WARM, True))
                dve.memset(state[k][:, 1, 0:SEGS * (GROUP - 1) + 1:SEGS], 0.0).then_inc(state_ready[k], 1)
                dve.wait_ge(state_ready[k], states(g, WARM, False))
                dve.tensor_copy(first_state[k][:], state[k][:, 1, :]).then_inc(first_kept, 1)

            def end(g):
                k = g % STREAMS
                dve.wait_ge(state_ready[k], states(g, STEPS, False))
                dve.wait_ge(first_kept, g + 1)
                last = tokens_at(g, STEPS - 1).rearrange("p (b k) -> p b k", b=GROUP)
                first = first_state[k][:].rearrange("p (b k) -> p b k", b=GROUP)
                if g:
                    dve.wait_ge(gap_step, 2 * g)
                dve.tensor_tensor(gap[:], last[:, :, 0:SEGS - 1], first[:, :, 1:SEGS], ALU.subtract).then_inc(gap_step, 1)
                dve.wait_ge(gap_step, 2 * g + 1)
                dve.tensor_reduce(gap_max[:, g:g + 1], gap[:].rearrange("p b k -> p (b k)"), AX.X, ALU.max,
                                  apply_absolute_value=True).then_inc(gap_step, 1)

            staggered(dve, step, begin, warmed, end)
            dve.memset(close[:, 1:2], 1.0).then_inc(gap_step, 1)
            dve.wait_ge(gap_step, 2 * GROUPS + 1)
            dve.tensor_reduce(gap_max[:, GROUPS:GROUPS + 1], gap_max[:, 0:GROUPS], AX.X, ALU.max).then_inc(gap_step, 1)
            dve.wait_ge(gap_step, 2 * GROUPS + 2)
            dve.tensor_scalar(close[:, 0:1], gap_max[:, GROUPS:GROUPS + 1], TOLERANCE, None, ALU.is_le)\
               .then_inc(gap_step, 1)
            dve.wait_ge(count_done, 1)
            dve.tensor_copy(close_count[:], banks[4][0:1, 0:1]).then_inc(count_ready, 1)
            with if_again(dve):
                dve.wait_ge(again_loaded, 16)
                dve.memset(again_state[:], 0.0).then_inc(again_step, 1)
                with dve.Fori(0, T // AGAIN) as n:
                    dve.wait_ge(again_loaded, n * 16 + 16)
                    dve.sem_inc(passed, 1)
                    with dve.Fori(0, AGAIN) as t:
                        dve.wait_ge(again_product, n * AGAIN + t + 1)
                        dve.scalar_tensor_tensor(again_pre[:], again_wx[:, :, bass.ds(t, 1)].rearrange("p b n -> p (b n)"),
                                                 norm_a[:], banks[5][:, 0:B], ALU.mult, ALU.add).then_inc(again_preact, 1)

        def scalar_b(act):
            def step(g, s, odd, warm):
                k = g % STREAMS
                alone(act, preact_ready[k], (g // STREAMS) * STEPS + s + 1)
                after = state[k][:, odd, :] if warm else tokens_at(g, s)
                act.activation(after, preact[k][:], ACT.Sigmoid, bias=norm_b[:]).then_inc(state_ready[k], 1)

            staggered(act, step)
            with if_again(act):
                with act.Fori(0, T) as t:
                    act.wait_ge(again_preact, t + 1)
                    act.wait_ge(again_placed, t + 1)
                    act.activation(again_state[:], again_pre[:], ACT.Sigmoid, bias=norm_b[:]).then_inc(again_step, 1)

        def gpsimd_b(pool):
            with if_again(pool):
                pool.sem_inc(again_placed, 1)
                with pool.Fori(0, T // AGAIN) as n:
                    with pool.Fori(0, AGAIN) as t:
                        pool.wait_ge(again_step, n * AGAIN + t + 2)
                        pool.sem_inc(passed, 1)
                        pool.tensor_copy(again_y[:, :, bass.ds(t, 1)].rearrange("p b n -> p (b n)"), again_state[:])\
                            .then_inc(again_placed, 1)

        band_cols = band[:].rearrange("p w j -> p (w j)")

        def sync_c(sp):
            sp.dma_start(gates_raw[:], gate_w).then_inc(c_loaded, 16)
            for half in range(2):
                sp.dma_start(gate_bias[half * E:(half + 1) * E, :], gate_b.unsqueeze(1)).then_inc(c_loaded, 16)
            sp.wait_ge(c_const, 1)
            for half in range(2):
                sp.dma_start(taps[half * IMG_W:(half + 1) * IMG_W, 1 + half:5 + half, :],
                             blur.rearrange("u v -> (u v)").partition_broadcast(IMG_W)
                             .rearrange("p (u v) -> p u v", v=4)).then_inc(c_loaded, 16)

            def at(tiles, r, c):
                n = c // PT * PT + c % 2 * IMG_TILES + c % PT // 2
                return tile_at(tiles, r, n, 2 * PT)

            def load(r, c):
                sp.dma_start(x_ring[:, c % PT, :], at(x1_dram, r, c)).then_inc(xy_loaded[c % 8], 16)
                sp.dma_start(y_ring[:, c % 8, :], at(y_dram, r, c)).then_inc(xy_loaded[c % 8], 16)

            for k in range(8):
                load(0, k)
            sp.sem_inc(prob_stored, 16)

            def step(r, c, has):
                if has(0):
                    if not isinstance(r, int) or c >= 4:
                        alone(sp, x3_stored[c % 4], 16 * (8 * r + (c - 4) // 4 + 1))
                    wait_c(sp, x3_ready, r, c)
                    sp.sem_inc(passed, 1)
                    sp.dma_start(at(x3_dram, r, c), x_ring[:, c % PT, :]).then_inc(x3_stored[c % 4], 16)
                if has(8) and c >= 0:
                    if not isinstance(r, int) or c >= 8:
                        wait_c(sp, gated, r, c - 8)
                        sp.sem_inc(passed, 1)
                    load(r, c + 8)
                pair, m = pair_of(r, c)
                if pair is not None and m == STORE_AT:
                    sp.wait_ge(prob_ready, 4 * pair + 4)
                    sp.sem_inc(passed, 1)
                    dst = (prob_dram[pair, :, :] if isinstance(r, int)
                           else prob_dram[bass.ds(pair, 1), :, :].rearrange("a p n -> p (a n)"))
                    sp.dma_start(dst, prob[:]).then_inc(prob_stored, 16)

            pipeline(sp, step, 2 * PT, PT, 8, PT)
            for k in range(4):
                sp.wait_ge(x3_stored[k], 16 * (TILES // 4))
            sp.wait_ge(prob_stored, 16 * PAIRS + 16)

        def tensor_c(pe):
            pe.wait_ge(c_loaded, 80)
            pe.transpose(banks[0][:, 0:E], gates_raw[:], ident[0:E, 0:E]).then_inc(gates_turned, 1)
            pe.wait_ge(gates_copied, 1)
            pe.matmul(banks[1][:, 0:E], centre[:], gates_t[:], start=True, stop=True).then_inc(gates_turned, 1)
            pe.wait_ge(gates_copied, 3 + 4 * 6)
            pe.sem_inc(pooled_done, 1)

            def turn(bank, src, done):
                for j in range(SUB):
                    mm = pe.transpose(bank[:, j * P:(j + 1) * P], src[:, j * P:(j + 1) * P], ident[:])
                mm.then_inc(done, 1)

            def step(r, c, has):
                coming, m = coming_pair(r, c)
                pair, _ = pair_of(r, c)

                def turn_logits(q):
                    pe.wait_ge(logits_tm_ready, 8 * coming + q + 1)
                    if 2 <= q < 6 and pair is not None:
                        pe.wait_ge(prob_tm_ready, 8 * pair + 2 * (q - 1))
                    elif not isinstance(coming, int) or 8 * coming + q:
                        pe.wait_ge(logits_ready, 8 * coming + q)
                    turn(p_turned, logits_tm[:, q % 4, :, :, :].rearrange("p s i e -> p (s i e)"), logits_turned)

                def turn_prob(q):
                    pe.wait_ge(prob_ready, 4 * pair + q // 2 + 1)
                    if q % 2:
                        pe.wait_ge(prob_tm_ready, 8 * pair + q)
                    elif coming is not None:
                        pe.wait_ge(logits_ready, 8 * coming + 2 + q // 2)
                    elif q:
                        pe.wait_ge(prob_tm_ready, 8 * pair + q)
                    turn(p_turned, prob[:, q * TOK:(q + 1) * TOK], prob_turned)

                if coming is not None and m in LOGITS_AT:
                    turn_logits(LOGITS_AT[m])
                if pair is not None and m in PROB_FIRST_AT:
                    turn_prob(PROB_FIRST_AT[m])
                if has(-2):
                    n = c - 2
                    wait_c(pe, x3_ready, r, n)
                    wait_c(pe, tokens_ready, r, n - 2)
                    turn(p_x3[n % 2], x_ring[:, n % PT, :], x3_turned)
                if has(4):
                    n = c + 4
                    wait_c(pe, x2_ready, r, n)
                    wait_c(pe, blur_in_ready, r, n - 2)
                    turn(p_x2[n % 2], x_ring[:, n % PT, :], x2_turned)
                if has(0):
                    wait_c(pe, blur_in_ready, r, c + 2 if c % PT < PT - 2 else c)
                    wait_c(pe, x3_ready, r, c - 1)
                    part = c % PT // 2
                    first, end = part * TOK, (part + 1) * TOK
                    reach = [s for s in range(part * SUB - 1, part * SUB + SUB + 1) if 0 <= s < SUBS]
                    for s in reach:
                        lo, hi = max(s * P - IMG_W, first), min((s + 2) * P, end)
                        if lo >= hi:
                            continue
                        n = c + 2 * (s // SUB - part)
                        mm = pe.matmul(p_blur[:, lo - first:hi - first],
                                       blur_in[:, n % 8, s % SUB * P:(s % SUB + 1) * P],
                                       band_cols[:, lo - s * P + P:hi - s * P + P],
                                       start=(s == reach[0]), stop=(s == reach[-1]), skip_group_check=True)
                    mm.then_inc(blurred, 1)
                if pair is not None and m in PROB_SECOND_AT:
                    turn_prob(PROB_SECOND_AT[m])
                if has(-2):
                    n = c - 2
                    if n % 2 == 0:
                        wait(pe, logits_tm_ready, r, n // 2 - 1, unroll=PT)
                    out = p_gates.rearrange("p (s i e) -> p s i e", s=SUB, i=2)
                    for s in range(SUB):
                        mm = pe.matmul(out[:, s, n % 2, :], x_ring[:, n % PT, s * P:(s + 1) * P], gates_c[:],
                                       start=True, stop=True)
                    mm.then_inc(gated, 1)
                if pair is not None and m in POOL_AT:
                    q = POOL_AT[m]
                    pe.wait_ge(prob_tm_ready, 8 * pair + q + 1)
                    for s in range(SUB):
                        for img in range(2):
                            mm = pe.matmul(p_pool[:, img * E:(img + 1) * E],
                                           tokens[:, (c // PT - 1) % 2, img, q * SUB + s, :],
                                           prob_tm[:, q % 2, s, img * E:(img + 1) * E],
                                           start=(q == 0 and s == 0 and img == 0),
                                           stop=(q == IMG_TILES - 1 and s == SUB - 1), skip_group_check=True)
                    if q == IMG_TILES - 1:
                        mm.then_inc(pooled_done, 1)

            pipeline_c(pe, step)

        def scalar_c(act):
            def normalise(dst, src, scale, bias, done):
                for j in range(SUB):
                    at = slice(j * P, (j + 1) * P)
                    ins = act.activation(dst[:, at], src[:, at], ACT.Identity, bias=bias[:, j:j + 1],
                                         scale=scale[:, j:j + 1])
                ins.then_inc(done, 1)

            def step(r, c, has):
                coming, m = coming_pair(r, c)
                pair, _ = pair_of(r, c)

                def copy_prob(q):
                    act.wait_ge(prob_turned, 8 * pair + q + 1)
                    act.activation(prob_tm[:, q % 2, :, :].rearrange("p s e -> p (s e)"), p_turned, ACT.Copy)\
                       .then_inc(prob_tm_ready, 1)

                def exponentials(half):
                    at = slice(half * T // 2, (half + 1) * T // 2)
                    act.activation(prob[:, at], logits[:, (c // PT - 1) % 2, at], ACT.Exp, bias=minus_max[:],
                                   accum_out=exp_sum[:, half:half + 1]).then_inc(exp_ready, 1)

                if pair is not None and m == EXP_AT:
                    act.wait_ge(minus_max_ready, pair + 1)
                    act.wait_ge(prob_stored, 16 * pair + 16)
                    exponentials(0)
                if coming is not None and m in LOGITS_AT:
                    q = LOGITS_AT[m]
                    act.wait_ge(logits_turned, 8 * coming + q + 1)
                    if q == 0:
                        if not isinstance(coming, int) or coming:
                            act.wait_ge(masked, 4 * coming)
                    act.activation(logits[:, (c - 4) // PT % 2, q * TOK:(q + 1) * TOK], p_turned, ACT.Identity,
                                   bias=gate_bias[:]).then_inc(logits_ready, 1)
                if pair is not None and m in PROB_FIRST_AT:
                    copy_prob(PROB_FIRST_AT[m])
                if has(-2):
                    n = c - 2
                    k = n % 2
                    if n % PT == 0:
                        if not isinstance(r, int) or n // PT:
                            act.wait_ge(pooled_done, 2 * r + n // PT)
                    wait_c(act, shift_t_ready, r, n)
                    lo = n % PT // 2 * SUB
                    normalise(tokens[:, n // PT % 2, n % 2, lo:lo + SUB, :].rearrange("p s d -> p (s d)"), p_x3[n % 2],
                              root_t[:, n // 2 % 2, n % 2, :], shift_t[:, k, :], tokens_ready)
                if pair is not None and m in PROB_SECOND_AT:
                    copy_prob(PROB_SECOND_AT[m])
                if has(4):
                    n = c + 4
                    wait_c(act, shift_c_ready, r, n)
                    wait_c(act, blurred, r, n - 5)
                    normalise(blur_in[:, n % 8, :], p_x2[n % 2], root_c[:, n % 2, :], shift_c[:, n % 2, :], blur_in_ready)
                if pair is not None and m == EXP_AT:
                    exponentials(1)

            pipeline_c(act, step)

        def gpsimd_c(pool):
            pool.memset(taps[:], 0.0).then_inc(c_const, 1)
            for k, (m, shift) in enumerate(((diags, 0), (diags_low, IMG_W))):
                pool.memset(m[:], 0.0).then_inc(diag_step, 1)
                pool.wait_ge(diag_step, 2 * k + 1)
                pool.affine_select(out=m[:], in_=m[:], compare_op=ALU.not_equal, fill=1.0, base=shift + 1,
                                   pattern=[[-1, 4], [1, IMG_W]], channel_multiplier=-1).then_inc(diag_step, 1)

            def inverse_root(r, n, given, eps, values, added_eps, added, result, ready, free):
                wait_c(pool, given, r, n)
                pool.tensor_tensor(added_eps[:, n % 2, :], values[:, n % 2, :, 1], eps[:], ALU.add).then_inc(added, 1)
                wait_c(pool, added, r, n)
                wait_c(pool, free, r, n - 2)
                pool.tensor_tensor(result, added_eps[:, n % 2, :], minus_half[:], ALU.pow).then_inc(ready, 1)

            def step(r, c, has):
                if has(-2):
                    n = c - 2
                    if n % 2 == 0:
                        wait(pool, logits_tm_ready, r, n // 2 - 2, unroll=PT)
                    inverse_root(r, n, mom_t_ready, eps_t, mom_t, eps_sum_t, eps_t_added, root_t[:, n // 2 % 2, n % 2, :],
                                 root_t_ready, tokens_ready)
                if has(4):
                    n = c + 4
                    inverse_root(r, n, mom_c_ready, eps_c, mom_c, eps_sum_c, eps_c_added, root_c[:, n % 2, :],
                                 root_c_ready, blur_in_ready)
                if has(6):
                    n = c + 6
                    pool.wait_ge(xy_loaded[n % 8], 32 * (4 * r + n // 8 + 1))
                    pool.tensor_tensor(x_ring[:, n % PT, :], x_ring[:, n % PT, :], y_ring[:, n % 8, :], ALU.add)\
                        .then_inc(x2_ready, 1)

            pipeline_c(pool, step)

        def vector_c(dve):
            dve.wait_ge(gates_turned, 1)
            dve.tensor_copy(gates_t[:], banks[0][:, 0:E]).then_inc(gates_copied, 1)
            dve.wait_ge(gates_turned, 2)
            dve.tensor_copy(gates_c[:], banks[1][:, 0:E]).then_inc(gates_copied, 1)
            dve.wait_ge(diag_step, 4)
            dve.tensor_copy(diags[IMG_W:P, :, :], diags_low[IMG_W:P, :, :]).then_inc(gates_copied, 1)
            dve.wait_ge(c_loaded, 80)
            dve.wait_ge(gates_copied, 3)
            for v in range(4):
                for w in range(6):
                    if v == 0:
                        ins = dve.tensor_scalar(band[:, w, :], diags[:, v, :], taps[:, w, v:v + 1], None, ALU.mult)
                    else:
                        ins = dve.scalar_tensor_tensor(band[:, w, :], diags[:, v, :], taps[:, w, v:v + 1], band[:, w, :],
                                                       ALU.mult, ALU.add)
                    ins.then_inc(gates_copied, 1)
                dve.wait_ge(gates_copied, 3 + 6 * (v + 1))

            dve.sem_inc(masked, 4)

            def token_moments(r, n, given, src, parts, parts_done, values, ready):
                wait_c(dve, given, r, n)
                for j in range(SUB):
                    ins = dve.bn_stats(parts[:, n % 2, j, :], src[:, j * P:(j + 1) * P])
                ins.then_inc(parts_done, 1)
                wait_c(dve, parts_done, r, n)
                dve.sem_inc(passed, 1)
                for j in range(SUB):
                    ins = dve.bn_aggr(values[:, n % 2, j, :], parts[:, n % 2, j, :])
                ins.then_inc(ready, 1)

            def shifts(r, n, root_ready, values, root, result, ready):
                wait_c(dve, root_ready, r, n)
                dve.scalar_tensor_tensor(result[:, n % 2, :], values[:, n % 2, :, 0], -1.0, root, ALU.mult, ALU.mult)\
                   .then_inc(ready, 1)

            def select(pair, m, slot):
                if m == TOP_AT:
                    alone(dve, part_top_ready, 4 * pair + 4)
                    dve.max(top8[:], part_top[:].rearrange("p k n -> p (k n)")).then_inc(top_found, 1)
                    dve.wait_ge(top_found, pair + 1)
                    dve.tensor_scalar(minus_max[:], top8[:, 0:1], -1.0, None, ALU.mult).then_inc(minus_max_ready, 1)
                if m == MARK_AT:
                    alone(dve, exp_ready, 2 * pair + 2)
                    dve.match_replace(logits[:, slot, :], top8[:], logits[:, slot, :], LOW).then_inc(marked, 1)
                    dve.tensor_tensor(exp_sum[:, 2:3], exp_sum[:, 0:1], exp_sum[:, 1:2], ALU.add).then_inc(exp_inv_ready, 1)
                if m in MASK_AT:
                    at = slice(MASK_AT[m] * QUARTER, (MASK_AT[m] + 1) * QUARTER)
                    if MASK_AT[m] == 0:
                        dve.wait_ge(exp_inv_ready, 2 * pair + 1)
                        dve.reciprocal(exp_inv[:], exp_sum[:, 2:3]).then_inc(exp_inv_ready, 1)
                        dve.wait_ge(marked, pair + 1)
                    dve.scalar_tensor_tensor(prob[:, at], logits[:, slot, at], LOW, prob[:, at], ALU.is_equal, ALU.mult)\
                       .then_inc(masked, 1)
                if m in SCALE_AT:
                    k = SCALE_AT[m]
                    at = slice(k * QUARTER, (k + 1) * QUARTER)
                    dve.wait_ge(masked, 4 * pair + k + 5)
                    if k == 0:
                        dve.wait_ge(exp_inv_ready, 2 * pair + 2)
                    dve.tensor_scalar(prob[:, at], prob[:, at], exp_inv[:], None, ALU.mult).then_inc(prob_ready, 1)

            def step(r, c, has):
                def add_blur():
                    wait_c(dve, blurred, r, c)
                    dve.tensor_tensor(x_ring[:, c % PT, :], p_blur, x_ring[:, c % PT, :], ALU.add).then_inc(x3_ready, 1)

                late = pair_of(r, c)[0] is not None and c % PT == MARK_AT + 1
                if late and has(0):
                    add_blur()
                if has(-2):
                    token_moments(r, c - 2, x3_turned, p_x3[c % 2], parts_t, parts_t_done, mom_t, mom_t_ready)
                if has(4):
                    token_moments(r, c + 4, x2_turned, p_x2[c % 2], parts_c, parts_c_done, mom_c, mom_c_ready)
                coming, m = coming_pair(r, c)
                if coming is not None and m in PART_TOP_AT:
                    k = PART_TOP_AT[m]
                    alone(dve, logits_ready, 8 * coming + 2 * k + 2)
                    dve.max(part_top[:, k, :], logits[:, (c - 4) // PT % 2, k * QUARTER:(k + 1) * QUARTER])\
                       .then_inc(part_top_ready, 1)
                if has(-2):
                    n = c - 2
                    wait_c(dve, tokens_ready, r, n - 2)
                    shifts(r, n, root_t_ready, mom_t, root_t[:, n // 2 % 2, n % 2, :], shift_t, shift_t_ready)
                if not late and has(0):
                    add_blur()
                if has(4):
                    wait_c(dve, blur_in_ready, r, c + 2)
                    shifts(r, c + 4, root_c_ready, mom_c, root_c[:, c % 2, :], shift_c, shift_c_ready)
                if has(-2) and c % 2 == 1:
                    n = c - 2
                    wait_c(dve, gated, r, n)
                    wait_c(dve, root_t_ready, r, n)
                    scale = root_t[:, n // 2 % 2, :, :].rearrange("p i s -> p s i").unsqueeze(3).to_broadcast([P, SUB, 2, E])
                    dve.tensor_tensor(logits_tm[:, n // 2 % 4, :, :, :], p_gates.rearrange("p (s i e) -> p s i e", s=SUB, i=2),
                                      scale, ALU.mult).then_inc(logits_tm_ready, 1)
                pair, m = pair_of(r, c)
                if pair is not None:
                    select(pair, m, (c // PT - 1) % 2)
                if pair is not None and m == POOLED_AT:
                    alone(dve, pooled_done, pair + 2)
                    for img in range(2):
                        b = 2 * pair + img
                        dst = (pooled[:, :, b] if isinstance(pair, int)
                               else pooled[:, :, bass.ds(b, 1)].rearrange("p e b -> p (e b)"))
                        dve.tensor_copy(dst, p_pool[:, img * E:(img + 1) * E]).then_inc(pooled_ready, 1)

            pipeline_c(dve, step)

        def expert_of(ap, r, c):
            if isinstance(r, int):
                return ap[UE * r + c]
            return ap[bass.ds(UE * r + c, 1)].rearrange("a d h -> (a d) h")

        def sync_d(sp):
            sp.dma_start(b1_raw[:], w1[:, P, :]).then_inc(bias1_loaded, 16)

            def load(r, c):
                sp.dma_start(w1_in[:, c, :], expert_of(w1[:, 0:P, :], r, c)).then_inc(w_loaded[c], 16)
                sp.dma_start(w2_in[:, c, :, :], expert_of(w2[:, 0:HID, :], r, c).rearrange("(k p) o -> p k o", p=P))\
                  .then_inc(w_loaded[c], 16)

            for k in range(2):
                sp.sem_inc(eo_stored[k], 16)
            for c in range(UE):
                load(0, c)

            def body(r, last):
                for c in range(UE):
                    sp.wait_ge(eo_ready, r * UE + c + 1)
                    sp.sem_inc(passed, 1)
                    if not last:
                        load(r + 1, c)
                    if c % 4 == 3:
                        k = c // 4
                        dst = (expert_dram[:, r * UE + c - 3:r * UE + c + 1, :] if isinstance(r, int)
                               else expert_dram[:, bass.ds(UE * r + c - 3, 4), :])
                        sp.dma_start(dst, eo[:, k, :, :]).then_inc(eo_stored[k], 16)

            for r in range(RING):
                body(r, False)
                load_pair(sp, 0, r)
            with sp.Fori(RING, E // UE - 1) as r:
                body(r, False)
            body(E // UE - 1, True)
            for k in range(2):
                sp.wait_ge(eo_stored[k], 16 + 16 * (E // UE))

        def tensor_d(pe):
            pe.wait_ge(bias1_loaded, 16)
            for k in range(HK):
                mm = pe.transpose(banks[4][:, k * E:(k + 1) * E], b1_raw[:, k * P:(k + 1) * P], ident[0:E, 0:E])
            mm.then_inc(bias1_turned, 1)

            def hidden(r, c):
                if c == UE:
                    r, c = r + 1, 0
                e = UE * r + c
                pe.wait_ge(w_loaded[c], 32 * r + 32)
                if not isinstance(r, int) or e >= 2:
                    pe.wait_ge(hid_pre_ready, e - 1)
                for k in range(HK):
                    mm = pe.matmul(banks[c % 2][:, k * B:(k + 1) * B], w1_in[:, c, k * P:(k + 1) * P],
                                   pooled[:, e, :] if isinstance(r, int)
                                   else pooled[:, bass.ds(e, 1), :].rearrange("p a b -> p (a b)"), start=True, stop=True)
                mm.then_inc(hid_done, 1)

            def output(r, c):
                pe.wait_ge(hid_ready, UE * r + c + 1)
                if not isinstance(r, int) or UE * r + c >= 2:
                    pe.wait_ge(eo_ready, UE * r + c - 1)
                for k in range(HK):
                    mm = pe.matmul(banks[2 + c % 2][0:B, 0:O], hid[:, c % 2, k * B:(k + 1) * B], w2_in[:, c, k, :],
                                   start=(k == 0), stop=(k == HK - 1))
                mm.then_inc(eo_done, 1)

            skewed(pe, hidden, output)

        def vector_d(dve):
            dve.wait_ge(bias1_turned, 1)
            dve.tensor_copy(b1_t[:], banks[4][:, 0:HK * E].rearrange("p (k e) -> p e k", k=HK)).then_inc(bias1_ready, 1)
            dve.wait_ge(bias1_ready, 1)

            def biased(r, c):
                if c == UE:
                    r, c = r + 1, 0
                e = UE * r + c
                dve.wait_ge(hid_done, e + 1)
                if not isinstance(r, int) or e >= 2:
                    dve.wait_ge(hid_ready, e - 1)
                bias = b1_t[:, e, :] if isinstance(r, int) else b1_t[:, bass.ds(e, 1), :].rearrange("p a k -> p (a k)")
                dve.tensor_tensor(hid_pre[:, c % 2, :].rearrange("p (k b) -> p k b", k=HK),
                                  banks[c % 2][:, 0:HK * B].rearrange("p (k b) -> p k b", k=HK),
                                  bias.unsqueeze(2).to_broadcast([P, HK, B]), ALU.add).then_inc(hid_pre_ready, 1)

            def copied(r, c):
                dve.wait_ge(eo_done, UE * r + c + 1)
                if c % 4 == 0:
                    dve.wait_ge(eo_stored[c // 4], 16 * r + 16)
                dve.tensor_copy(eo[:, c // 4, c % 4, :], banks[2 + c % 2][0:B, 0:O]).then_inc(eo_ready, 1)

            skewed(dve, biased, copied)

        def scalar_d(act):
            def body(r, last):
                for c in range(UE):
                    e = UE * r + c
                    act.wait_ge(hid_pre_ready, e + 1)
                    if not isinstance(r, int) or c >= 2:
                        act.wait_ge(eo_done, e - 1)
                    act.activation(hid[:, c % 2, :], hid_pre[:, c % 2, :], ACT.Gelu).then_inc(hid_ready, 1)

            body(0, False)
            with act.Fori(1, E // UE) as r:
                body(r, False)

        def gpsimd_d(pool):
            pass

        def sync_e(sp):
            by_expert = expert_dram.rearrange("(q i) e o -> i e q o", i=2)
            for img in range(2):
                half = slice(img * E, (img + 1) * E)
                sp.dma_start(outputs[half, :, :], by_expert[img]).then_inc(outputs_loaded, 16)
                sp.dma_start(b2_in[half, :], w2[:, HID, :]).then_inc(outputs_loaded, 16)

            def step(r, c):
                q = RING * r + c
                for img in range(2):
                    sp.wait_ge(out_ready, (2 * q + img + 1) * IMG_TILES)
                    sp.sem_inc(passed, 1)
                    b = 2 * q + img
                    dst = out_img[b, :, :] if isinstance(b, int) else out_img[bass.ds(b, 1), :, :].rearrange("a p n -> p (a n)")
                    sp.dma_start(dst, x3_in[:, 2 * c + img, :]).then_inc(out_stored[c], 16)
                if not isinstance(q, int) or 1 <= q < PAIRS + 1 - RING:
                    sp.wait_ge(out_stored[(c - 1) % RING], 32 * (r + (c - 1) // RING + 1))
                    sp.sem_inc(passed, 1)
                    load_pair(sp, r, c - 1 + RING)

            for c in range(RING):
                step(0, c)
            with sp.Fori(1, FULL - 1) as r:
                for c in range(RING):
                    step(r, c)
            for q in range(RING * (FULL - 1), PAIRS):
                step(q // RING, q % RING)
            for c in range(RING):
                sp.wait_ge(out_stored[c], 32 * len(range(c, PAIRS, RING)))

        def tensor_e(pe):
            def step(r, c):
                q = RING * r + c
                pe.wait_ge(chosen_ready, q + 1)
                pe.wait_ge(pair_loaded[c], 48 * r + 48)
                for img in range(2):
                    half = slice(img * E, (img + 1) * E)
                    for t in range(IMG_TILES):
                        n = (2 * q + img) * IMG_TILES + t
                        if not isinstance(n, int) or n >= 8:
                            pe.wait_ge(out_ready, n - 7)
                        pe.matmul(banks[t][:], chosen[half, c, :], prob_in[half, c, t * TOK:(t + 1) * TOK],
                                  start=True, stop=True).then_inc(spread, 1)

            for c in range(RING):
                step(0, c)
            with pe.Fori(1, FULL) as r:
                for c in range(RING):
                    step(r, c)
            for q in range(RING * FULL, PAIRS):
                step(q // RING, q % RING)

        def vector_e(dve):
            dve.wait_ge(outputs_loaded, 64)
            dve.tensor_tensor(outputs[:], outputs[:], b2_in[:].unsqueeze(1).to_broadcast([P, PAIRS, O]), ALU.add)\
               .then_inc(outputs_ready, 1)
            dve.wait_ge(outputs_ready, 1)

            def choose(r, c):
                q = RING * r + c
                src = outputs[:, q, :] if isinstance(q, int) else outputs[:, bass.ds(q, 1), :].rearrange("p a o -> p (a o)")
                dve.tensor_copy(chosen[:, c, :], src).then_inc(chosen_ready, 1)

            def add(r, c):
                for img in range(2):
                    for t in range(IMG_TILES):
                        at = slice(t * TOK, (t + 1) * TOK)
                        dve.wait_ge(spread, (2 * (RING * r + c) + img) * IMG_TILES + t + 1)
                        dve.tensor_tensor(x3_in[:, 2 * c + img, at], banks[t][:], x3_in[:, 2 * c + img, at], ALU.add)\
                           .then_inc(out_ready, 1)

            with dve.Fori(0, FULL) as r:
                for c in range(RING):
                    choose(r, c)
                for c in range(RING):
                    add(r, c)
            for q in range(RING * FULL, PAIRS):
                choose(q // RING, q % RING)
                add(q // RING, q % RING)

        def scalar_e(act):
            pass

        def gpsimd_e(pool):
            pass

        block = ctx.enter_context(nc.Block())

        @block.sync
        def _(sp):
            run_phases(sp, sync_a, sync_b, sync_c, sync_d, sync_e)

        @block.tensor
        def _(pe):
            run_phases(pe, tensor_a, tensor_b, tensor_c, tensor_d, tensor_e)

        @block.scalar
        def _(act):
            run_phases(act, scalar_a, scalar_b, scalar_c, scalar_d, scalar_e)

        @block.gpsimd
        def _(pool):
            run_phases(pool, gpsimd_a, gpsimd_b, gpsimd_c, gpsimd_d, gpsimd_e)

        @block.vector
        def _(dve):
            run_phases(dve, vector_a, vector_b, vector_c, vector_d, vector_e)

_INS = ["x", "L0_conv_weights", "L0_ffn_W", "L0_ffn_V", "L0_ffn_gamma", "L0_ffn_beta", "L1_conv_kernel",
        "L1_ffn_gate_w", "L1_ffn_gate_b", "L1_ffn_weight1", "L1_ffn_weight2"]
_SCRATCH = [("x1", (256, 128, 512)), ("wx", (256, 128, 512)), ("y", (256, 128, 512)), ("x3", (256, 128, 512)),
            ("prob", (16, 128, 4096)), ("expert", (32, 64, 128))]


def kernel(**inputs):
    import concourse.bacc as _bacc
    from concourse import mybir as _mybir
    from concourse.bass_utils import run_bass_kernel_spmd as _run

    nc = _bacc.Bacc("TRN2", target_bir_lowering=False, num_devices=1)
    arrays, args = {}, []
    for name in _INS:
        a = np.ascontiguousarray(inputs[name])
        arrays[f"in_{name}_dram"] = a
        args.append(nc.dram_tensor(f"in_{name}_dram", a.shape, _mybir.dt.from_np(a.dtype), kind="ExternalInput").ap())
    out = nc.dram_tensor("out_0_dram", (32, 128, 64, 64), _mybir.dt.float32, kind="ExternalOutput").ap()
    scratch = [nc.dram_tensor(f"{name}_dram", shape, _mybir.dt.float32, kind="Internal").ap()
               for name, shape in _SCRATCH]
    metaformer(nc, *args, out, scratch)
    r = _run(nc, [arrays], core_ids=[0])
    return r.results[0]['out_0_dram']
```
